# Optimizing a Trainium2 kernel written in Bass

```python
import numpy as np
import jax
import jax.numpy as jnp

def _softmax(x, axis=-1):
    return jax.nn.softmax(x, axis=axis)

def _gelu(x):
    return jax.nn.gelu(x, approximate=True)

def _silu(x):
    return jax.nn.silu(x)

def _sigmoid(x):
    return jax.nn.sigmoid(x)

def _layernorm(x, axis=-1, eps=1e-05):
    m = jnp.mean(x, axis=axis, keepdims=True)
    v = jnp.var(x, axis=axis, keepdims=True)
    return (x - m) / jnp.sqrt(v + eps)

def _scatter_add(tgt, idx, src, axis=0):
    return tgt.at[idx].add(src)

def _segment_sum(src, seg, n):
    return jax.ops.segment_sum(src, seg, n)
kernel_name = 'mk_early_fusion_embed_d2_tok_img256_r4_7447a6'

def setup_inputs(seed: int=0):
    np.random.seed(seed)
    _w = jnp.asarray

    def _rec_inputs():
        import jax
        import jax.numpy as jnp
        _rk = jax.random.key(seed)
        x = 7.22013e-05 + 1.00017 * jax.random.normal(jax.random.fold_in(_rk, 1), (2, 1, 1024, 64), jnp.float32)
        x_txt = jax.random.randint(jax.random.fold_in(_rk, 51), (2, 128), 0, 12564, jnp.int32)
        return (x, x_txt)
    x, x_txt = _rec_inputs()

    def _L0_tok_setup():
        import jax, jax.numpy as jnp
        import numpy as np
        T, D_IN, D_INT, D_OUT, B = (1024, 64, 64, 64, 8)
        key = jax.random.key(seed)
        ks = jax.random.split(key, 12)
        s_in = 1.0 / np.sqrt(D_IN)
        s_int = 1.0 / np.sqrt(D_INT)
        return {'x_batched': jax.random.normal(ks[0], (B, 1, T, D_IN), dtype=jnp.float32), 'd_gamma_batched': jax.random.uniform(ks[1], (T, T), dtype=jnp.float32), 'Wq': jax.random.uniform(ks[2], (D_IN, D_INT), jnp.float32, -s_in, s_in), 'bq': jax.random.uniform(ks[3], (D_INT,), jnp.float32, -s_in, s_in), 'Wk': jax.random.uniform(ks[4], (D_IN, D_INT), jnp.float32, -s_in, s_in), 'bk': jax.random.uniform(ks[5], (D_INT,), jnp.float32, -s_in, s_in), 'Wv': jax.random.uniform(ks[6], (D_IN, D_INT), jnp.float32, -s_in, s_in), 'bv': jax.random.uniform(ks[7], (D_INT,), jnp.float32, -s_in, s_in), 'Wo': jax.random.uniform(ks[8], (D_INT, D_OUT), jnp.float32, -s_int, s_int), 'bo': jax.random.uniform(ks[9], (D_OUT,), jnp.float32, -s_int, s_int), 'prelu_a': jnp.float32(0.25)}
    _L0_tok_all = _L0_tok_setup()
    _L0_tok_in = {k: v for k, v in _L0_tok_all.items() if k in ('d_gamma_batched', 'Wq', 'bq', 'Wk', 'bk', 'Wv', 'bv', 'Wo', 'bo', 'prelu_a')}
    del _L0_tok_all

    def _L0_txt_setup():
        import jax, jax.numpy as jnp
        import numpy as np
        VOCAB, N_TURNS, OUT_DIM, POLY_DEG = (50257, 4, 64, 4)
        key = jax.random.key(seed)
        k1, k2, k3 = jax.random.split(key, 3)
        token_ids = jax.random.randint(k1, (16, 1024), 0, VOCAB)
        turns = jax.random.normal(k2, (VOCAB, N_TURNS), dtype=jnp.float32) * 3.0
        poly_coeffs = jax.random.normal(k3, (N_TURNS, POLY_DEG + 1, OUT_DIM), dtype=jnp.float32) * 0.01
        return {'token_ids': token_ids, 'turns': turns, 'poly_coeffs': poly_coeffs}
    _L0_txt_all = _L0_txt_setup()
    _L0_txt_in = {k: v for k, v in _L0_txt_all.items() if k in ('turns', 'poly_coeffs')}
    del _L0_txt_all

    def _L0_attn_setup():
        import jax, jax.numpy as jnp
        import numpy as np
        import math
        B, N, D = (4, 1024, 64)
        key = jax.random.key(seed)
        k0, k1, k2, k3 = jax.random.split(key, 4)
        bound = math.sqrt(6.0 / D)
        return {'x': jax.random.normal(k0, (B, N, D), dtype=jnp.float32), 'Wq': jax.random.uniform(k1, (D, D), dtype=jnp.float32, minval=-bound, maxval=bound), 'Wk': jax.random.uniform(k2, (D, D), dtype=jnp.float32, minval=-bound, maxval=bound), 'Wv': jax.random.uniform(k3, (D, D), dtype=jnp.float32, minval=-bound, maxval=bound)}
    _L0_attn_all = _L0_attn_setup()
    _L0_attn_in = {k: v for k, v in _L0_attn_all.items() if k in ('Wq', 'Wk', 'Wv')}
    del _L0_attn_all

    def _L0_ffn_setup():
        import jax, jax.numpy as jnp
        import numpy as np
        B, T, IN_DIM = (64, 64, 64)
        HID, OUT_DIM = (128, 64)
        N_LAYERS, N_EXPERTS, N_SHARED = (2, 16, 1)
        key = jax.random.key(seed)
        ks = jax.random.split(key, 10)
        s = 0.02
        x = jax.random.normal(ks[0], (B, T, IN_DIM), dtype=jnp.float32)
        route_id = jax.random.randint(ks[1], (B,), 0, N_EXPERTS)
        Wi = jax.random.normal(ks[2], (HID, IN_DIM), dtype=jnp.float32) * s
        bi = jnp.zeros((HID,), dtype=jnp.float32)
        Wr = jax.random.normal(ks[3], (N_LAYERS, N_EXPERTS, HID, HID), dtype=jnp.float32) * s
        br = jax.random.normal(ks[4], (N_LAYERS, N_EXPERTS, HID), dtype=jnp.float32) * s
        Ws = jax.random.normal(ks[5], (N_LAYERS, N_SHARED, HID, HID), dtype=jnp.float32) * s
        bs = jax.random.normal(ks[6], (N_LAYERS, N_SHARED, HID), dtype=jnp.float32) * s
        Wo = jax.random.normal(ks[7], (OUT_DIM, HID), dtype=jnp.float32) * s
        bo = jnp.zeros((OUT_DIM,), dtype=jnp.float32)
        return {'x': x, 'route_id': route_id, 'Wi': Wi, 'bi': bi, 'Wr': Wr, 'br': br, 'Ws': Ws, 'bs': bs, 'Wo': Wo, 'bo': bo}
    _L0_ffn_all = _L0_ffn_setup()
    _L0_ffn_in = {k: v for k, v in _L0_ffn_all.items() if k in ('route_id', 'Wi', 'bi', 'Wr', 'br', 'Ws', 'bs', 'Wo', 'bo')}
    del _L0_ffn_all

    def _L1_attn_setup():
        import jax, jax.numpy as jnp
        import numpy as np
        B, S, F, H = (4, 256, 64, 8)
        SCALE = float(F) ** 0.5
        key = jax.random.key(seed)
        ks = jax.random.split(key, 5)
        return {'q_input': jax.random.normal(ks[0], (B, S, F), dtype=jnp.float32), 'Wq': jax.random.normal(ks[1], (F, F * H), dtype=jnp.float32) * 0.02, 'Wk': jax.random.normal(ks[2], (F, F * H), dtype=jnp.float32) * 0.02, 'Wv': jax.random.normal(ks[3], (F, F * H), dtype=jnp.float32) * 0.02, 'Wo': jax.random.normal(ks[4], (F * H, F), dtype=jnp.float32) * 0.02}
    _L1_attn_all = _L1_attn_setup()
    _L1_attn_in = {k: v for k, v in _L1_attn_all.items() if k in ('Wq', 'Wk', 'Wv', 'Wo')}
    del _L1_attn_all

    def _L1_ffn_setup():
        import jax, jax.numpy as jnp
        import numpy as np
        NUM_EXPERTS = 8
        TOP_K = 2
        B, S, D = (8, 2048, 64)

        def _moe(tokens, router_w, w1, b1, w2, b2):
            N = tokens.shape[0]
            E = router_w.shape[0]
            logits = tokens.astype(jnp.float32) @ router_w.astype(jnp.float32).T
            probs = jax.nn.softmax(logits, axis=-1)
            rw, re = jax.lax.top_k(probs, TOP_K)
            if TOP_K > 1:
                rw = rw / jnp.maximum(rw.sum(-1, keepdims=True), 1e-12)
            rw = rw.astype(tokens.dtype)
            combine = jnp.zeros((N, E), tokens.dtype).at[jnp.arange(N)[:, None], re].set(rw)
            out = tokens
            for e in range(E):
                h = jax.nn.gelu(tokens @ w1[e] + b1[e], approximate=False)
                y = h @ w2[e] + b2[e]
                out = out + combine[:, e:e + 1] * y
            return out
        key = jax.random.key(seed)
        ks = jax.random.split(key, 4)
        scale = 1.0 / np.sqrt(D).astype(np.float32)
        return {'input_embeddings': jax.random.normal(ks[0], (B, S, D), jnp.float32), 'router_w': jax.random.normal(ks[1], (NUM_EXPERTS, D), jnp.float32) * scale, 'w1': jax.random.normal(ks[2], (NUM_EXPERTS, D, D), jnp.float32) * scale, 'b1': jnp.zeros((NUM_EXPERTS, D), jnp.float32), 'w2': jax.random.normal(ks[3], (NUM_EXPERTS, D, D), jnp.float32) * scale, 'b2': jnp.zeros((NUM_EXPERTS, D), jnp.float32)}
    _L1_ffn_all = _L1_ffn_setup()
    _L1_ffn_in = {k: v for k, v in _L1_ffn_all.items() if k in ('router_w', 'w1', 'b1', 'w2', 'b2')}
    del _L1_ffn_all
    return {'x': x, 'x_txt': x_txt, 'L0_tok_d_gamma_batched': _L0_tok_in['d_gamma_batched'], 'L0_tok_Wq': _L0_tok_in['Wq'], 'L0_tok_bq': _L0_tok_in['bq'], 'L0_tok_Wk': _L0_tok_in['Wk'], 'L0_tok_bk': _L0_tok_in['bk'], 'L0_tok_Wv': _L0_tok_in['Wv'], 'L0_tok_bv': _L0_tok_in['bv'], 'L0_tok_Wo': _L0_tok_in['Wo'], 'L0_tok_bo': _L0_tok_in['bo'], 'L0_tok_prelu_a': _L0_tok_in['prelu_a'], 'L0_txt_turns': _L0_txt_in['turns'], 'L0_txt_poly_coeffs': _L0_txt_in['poly_coeffs'], 'L0_attn_Wq': _L0_attn_in['Wq'], 'L0_attn_Wk': _L0_attn_in['Wk'], 'L0_attn_Wv': _L0_attn_in['Wv'], 'L0_ffn_route_id': _L0_ffn_in['route_id'], 'L0_ffn_Wi': _L0_ffn_in['Wi'], 'L0_ffn_bi': _L0_ffn_in['bi'], 'L0_ffn_Wr': _L0_ffn_in['Wr'], 'L0_ffn_br': _L0_ffn_in['br'], 'L0_ffn_Ws': _L0_ffn_in['Ws'], 'L0_ffn_bs': _L0_ffn_in['bs'], 'L0_ffn_Wo': _L0_ffn_in['Wo'], 'L0_ffn_bo': _L0_ffn_in['bo'], 'L1_attn_Wq': _L1_attn_in['Wq'], 'L1_attn_Wk': _L1_attn_in['Wk'], 'L1_attn_Wv': _L1_attn_in['Wv'], 'L1_attn_Wo': _L1_attn_in['Wo'], 'L1_ffn_router_w': _L1_ffn_in['router_w'], 'L1_ffn_w1': _L1_ffn_in['w1'], 'L1_ffn_b1': _L1_ffn_in['b1'], 'L1_ffn_w2': _L1_ffn_in['w2'], 'L1_ffn_b2': _L1_ffn_in['b2']}

def reference(x, x_txt, L0_tok_d_gamma_batched, L0_tok_Wq, L0_tok_bq, L0_tok_Wk, L0_tok_bk, L0_tok_Wv, L0_tok_bv, L0_tok_Wo, L0_tok_bo, L0_tok_prelu_a, L0_txt_turns, L0_txt_poly_coeffs, L0_attn_Wq, L0_attn_Wk, L0_attn_Wv, L0_ffn_route_id, L0_ffn_Wi, L0_ffn_bi, L0_ffn_Wr, L0_ffn_br, L0_ffn_Ws, L0_ffn_bs, L0_ffn_Wo, L0_ffn_bo, L1_attn_Wq, L1_attn_Wk, L1_attn_Wv, L1_attn_Wo, L1_ffn_router_w, L1_ffn_w1, L1_ffn_b1, L1_ffn_w2, L1_ffn_b2):
    import jax
    import jax.numpy as jnp

    def _L0_tok_ref(x_batched, d_gamma_batched, Wq, bq, Wk, bk, Wv, bv, Wo, bo, prelu_a):
        import jax, jax.numpy as jnp
        import numpy as np
        T, D_IN, D_INT, D_OUT, B = (1024, 64, 64, 64, 8)
        x = x_batched.reshape(x_batched.shape[0], T, D_IN)
        q = x @ Wq + bq
        k = x @ Wk + bk
        v = x @ Wv + bv
        scores = jnp.einsum('btd,bsd->bts', q, k)
        retained = jnp.einsum('bts,bsd->btd', d_gamma_batched * scores, v)
        y = retained @ Wo + bo
        out = jnp.where(y >= 0, y, prelu_a * y)
        return out

    def _L0_txt_ref(token_ids, turns, poly_coeffs):
        import jax, jax.numpy as jnp
        import numpy as np
        VOCAB, N_TURNS, OUT_DIM, POLY_DEG = (50257, 4, 64, 4)
        base_turns = turns[token_ids]
        x = jax.lax.stop_gradient(jnp.trunc(base_turns)).astype(jnp.float32)
        degs = jnp.arange(POLY_DEG + 1, dtype=jnp.float32)
        xp = x[..., None] ** degs
        emb = jnp.einsum('bstd,tdo->bso', xp, poly_coeffs)
        return emb

    def _L0_attn_ref(x, Wq, Wk, Wv):
        import jax, jax.numpy as jnp
        import numpy as np
        import math
        B, N, D = (4, 1024, 64)
        q = x @ Wq.T
        k = x @ Wk.T
        v = x @ Wv.T
        n = x.shape[1]
        d_k = x.shape[2]
        mask = jnp.triu(jnp.ones((n, n), dtype=x.dtype), k=1)
        scale = jnp.asarray(1.0 / math.sqrt(d_k), dtype=x.dtype)
        s = (jnp.einsum('bnd,bmd->bnm', q, k) - (1.0 - mask) * 10000000000.0) * scale
        s = jax.nn.softmax(s, axis=1)
        return jnp.einsum('bnm,bmd->bnd', s, v)

    def _L0_ffn_ref(x, route_id, Wi, bi, Wr, br, Ws, bs, Wo, bo):
        import jax, jax.numpy as jnp
        import numpy as np
        B, T, IN_DIM = (64, 64, 64)
        HID, OUT_DIM = (128, 64)
        N_LAYERS, N_EXPERTS, N_SHARED = (2, 16, 1)
        flat = x.reshape(-1, x.shape[-1])
        n_tok = flat.shape[0]
        route = jnp.repeat(route_id, n_tok // route_id.shape[0])
        h = jax.nn.relu(flat @ Wi.T + bi)
        n_layers, n_experts = (Wr.shape[0], Wr.shape[1])
        for l in range(n_layers):
            shared = (jnp.einsum('nd,shd->snh', h, Ws[l]) + bs[l][:, None, :]).mean(axis=0)
            routed = jnp.zeros_like(h)
            for e in range(n_experts):
                ye = h @ Wr[l, e].T + br[l, e]
                routed = routed + jnp.where((route == e)[:, None], ye, 0.0)
            h = jax.nn.relu(shared + routed + h)
        out = h @ Wo.T + bo
        return out.reshape(*x.shape[:-1], out.shape[-1])

    def _L1_attn_ref(q_input, Wq, Wk, Wv, Wo):
        import jax, jax.numpy as jnp
        import numpy as np
        B, S, F, H = (4, 256, 64, 8)
        SCALE = float(F) ** 0.5
        b, s, f = q_input.shape
        h = Wq.shape[1] // f
        q = (q_input.reshape(b * s, f) @ Wq).reshape(b, s, f, h)
        k = (q_input.reshape(b * s, f) @ Wk).reshape(b, s, f, h)
        v = (q_input.reshape(b * s, f) @ Wv).reshape(b, s, f, h)
        qkt = jnp.einsum('bifh,bjfh->bijh', q, k)
        attn = jax.nn.sigmoid(qkt * SCALE)
        wv = jnp.einsum('bijh,bjfh->bifh', attn, v)
        wv = wv.reshape(b * s, f * h)
        out = jax.nn.relu(wv @ Wo)
        return out.reshape(b, s, f)

    def _L1_ffn_ref(input_embeddings, router_w, w1, b1, w2, b2):
        import jax, jax.numpy as jnp
        import numpy as np
        NUM_EXPERTS = 8
        TOP_K = 2
        B, S, D = (8, 2048, 64)

        def _moe(tokens, router_w, w1, b1, w2, b2):
            N = tokens.shape[0]
            E = router_w.shape[0]
            logits = tokens.astype(jnp.float32) @ router_w.astype(jnp.float32).T
            probs = jax.nn.softmax(logits, axis=-1)
            rw, re = jax.lax.top_k(probs, TOP_K)
            if TOP_K > 1:
                rw = rw / jnp.maximum(rw.sum(-1, keepdims=True), 1e-12)
            rw = rw.astype(tokens.dtype)
            combine = jnp.zeros((N, E), tokens.dtype).at[jnp.arange(N)[:, None], re].set(rw)
            out = tokens
            for e in range(E):
                h = jax.nn.gelu(tokens @ w1[e] + b1[e], approximate=False)
                y = h @ w2[e] + b2[e]
                out = out + combine[:, e:e + 1] * y
            return out
        b, s, d = input_embeddings.shape
        tokens = input_embeddings.reshape(b * s, d)
        return _moe(tokens, router_w, w1, b1, w2, b2).reshape(b, s, d)
    h = _L0_tok_ref(x, L0_tok_d_gamma_batched, L0_tok_Wq, L0_tok_bq, L0_tok_Wk, L0_tok_bk, L0_tok_Wv, L0_tok_bv, L0_tok_Wo, L0_tok_bo, L0_tok_prelu_a)
    h = jnp.concatenate([h, _L0_txt_ref(x_txt, L0_txt_turns, L0_txt_poly_coeffs)], axis=1)
    h = h + _L0_attn_ref(_layernorm(h, axis=-1), L0_attn_Wq, L0_attn_Wk, L0_attn_Wv)
    h = h + _L0_ffn_ref(_layernorm(h, axis=-1), L0_ffn_route_id, L0_ffn_Wi, L0_ffn_bi, L0_ffn_Wr, L0_ffn_br, L0_ffn_Ws, L0_ffn_bs, L0_ffn_Wo, L0_ffn_bo)
    h = h + _L1_attn_ref(_layernorm(h, axis=-1), L1_attn_Wq, L1_attn_Wk, L1_attn_Wv, L1_attn_Wo)
    h = h + _L1_ffn_ref(_layernorm(h, axis=-1), L1_ffn_router_w, L1_ffn_w1, L1_ffn_b1, L1_ffn_w2, L1_ffn_b2)
    return h

_drawn_inputs = setup_inputs


def setup_inputs(seed=0):
    import zlib

    import numpy as np

    out = dict(_drawn_inputs(seed))
    spreads = {'L0_ffn_bi': (0.0, 0.8),
     'L0_ffn_bo': (0.0, 1.481),
     'L1_ffn_b1': (0.0, 0.8),
     'L1_ffn_b2': (0.0, 2.0)}
    factors = {'L0_tok_bo': 23.487,
     'L0_ffn_Wi': 8.0,
     'L0_ffn_Wr': 8.0,
     'L0_ffn_br': 21.587,
     'L0_ffn_Ws': 8.0,
     'L0_ffn_bs': 8.0,
     'L0_ffn_Wo': 8.0,
     'L1_ffn_router_w': 5.566,
     'L1_ffn_w1': 5.602,
     'L1_ffn_w2': 5.052}
    for name, (base, spread) in spreads.items():
        noise = np.random.default_rng([zlib.crc32(name.encode()), seed]).standard_normal(out[name].shape)
        drawn = base * np.exp(spread * noise) if base else spread * noise
        out[name] = jnp.asarray(drawn.astype(out[name].dtype))
    for name, factor in factors.items():
        out[name] = (out[name] * factor).astype(out[name].dtype)
    return out
```

```python
from contextlib import ExitStack

import numpy as np

import concourse.bass as bass
from concourse import mybir

ALU = mybir.AluOpType
ACT = mybir.ActivationFunctionType
F32 = mybir.dt.float32
F32R = mybir.dt.float32r
I32 = mybir.dt.int32
AX_X = mybir.AxisListType.X

P = 128
B = 2
D = 64
T_IMG = 1024
JI = T_IMG // P
T_TXT = 128
J = JI + 1
S = J * P
NT = B * J
TOK = B * S
TURNS, DEGS = 4, 5
HID = 128
LAYERS, EXPERTS = 2, 16
GROUPS = 64
GT = TOK // GROUPS
HEADS = 8
PAIRS = HEADS // 2
ME = 8
EARLY = 56
WG = LAYERS * HID
EPS = 1e-5
MASKED = -1e10
CH = 384
NCH = S // CH
BANK = 512

W_AQ, W_AK, W_AV = 0, 128, 256
W_CQ, W_CK, W_CV = 320, 448, 576
W_DI = 640
W_EV = 768
W_FR = W_EV + HEADS * D
W_F1 = W_FR + ME
W_FB2 = W_F1 + ME * D
NW = W_FB2 + D
K_WOA = 0
K_WS = 128
K_WOD = K_WS + LAYERS * HID
K_ID = K_WOD + D
K_MASK = K_ID + P
K_BVA, K_BOA, K_BOD = K_MASK + P, K_MASK + P + D, K_MASK + P + 2 * D
K_REV = K_BOD + D
K_COL = K_REV + ME
NK = K_COL + 11
C_BQ, C_BK, C_BI, C_BS, C_B1, C_SLOPE, C_EIDX = (K_COL + n for n in (0, 1, 2, 3, 5, 9, 10))


def program(nc, x_stack, w_stack, w_plain, w_qk, w_late, gamma_t, w_br, w_poly, ids, turns, route, w_route, out):
    with ExitStack() as ctx:
        def sb(name, shape, dt=F32):
            return ctx.enter_context(nc.sbuf_tensor(name, shape, dt))

        sems = {}

        def s(name):
            if name not in sems:
                sems[name] = ctx.enter_context(nc.semaphore(name))
            return sems[name]

        raw1 = sb("raw1", [P, 2048])
        raw2 = sb("raw2", [P, NW])
        w_hi = sb("w_hi", [P, NW], F32R)
        w_lo = sb("w_lo", [P, NW], F32R)
        plain = sb("plain", [P, NK])
        halves = sb("halves", [P, TOK + 2 * 6 * S], F32R)
        big = sb("big", [P, GROUPS * LAYERS * HID])
        mid = sb("mid", [P, 4 * TOK])
        tmp = sb("tmp", [P, B * J * P])
        br = sb("br", [EXPERTS, LAYERS * HID])
        idx = sb("idx", [P, B], I32)
        route_row = sb("route_row", [1, GROUPS], I32)
        route_all = sb("route_all", [EXPERTS, GROUPS], I32)
        onehot = sb("onehot", [EXPERTS, GROUPS])
        stat = sb("stat", [P, 4, NT])
        tok4i = sb("tok4i", [P, B * TURNS], I32)
        small = sb("small", [P, 16])
        ps = ctx.enter_context(nc.psum_tensor("ps", [P, 8 * BANK], F32))

        def bank(n, lo=0, hi=BANK):
            return ps[:, n * BANK + lo:n * BANK + hi]

        h = raw2[:, 0:NT * D].rearrange("p (t d) -> p t d", d=D)
        wo_e = raw2[:, NT * D:NT * D + PAIRS * D]
        w2_f = raw2[:, NT * D + PAIRS * D:NT * D + 2 * PAIRS * D]
        bias_g = raw2[:, NT * D + 2 * PAIRS * D:NT * D + 2 * PAIRS * D + LAYERS * GROUPS].rearrange("p (l g) -> p l g", l=LAYERS)
        ident = plain[:, K_ID:K_ID + P]
        x_hl = halves[:, 0:TOK]
        split = halves[:, TOK + 2 * 5 * S:TOK + 2 * 6 * S].rearrange("p (t c) -> p t c", c=P)
        xc = tmp[:, 0:NT * D].rearrange("p (t d) -> p t d", d=D)
        sq = tmp[:, NT * D:2 * NT * D].rearrange("p (t d) -> p t d", d=D)

        def stacked(sec, n):
            return w_hi[:, sec:sec + n], w_lo[:, sec:sec + n]

        xa = halves[:, 0:B * T_IMG]
        qa_hi = halves[:, TOK:TOK + B * T_IMG]
        qa_lo = halves[:, TOK + B * T_IMG:TOK + 2 * B * T_IMG]
        ka = halves[:, TOK + 2 * B * T_IMG:TOK + 3 * B * T_IMG]
        va = big[:, EARLY * WG:EARLY * WG + B * JI * D]
        o = EARLY * WG + B * JI * D
        poly = big[0:TURNS * DEGS, o:o + D]
        powers_t = big[0:TURNS * DEGS, o + D:o + D + B * P].rearrange("p (b t) -> p b t", b=B)
        o += D + B * P
        tok4 = big[:, o:o + 8 * B * TURNS].rearrange("p (n t) -> p n t", n=8)
        o += 8 * B * TURNS
        powers = big[:, o:o + B * TURNS * DEGS].rearrange("p (b t k) -> p b t k", b=B, t=TURNS)
        gamma = mid[:, 0:JI * T_IMG].rearrange("p (j t) -> p j t", j=JI)
        ret = mid[:, JI * T_IMG:JI * T_IMG + T_IMG]
        pa = tmp[:, 0:B * T_IMG].rearrange("p (b t) -> p b t", b=B)
        qc_hi = [halves[:, TOK + b * 3 * S:TOK + b * 3 * S + S] for b in range(B)]
        qc_lo = [halves[:, TOK + b * 3 * S + S:TOK + b * 3 * S + 2 * S] for b in range(B)]
        kc = [halves[:, TOK + b * 3 * S + 2 * S:TOK + b * 3 * S + 3 * S] for b in range(B)]
        vc = mid[:, 0:NT * D]
        pc = [mid[:, NT * D + n * S:NT * D + n * S + S] for n in range(2)]
        vs = [mid[:, NT * D + 2 * S + n * D:NT * D + 2 * S + n * D + D] for n in range(2)]
        hid = [mid[:, n * TOK:(n + 1) * TOK] for n in range(3)]
        res = mid[:, 3 * TOK:4 * TOK]
        wr = big[:, :].rearrange("p (g l n) -> p g l n", g=GROUPS, l=LAYERS)
        v_all = mid[:, :].rearrange("p (t n) -> p t n", n=HEADS * D)
        wv = big[:, 0:PAIRS * B * S].rearrange("p (hp b t) -> p hp b t", hp=PAIRS, b=B)
        pe_ring = big[:, PAIRS * B * S:PAIRS * B * S + 3 * 2 * CH].rearrange("p (n h t) -> p n h t", n=3, h=2)
        v_cur = [big[:, PAIRS * B * S + 6 * CH + b * S:PAIRS * B * S + 6 * CH + b * S + S]
                 .rearrange("p (j n) -> p j n", n=P) for b in range(B)]
        q_hi, q_lo, k_e = ([halves[:, TOK + b * 6 * S + m * 2 * S:TOK + b * 6 * S + (m + 1) * 2 * S]
                            .rearrange("p (h t) -> p h t", h=2) for b in range(B)] for m in range(3))

        act_f = mid[:, :].rearrange("p (u t) -> p u t", u=ME // 2)
        c_hl = halves[:, TOK:2 * TOK]
        cc = halves[:, 2 * TOK:3 * TOK].rearrange("p (t c) -> p t c", c=P)
        sel = halves[:, 3 * TOK:3 * TOK + ME * D]
        sel_in = big[:, PAIRS * B * S + 6 * CH + B * S:PAIRS * B * S + 6 * CH + B * S + ME * D]
        slot = [tmp[:, (NT * D) + n * NT * ME:(NT * D) + (n + 1) * NT * ME] for n in range(8)]
        gate = [v.rearrange("p (t e) -> p t e", e=ME) for v in slot[:7]]
        per_tok = [slot[7][:, n * NT:(n + 1) * NT] for n in range(8)]

        DG = 8
        DW = DG * GT
        NDC = GROUPS // DG

        STEPS = J * NCH
        PV0 = 3
        AF0 = NCH
        UNITS = 4 * NCH
        FUNITS = [(ch, u) for ch in range(B * NCH) for u in range(ME // 2)]

        block = ctx.enter_context(nc.Block())

        @block.sync
        def _(sp):
            sp.dma_start(raw1[:, :], x_stack).then_inc(s("x_in"), 16)
            sp.dma_start(raw2[:, 0:W_CQ], w_stack[:, 0:W_CQ]).then_inc(s("w_first_in"), 16)
            sp.dma_start(plain[:, :], w_plain).then_inc(s("plain_in"), 16)
            sp.dma_start(idx[:, :], ids).then_inc(s("ids_in"), 16)
            for j in range(JI):
                sp.dma_start(gamma[:, j, :], gamma_t[j]).then_inc(s(f"gamma_in{j}"), 16)
            sp.dma_start(raw2[:, W_CQ:NW], w_stack[:, W_CQ:NW]).then_inc(s("w_rest_in"), 16)
            sp.dma_start(br[:, :], w_br).then_inc(s("small_in"), 16)
            sp.dma_start(poly[:, :], w_poly).then_inc(s("small_in"), 16)
            sp.dma_start(route_row[:, :], route).then_inc(s("route_in"), 16)
            sp.dma_start(route_all[:, :], route.broadcast_to([EXPERTS, GROUPS])).then_inc(s("small_in"), 16)
            sp.wait_ge(s("xa_lo"), 4)
            sp.dma_start(raw1[:, :], w_qk).then_inc(s("qk_in"), 16)
            sp.wait_ge(s("route_in"), 16)
            for g0, g1 in ((0, EARLY), (EARLY, GROUPS)):
                if g0:
                    sp.wait_ge(s("b_emb"), 1)
                with sp.Fori(g0 // 4, g1 // 4) as g4:
                    for n in range(4):
                        e = sp.value_load(route_row[0:1, bass.ds(g4 * 4 + n, 1)], min_val=0, max_val=EXPERTS - 1)
                        sp.dma_start(big[:, bass.ds((g4 * 4 + n) * WG, WG)],
                                     w_route[bass.ds(e, 1), :, :].rearrange("e p n -> p (e n)")).then_inc(s(f"wr_in{n}"), 16)
            sp.wait_ge(s("w_rest_lo"), 1)
            sp.dma_start(raw2[:, NT * D:NT * D + 2 * PAIRS * D], w_late[:, 0:2 * PAIRS * D]).then_inc(s("late_in"), 16)
            sp.wait_ge(s("h3"), 2)
            sp.dma_start(sel_in, w_late[:, 2 * PAIRS * D:2 * PAIRS * D + ME * D]).then_inc(s("sel_in"), 16)
            for b in range(B):
                sp.wait_ge(s("h5"), b + 1)
                sp.dma_start(out[b].rearrange("(j p) d -> p j d", p=P), h[:, b * J:(b + 1) * J, :]).then_inc(s("out"), 16)
            sp.wait_ge(s("out"), 32)

        @block.gpsimd
        def _(pool):
            pool.memset(stat[:, 3, :], -0.5).then_inc(s("expo"), 1)
            pool.wait_ge(s("ids_in"), 16)
            for b in range(B):
                pool.indirect_dma_start(tok4[:, 0, b * TURNS:(b + 1) * TURNS], None, turns,
                                        bass.IndirectOffsetOnAxis(ap=idx[:, b:b + 1], axis=0)).then_inc(s("turns_in"), 16)

            def rstd(st, b):
                t = slice(b * J, (b + 1) * J)
                pool.wait_ge(s(st + "_var"), b + 1)
                pool.tensor_tensor(stat[:, 2, t], stat[:, 1, t], stat[:, 3, t], ALU.pow).then_inc(s(st + "_rstd"), 1)

            pool.wait_ge(s("expo"), 1)
            for st in "cde":
                for b in range(B):
                    rstd(st, b)
            def v_copy(hp, b):
                pool.tensor_copy(v_cur[b], v_all[:, b * J:(b + 1) * J, bass.ds(hp * P, P)]).then_inc(s("e_vcur"), 1)

            for b in range(B):
                pool.wait_ge(s("e_v_read"), J * (b + 1))
                v_copy(0, b)
            with pool.Fori(1, PAIRS) as hp:
                for b in range(B):
                    pool.wait_ge(s("e_pv"), hp * (B * STEPS) + (b - 1) * STEPS + PV0)
                    v_copy(hp, b)
            pool.wait_ge(s("h4"), 2)
            pool.memset(cc.rearrange("p t c -> p (t c)").bitcast(F32), 0.0).then_inc(s("f_zero"), 1)
            for b in range(B):
                rstd("f", b)

        def product(pe, dst, stationary, moving_hi, moving_lo, sem=None):
            pe.matmul(dst, stationary, moving_hi, start=True, stop=False)
            m = pe.matmul(dst, stationary, moving_lo, start=False, stop=True)
            if sem is not None:
                m.then_inc(sem, 1)

        def product_w(pe, dst, w_pair, moving, sem=None):
            pe.matmul(dst, w_pair[0], moving, start=True, stop=False)
            m = pe.matmul(dst, w_pair[1], moving, start=False, stop=True)
            if sem is not None:
                m.then_inc(sem, 1)

        def nth(st, b):
            return B * "cdef".index(st) + b + 1

        def norm_dve(dve, st):
            def first(b):
                t = slice(b * J, (b + 1) * J)
                dve.reduce_sum(stat[:, 0, t], h[:, t, :], AX_X).then_inc(s("norm_sum"), 1)
                dve.wait_ge(s("norm_sum"), nth(st, b))
                dve.scalar_tensor_tensor(out=xc[:, t, :], in0=stat[:, 0, t].unsqueeze(2).broadcast_to([P, J, D]),
                                         scalar=-1.0 / D, in1=h[:, t, :], op0=ALU.mult, op1=ALU.add).then_inc(s("norm_xc"), 1)
                dve.wait_ge(s("norm_xc"), nth(st, b))
                dve.tensor_tensor(sq[:, t, :], xc[:, t, :], xc[:, t, :], ALU.mult).then_inc(s("norm_sq"), 1)
                dve.wait_ge(s("norm_sq"), nth(st, b))
                dve.reduce_sum(stat[:, 1, t], sq[:, t, :], AX_X).then_inc(s("norm_ssq"), 1)
                dve.wait_ge(s("norm_ssq"), nth(st, b))
                dve.tensor_scalar(stat[:, 1, t], stat[:, 1, t], 1.0 / D, EPS, ALU.mult, ALU.add).then_inc(s(st + "_var"), 1)

            def second(b):
                t = slice(b * J, (b + 1) * J)
                dve.wait_ge(s(st + "_rstd"), b + 1)
                dve.tensor_tensor(xc[:, t, :], xc[:, t, :], stat[:, 2, t].unsqueeze(2).broadcast_to([P, J, D]),
                                  ALU.mult).then_inc(s("norm_xn"), 1)
                dve.wait_ge(s("norm_xn"), nth(st, b))
                dve.tensor_copy(split[:, t, 0:D], xc[:, t, :]).then_inc(s("norm_xhi"), 1)
                dve.wait_ge(s("norm_xhi"), nth(st, b))
                dve.tensor_tensor(split[:, t, D:P], xc[:, t, :], split[:, t, 0:D].bitcast(F32),
                                  ALU.subtract).then_inc(s(st + "_split"), 1)
            return first, second

        TG = [(b, j0, n) for b in range(B) for j0, n in ((0, 4), (4, 4), (8, 1))]

        def transposes_pe(pe, st):
            for n, (b, j0, k) in enumerate(TG):
                pe.wait_ge(s(st + "_split"), b + 1)
                if n >= 2:
                    pe.wait_ge(s(st + "_xt"), n - 1)
                for i in range(k):
                    m = pe.transpose(bank(6 + n % 2, i * P, (i + 1) * P), split[:, b * J + j0 + i, :].bitcast(F32), ident)
                m.then_inc(s(st + "_tr"), 1)

        def transposes_act(act, st):
            for n, (b, j0, k) in enumerate(TG):
                act.wait_ge(s(st + "_tr"), n + 1)
                act.copy(x_hl[:, (b * J + j0) * P:(b * J + j0 + k) * P], bank(6 + n % 2, 0, k * P)).then_inc(s(st + "_xt"), 1)

        NX = [3, 6]

        CU = [(b, u) for b in range(B) for u in range(8)]
        CSTEP = [(b, j) for b in range(B) for j in range(J)]

        def c_width(j):
            return S if j == 0 else (j + 1) * P

        @block.tensor
        def _(pe):
            pe.wait_ge(s("w_first_lo"), 1)
            for c in range(4):
                pe.wait_ge(s("xa_lo"), c + 1)
                cols = slice(c * BANK, (c + 1) * BANK)
                if c >= 2:
                    pe.wait_ge(s("qa_lo"), c - 1)
                product_w(pe, bank(4 + c % 2), stacked(W_AQ, P), xa[:, cols], s("a_q"))
                if c >= 2:
                    pe.wait_ge(s("ka_lo"), c - 1)
                product_w(pe, bank(6 + c % 2), stacked(W_AK, P), xa[:, cols], s("a_k"))
            for t in range(B * JI):
                product(pe, bank(t // JI, (t % JI) * D, (t % JI + 1) * D), xa[:, t * P:(t + 1) * P],
                        *stacked(W_AV, D), s("a_v"))
            for j in range(JI + 1):
                for b in range(B):
                    if j == JI:
                        break
                    if j == 0:
                        pe.wait_ge(s("va"), 2)
                        pe.wait_ge(s("qa_lo"), 2 * (b + 1))
                        pe.wait_ge(s("ka_lo"), 2 * (b + 1))
                    else:
                        pe.wait_ge(s("pa"), 2 * (j - 1) + b + 1)
                    st = ka[:, b * T_IMG + j * P:b * T_IMG + (j + 1) * P]
                    for c in range(2):
                        q = slice(b * T_IMG + c * BANK, b * T_IMG + (c + 1) * BANK)
                        product(pe, bank(2 * b + c), st, qa_hi[:, q], qa_lo[:, q], s("a_s") if c == 1 else None)
                if j >= 1:
                    if j == 1:
                        pe.wait_ge(s("qa_lo"), 4)
                    pe.wait_ge(s("pa"), 2 * j)
                    for c in range(2):
                        for b in range(B):
                            m = pe.matmul(ps[b * D:(b + 1) * D, (4 + c) * BANK:(5 + c) * BANK],
                                          va[:, (b * JI + j - 1) * D:(b * JI + j) * D],
                                          pa[:, b, c * BANK:(c + 1) * BANK], start=(j == 1), stop=(j == JI),
                                          skip_group_check=True)
                    m.then_inc(s("a_pv"), 1)
            pe.wait_ge(s("ret"), 2)
            for j in range(JI):
                m = pe.matmul(bank(j // 4, (j % 4) * P, (j % 4 + 1) * P), ret[:, j * P:(j + 1) * P],
                              plain[:, K_WOA:K_WOA + P], start=True, stop=True)
            m.then_inc(s("a_y"), 1)
            for b in range(B):
                pe.wait_ge(s("powers"), 4)
                m = pe.transpose(ps[0:TURNS * DEGS, 2 * BANK + b * P:2 * BANK + (b + 1) * P],
                                 powers[:, b, :, :].rearrange("p t k -> p (t k)"), ident)
            m.then_inc(s("b_tr"), 1)
            pe.wait_ge(s("powers_t"), 1)
            pe.wait_ge(s("small_in"), 48)
            for b in range(B):
                m = pe.matmul(bank(3, b * D, (b + 1) * D), powers_t[:, b, :], poly[:, :], start=True, stop=True)
            m.then_inc(s("b_emb"), 1)
            transposes_pe(pe, "c")
            pe.wait_ge(s("w_rest_lo"), 1)
            for n, (b, u) in enumerate(CU):
                if u == 0:
                    pe.wait_ge(s("c_xt"), NX[b])
                if n >= 6:
                    pe.wait_ge(s("c_proj_read"), n - 5)
                if u < 6:
                    x = x_hl[:, b * S + u % 3 * CH:b * S + (u % 3 + 1) * CH]
                    product_w(pe, bank(n % 6, 0, CH), stacked(W_CQ if u < 3 else W_CK, P), x, s("c_proj"))
                else:
                    tiles = range(8) if u == 6 else [8]
                    for t in tiles:
                        product(pe, bank(n % 6, (t % 8) * D, (t % 8 + 1) * D), x_hl[:, (b * J + t) * P:(b * J + t + 1) * P],
                                *stacked(W_CV, D), s("c_proj") if t == tiles[-1] else None)

            def c_pv(n):
                b, j = CSTEP[n]
                pe.wait_ge(s("c_vs"), n + 1)
                if j == 0:
                    if b == 0:
                        pe.wait_ge(s("c_xt"), NX[1])
                    else:
                        pe.wait_ge(s("h2"), 1)
                tiles = range(J if j == 0 else j + 1)
                for i in tiles:
                    m = pe.matmul(ps[:, 6 * BANK + i * D:6 * BANK + (i + 1) * D], pc[n % 2][:, i * P:(i + 1) * P], vs[n % 2],
                                  start=(j == 0 and i % 8 == 0), stop=(j == J - 1), skip_group_check=True)
                m.then_inc(s("c_pv"), 1)

            for n, (b, j) in enumerate(CSTEP):
                if j == 0:
                    pe.wait_ge(s("c_proj_read"), 8 * (b + 1))
                if n == 0:
                    pe.wait_ge(s("c_proj_read"), 16)
                if n >= 2:
                    pe.wait_ge(s("c_exp"), n - 1)
                w = c_width(j)
                for c0 in range(0, w, BANK):
                    c1 = min(c0 + BANK, w)
                    o = (n % 2) * 3 * BANK
                    m = product(pe, ps[:, o + c0:o + c1], kc[b][:, j * P:(j + 1) * P],
                                qc_hi[b][:, c0:c1], qc_lo[b][:, c0:c1], s("c_s") if c1 == w else None)
                if n >= 1:
                    c_pv(n - 1)
            c_pv(len(CSTEP) - 1)
            transposes_pe(pe, "d")
            for n in range(B * NCH):
                pe.wait_ge(s("d_xt"), NX[n // NCH])
                if n >= 4:
                    pe.wait_ge(s("d_h0"), n - 3)
                product_w(pe, bank(n % 4, 0, CH), stacked(W_DI, HID), x_hl[:, n * CH:(n + 1) * CH], s("d_in"))
            pe.wait_ge(s("d_onehot"), 1)
            for l in range(LAYERS):
                m = pe.matmul(bank(4, l * GROUPS, (l + 1) * GROUPS), br[:, l * HID:(l + 1) * HID], onehot[:, :],
                              start=True, stop=True)
            m.then_inc(s("d_bp"), 1)
            for n in range(4):
                pe.wait_ge(s(f"wr_in{n}"), 16 * GROUPS // 4)
            for l in range(LAYERS):
                for c in range(NDC):
                    n = l * NDC + c
                    if n == 0:
                        pe.wait_ge(s("d_h0"), B * NCH)
                        pe.wait_ge(s("d_bias"), LAYERS)
                    if n >= 6:
                        pe.wait_ge(s("d_z"), n - 5)
                    if l == 1:
                        pe.wait_ge(s("d_h1"), c + 1)
                    o = c * DW
                    for g in range(DG):
                        pe.matmul(bank(n % 6, g * GT, (g + 1) * GT), wr[:, c * DG + g, l, :],
                                  hid[l][:, o + g * GT:o + (g + 1) * GT], start=(g == 0), stop=False,
                                  skip_group_check=True)
                    m = pe.matmul(bank(n % 6, 0, DW), plain[:, K_WS + l * HID:K_WS + (l + 1) * HID], hid[l][:, o:o + DW],
                                  start=False, stop=True, skip_group_check=True)
                    m.then_inc(s("d_f"), 1)
            pe.wait_ge(s("d_z"), LAYERS * NDC)
            pe.wait_ge(s("d_h2"), NDC)
            for b in range(B):
                for j in range(J):
                    m = pe.matmul(ps[:, 2 * b * BANK + j * D:2 * b * BANK + (j + 1) * D],
                                  hid[2][:, (b * J + j) * P:(b * J + j + 1) * P], plain[:, K_WOD:K_WOD + D],
                                  start=True, stop=True)
                m.then_inc(s("d_o"), 1)
            def unit(parity, u, b_x, dst):
                c = u % NCH
                product_w(pe, dst, stacked(u // NCH * P, P), x_hl[:, b_x * S + c * CH:b_x * S + (c + 1) * CH], s("e_proj"))

            def scores(step):
                b, k = step // STEPS % B, step % STEPS
                j, c = k // NCH, k % NCH
                for hd in range(2):
                    product(pe, bank(3 + 2 * (step % 2) + hd, 0, CH), k_e[b][:, hd, j * P:(j + 1) * P],
                            q_hi[b][:, hd, c * CH:(c + 1) * CH], q_lo[b][:, hd, c * CH:(c + 1) * CH],
                            s("e_qk") if hd == 1 else None)

            transposes_pe(pe, "e")
            pe.sem_inc(s("e_pv"), PV0)
            pe.wait_ge(s("e_xt"), NX[1])
            pe.wait_ge(s("e_w"), 1)
            for t in range(NT):
                if t < UNITS:
                    if t >= 4:
                        pe.wait_ge(s("e_proj_read"), t - 3)
                    unit(0, t, 0, bank(4 + t % 4, 0, CH))
                if t >= 4:
                    pe.wait_ge(s("e_v_read"), t - 3)
                product(pe, bank(t % 4), x_hl[:, t * P:(t + 1) * P], *stacked(W_EV, HEADS * D), s("e_v"))
            pe.wait_ge(s("e_v_read"), NT)
            pe.wait_ge(s("e_proj_read"), UNITS)
            scores(0)
            scores(1)

            def pair_steps(it, last):
                for n in range(B * STEPS):
                    b, k = n // STEPS, n % STEPS
                    j, c = k // NCH, k % NCH
                    if k == 0:
                        pe.wait_ge(s("e_vcur"), it * B + (b + 1))
                    if j == 0:
                        pe.wait_ge(s("e_acc_read"), it * (B * NCH) + (b * NCH + c + 1))
                    pe.wait_ge(s("e_sig"), it * (B * STEPS) + (n + 1))
                    for hd in range(2):
                        m = pe.matmul(ps[hd * D:(hd + 1) * D, c * BANK:c * BANK + CH], v_cur[b][:, j, hd * D:(hd + 1) * D],
                                      pe_ring[:, n % 3, hd, :], start=(j == 0), stop=(j == J - 1), skip_group_check=True)
                    m.then_inc(s("e_pv"), 1)
                    if not (last and n + 2 >= B * STEPS):
                        if (n + 2) % STEPS == 0:
                            pe.wait_ge(s("e_proj_read"), it * (B * UNITS) + ((n + 2) // STEPS + 1) * UNITS)
                        scores((n + 2) % (B * STEPS))
                    if k >= 2 and k % 2 == 0 and (k - 2) // 2 < UNITS and not (last and b == B - 1):
                        u = (k - 2) // 2
                        if u == 0 and b == B - 1:
                            pe.wait_ge(s("e_w"), it + 2)
                        pe.wait_ge(s("e_proj_read"), it * (B * UNITS) + ((b + 1) * UNITS + u))
                        unit(1 - b, u, 1 - b, bank(7, 0, CH))

            with pe.Fori(0, PAIRS - 1) as it:
                pair_steps(it, False)
            pair_steps(PAIRS - 1, True)
            pe.wait_ge(s("e_acc_read"), PAIRS * B * NCH + AF0)
            pe.wait_ge(s("late_in"), 16)
            for b in range(B):
                for j in range(J):
                    for hp in range(PAIRS):
                        o = (3 + 2 * b) * BANK + j * D
                        m = pe.matmul(ps[:, o:o + D], wv[:, hp, b, j * P:(j + 1) * P], wo_e[:, hp * D:(hp + 1) * D],
                                      start=(hp == 0), stop=(hp == PAIRS - 1))
                m.then_inc(s("e_o"), 1)
            transposes_pe(pe, "f")
            for b in range(B):
                pe.wait_ge(s("f_xt"), NX[b])
                for t in range(b * J, (b + 1) * J):
                    product(pe, bank(0, t * ME, (t + 1) * ME), x_hl[:, t * P:(t + 1) * P], *stacked(W_FR, ME),
                            s("f_r") if t == NT - 1 else None)
            for n, (ch, u) in enumerate(FUNITS):
                if n >= 4:
                    pe.wait_ge(s("f_gelu"), n - 3)
                product_w(pe, bank(1 + n % 4, 0, CH), stacked(W_F1 + u * P, P), x_hl[:, ch * CH:(ch + 1) * CH], s("f_1"))
            for n, (b, j0, k) in enumerate(TG):
                pe.wait_ge(s("f_cc"), 1)
                if n >= 2:
                    pe.wait_ge(s("f_ct"), n - 1)
                for i in range(k):
                    m = pe.transpose(bank(6 + n % 2, i * P, (i + 1) * P), cc[:, b * J + j0 + i, :].bitcast(F32), ident)
                m.then_inc(s("f_ctr"), 1)
            pe.wait_ge(s("f_ct"), len(TG))
            pe.wait_ge(s("f_sel"), 1)
            pe.wait_ge(s("f_gelu"), len(FUNITS))

            def second_layer(ch):
                pe.wait_ge(s("f_hc"), 4 * (ch + 1))
                for t in range(3 * ch, 3 * ch + 3):
                    o = (4 + 2 * (t // J)) * BANK + t % J * D
                    for u in range(ME // 2):
                        pe.matmul(ps[:, o:o + D], act_f[:, u, t * P:(t + 1) * P], w2_f[:, u * D:(u + 1) * D],
                                  start=(u == 0), stop=False)
                    pe.matmul(ps[:, o:o + D], c_hl[:, t * P:(t + 1) * P], w_hi[:, W_FB2:W_FB2 + D], start=False, stop=False)
                    m = pe.matmul(ps[:, o:o + D], c_hl[:, t * P:(t + 1) * P], w_lo[:, W_FB2:W_FB2 + D], start=False, stop=True)
                    if t % J == J - 1:
                        m.then_inc(s("f_y"), 1)

            for n, (ch, u) in enumerate(FUNITS):
                if n >= 4:
                    pe.wait_ge(s("f_hc"), n - 3)
                pe.matmul(bank(n % 4, 0, CH), sel[:, u * P:(u + 1) * P], c_hl[:, ch * CH:(ch + 1) * CH],
                          start=True, stop=True).then_inc(s("f_cb"), 1)
                if u == ME // 2 - 1 and ch >= 1:
                    second_layer(ch - 1)
            second_layer(B * NCH - 1)

        @block.vector
        def _(dve):
            dve.wait_ge(s("w_first_in"), 16)
            dve.tensor_copy(w_hi[:, 0:W_CQ], raw2[:, 0:W_CQ]).then_inc(s("w_first_hi"), 1)
            dve.wait_ge(s("w_first_hi"), 1)
            dve.tensor_tensor(w_lo[:, 0:W_CQ], raw2[:, 0:W_CQ], w_hi[:, 0:W_CQ].bitcast(F32),
                              ALU.subtract).then_inc(s("w_first_lo"), 1)
            dve.wait_ge(s("x_in"), 16)
            for c in range(4):
                cols = slice(c * BANK, (c + 1) * BANK)
                dve.tensor_copy(xa[:, cols], raw1[:, cols]).then_inc(s("xa_hi"), 1)
                dve.wait_ge(s("xa_hi"), c + 1)
                dve.tensor_tensor(xa[D:P, cols], raw1[D:P, cols], xa[D:P, cols].bitcast(F32),
                                  ALU.subtract).then_inc(s("xa_lo"), 1)
            dve.wait_ge(s("plain_in"), 16)
            for c in range(4):
                cols = slice(c * BANK, (c + 1) * BANK)
                dve.wait_ge(s("qa_hi"), c + 1)
                dve.scalar_tensor_tensor(out=qa_lo[:, cols], in0=bank(4 + c % 2), scalar=plain[:, C_BQ:C_BQ + 1],
                                         in1=qa_hi[:, cols].bitcast(F32), op0=ALU.add, op1=ALU.subtract).then_inc(s("qa_lo"), 1)
                dve.wait_ge(s("ka_hi"), c + 1)
                dve.scalar_tensor_tensor(out=ka[D:P, cols], in0=bank(6 + c % 2)[D:P, :], scalar=plain[D:P, C_BK:C_BK + 1],
                                         in1=ka[D:P, cols].bitcast(F32), op0=ALU.add, op1=ALU.subtract).then_inc(s("ka_lo"), 1)
            for b in range(B):
                dve.wait_ge(s("a_v"), JI * (b + 1))
                dve.tensor_tensor(va[:, b * JI * D:(b + 1) * JI * D].rearrange("p (j d) -> p j d", d=D),
                                  bank(b).rearrange("p (j d) -> p j d", d=D),
                                  plain[:, K_BVA:K_BVA + D].unsqueeze(1).broadcast_to([P, JI, D]), ALU.add).then_inc(s("va"), 1)
            dve.wait_ge(s("w_rest_in"), 16)
            dve.tensor_copy(w_hi[:, W_CQ:NW], raw2[:, W_CQ:NW]).then_inc(s("w_rest_hi"), 1)
            flat = [tok4[:, n, :] for n in range(8)]
            dve.wait_ge(s("turns_in"), 32)
            dve.scalar_tensor_tensor(out=flat[1], in0=flat[0], scalar=-1.0, in1=flat[0], op0=ALU.mult, op1=ALU.max)\
               .then_inc(s("b_abs"), 1)
            dve.wait_ge(s("b_abs"), 1)
            dve.tensor_copy(tok4i[:, :], flat[1]).then_inc(s("b_int"), 1)
            dve.wait_ge(s("b_int"), 1)
            dve.tensor_copy(flat[2], tok4i[:, :]).then_inc(s("b_round"), 1)
            dve.wait_ge(s("b_round"), 1)
            dve.tensor_tensor(flat[3], flat[2], flat[1], ALU.is_gt).then_inc(s("b_over"), 1)
            dve.wait_ge(s("b_over"), 1)
            dve.tensor_tensor(flat[4], flat[2], flat[3], ALU.subtract).then_inc(s("b_floor"), 1)
            dve.tensor_scalar(flat[5], flat[0], 0.0, 2.0, ALU.is_ge, ALU.mult).then_inc(s("b_sign"), 1)
            dve.wait_ge(s("b_floor"), 1)
            dve.wait_ge(s("b_sign"), 1)
            dve.scalar_tensor_tensor(out=flat[6], in0=flat[5], scalar=-1.0, in1=flat[4], op0=ALU.add, op1=ALU.mult)\
               .then_inc(s("b_trunc"), 1)
            pw = [powers[:, :, :, k].rearrange("p b t -> p (b t)") for k in range(DEGS)]
            dve.memset(pw[0], 1.0).then_inc(s("b_one"), 1)
            dve.wait_ge(s("b_trunc"), 1)
            dve.tensor_copy(pw[1], flat[6]).then_inc(s("powers"), 1)
            dve.tensor_tensor(pw[2], flat[6], flat[6], ALU.mult).then_inc(s("powers"), 1)
            dve.wait_ge(s("powers"), 2)
            dve.tensor_tensor(pw[3], pw[2], flat[6], ALU.mult).then_inc(s("powers"), 1)
            dve.tensor_tensor(pw[4], pw[2], pw[2], ALU.mult).then_inc(s("powers"), 1)
            for j in range(JI):
                for b in range(B):
                    if b == 0:
                        dve.wait_ge(s(f"gamma_in{j}"), 16)
                    if j >= 1:
                        dve.wait_ge(s("a_pv"), j)
                    dve.wait_ge(s("a_s"), 2 * j + b + 1)
                    dve.tensor_tensor(pa[:, b, :], ps[:, 2 * b * BANK:2 * (b + 1) * BANK], gamma[:, j, :],
                                      ALU.mult).then_inc(s("pa"), 1)
                if j == 1:
                    dve.wait_ge(s("w_rest_hi"), 1)
                    dve.tensor_tensor(w_lo[:, W_CQ:NW], raw2[:, W_CQ:NW], w_hi[:, W_CQ:NW].bitcast(F32),
                                      ALU.subtract).then_inc(s("w_rest_lo"), 1)
            dve.wait_ge(s("a_pv"), JI)
            dve.tensor_copy(ret[:, 0:BANK], bank(4)).then_inc(s("ret"), 1)
            dve.wait_ge(s("a_y"), 1)
            y = tmp[:, 0:2 * BANK]
            neg = tmp[:, 2 * BANK:4 * BANK]
            dve.tensor_tensor(y.rearrange("p (c d) -> p c d", d=D), ps[:, 0:2 * BANK].rearrange("p (c d) -> p c d", d=D),
                              plain[:, K_BOA:K_BOA + D].unsqueeze(1).broadcast_to([P, B * JI, D]), ALU.add).then_inc(s("a_yb"), 1)
            dve.wait_ge(s("a_yb"), 1)
            dve.tensor_scalar(neg, y, 0.0, plain[:, C_SLOPE:C_SLOPE + 1], ALU.min, ALU.mult).then_inc(s("a_neg"), 1)
            dve.wait_ge(s("a_neg"), 1)
            dve.wait_ge(s("w_rest_lo"), 1)
            dve.wait_ge(s("b_emb"), 1)
            for b in range(B):
                dve.tensor_copy(h[:, b * J + JI, :], bank(3, b * D, (b + 1) * D)).then_inc(s("h1t"), 1)
            for b in range(B):
                view = [v.rearrange("p (j b d) -> p b j d", b=B, d=D)[:, b, :, :] for v in (y, neg)]
                dve.scalar_tensor_tensor(out=h[:, b * J:b * J + JI, :], in0=view[0], scalar=0.0, in1=view[1],
                                         op0=ALU.max, op1=ALU.add).then_inc(s("h1"), 1)
            first, second = norm_dve(dve, "c")
            dve.wait_ge(s("h1t"), 2)
            dve.wait_ge(s("h1"), 2)
            first(0)
            first(1)
            second(0)
            second(1)
            for n, (b, u) in enumerate(CU):
                if u < 3:
                    cols = slice(u * CH, (u + 1) * CH)
                    dve.wait_ge(s("c_hi"), 6 * b + u + 1)
                    dve.tensor_tensor(qc_lo[b][:, cols], bank(n % 6, 0, CH), qc_hi[b][:, cols].bitcast(F32),
                                      ALU.subtract).then_inc(s("c_proj_read"), 1)
                elif u < 6:
                    cols = slice((u - 3) * CH, (u - 2) * CH)
                    dve.wait_ge(s("c_hi"), 6 * b + u + 1)
                    dve.tensor_tensor(kc[b][D:P, cols], bank(n % 6, 0, CH)[D:P, :], kc[b][D:P, cols].bitcast(F32),
                                      ALU.subtract).then_inc(s("c_proj_read"), 1)
                else:
                    dve.wait_ge(s("c_proj"), n + 1)
                    t0, t1 = (0, 8) if u == 6 else (8, 9)
                    dve.tensor_copy(vc[:, (b * J + t0) * D:(b * J + t1) * D], bank(n % 6, 0, (t1 - t0) * D))\
                       .then_inc(s("c_proj_read"), 1)

            def c_scale_v(n):
                b, j = CSTEP[n]
                den, inv = small[:, 4 + n % 2:5 + n % 2], small[:, 6 + n % 2:7 + n % 2]
                dve.wait_ge(s("c_exp"), n + 1)
                dve.reciprocal(inv, den).then_inc(s("c_inv"), 1)
                dve.wait_ge(s("c_inv"), n + 1)
                if n >= 2:
                    dve.wait_ge(s("c_pv"), n - 1)
                dve.tensor_scalar(vs[n % 2], vc[:, (b * J + j) * D:(b * J + j + 1) * D], inv, None, ALU.mult)\
                   .then_inc(s("c_vs"), 1)

            def c_add(b):
                t = slice(b * J, (b + 1) * J)
                dve.wait_ge(s("c_pv"), J * (b + 1))
                dve.tensor_tensor(h[:, t, :], ps[:, 6 * BANK:6 * BANK + J * D].rearrange("p (j d) -> p j d", d=D),
                                  h[:, t, :], ALU.add).then_inc(s("h2"), 1)

            for n, (b, j) in enumerate(CSTEP):
                o, w = (n % 2) * 3 * BANK, c_width(j)
                dve.wait_ge(s("c_s"), n + 1)
                diag = ps[:, o + j * P:o + (j + 1) * P]
                dve.tensor_tensor(diag, diag, plain[:, K_MASK:K_MASK + P], ALU.add).then_inc(s("c_mask"), 1)
                if j == 0:
                    rest = ps[:, o + P:o + S]
                    dve.tensor_scalar(rest, rest, MASKED, None, ALU.add).then_inc(s("c_mask0"), 1)
                    dve.wait_ge(s("c_mask0"), b + 1)
                dve.wait_ge(s("c_mask"), n + 1)
                dve.reduce_max(small[:, n % 2:n % 2 + 1], ps[:, o:o + w], AX_X, negate=True).then_inc(s("c_max"), 1)
                dve.wait_ge(s("c_max"), n + 1)
                dve.tensor_scalar(small[:, 2 + n % 2:3 + n % 2], small[:, n % 2:n % 2 + 1], D ** -0.5, None,
                                  ALU.mult).then_inc(s("c_bias"), 1)
                if n >= 1:
                    c_scale_v(n - 1)
                if n == J:
                    c_add(0)
            c_scale_v(len(CSTEP) - 1)
            c_add(1)
            first, second = norm_dve(dve, "d")
            dve.wait_ge(s("small_in"), 48)
            dve.tensor_scalar(onehot[:, :], route_all[:, :], plain[0:EXPERTS, C_EIDX:C_EIDX + 1], None, ALU.is_equal)\
               .then_inc(s("d_onehot"), 1)
            dve.wait_ge(s("h2"), 2)
            first(0)
            first(1)
            second(0)
            second(1)
            dve.wait_ge(s("d_bp"), 1)
            for l in range(LAYERS):
                dve.tensor_scalar(bias_g[:, l, :], bank(4, l * GROUPS, (l + 1) * GROUPS), plain[:, C_BS + l:C_BS + l + 1], None,
                                  ALU.add).then_inc(s("d_bias"), 1)
            dve.wait_ge(s("d_bias"), LAYERS)
            for l in range(LAYERS):
                for c in range(NDC):
                    n = l * NDC + c
                    cols = slice(c * DW, (c + 1) * DW)
                    if l == 0:
                        dve.wait_ge(s("d_h0"), -(-(c + 1) * DW // CH))
                    else:
                        dve.wait_ge(s("d_h1"), c + 1)
                    dve.tensor_tensor(res[:, cols].rearrange("p (g t) -> p g t", t=GT),
                                      hid[l][:, cols].rearrange("p (g t) -> p g t", t=GT),
                                      bias_g[:, l, c * DG:(c + 1) * DG].unsqueeze(2).broadcast_to([P, DG, GT]),
                                      ALU.add).then_inc(s("d_res"), 1)
                    dve.wait_ge(s("d_res"), n + 1)
                    dve.wait_ge(s("d_f"), n + 1)
                    dve.tensor_tensor(res[:, cols], bank(n % 6, 0, DW), res[:, cols], ALU.add).then_inc(s("d_z"), 1)
            for b in range(B):
                t = slice(b * J, (b + 1) * J)
                dve.wait_ge(s("d_o"), b + 1)
                dve.tensor_tensor(sq[:, t, :], ps[:, 2 * b * BANK:2 * b * BANK + J * D].rearrange("p (j d) -> p j d", d=D),
                                  plain[:, K_BOD:K_BOD + D].unsqueeze(1).broadcast_to([P, J, D]), ALU.add).then_inc(s("d_ob"), 1)
                dve.wait_ge(s("d_ob"), b + 1)
                dve.tensor_tensor(h[:, t, :], sq[:, t, :], h[:, t, :], ALU.add).then_inc(s("h3"), 1)
            first, second = norm_dve(dve, "e")
            dve.sem_inc(s("e_acc_read"), AF0)

            def weights_of(hp):
                src = raw1[:, bass.ds(hp * 4 * P, 4 * P)]
                dve.tensor_copy(w_hi[:, 0:4 * P], src).then_inc(s("e_whi"), 1)
                dve.wait_ge(s("e_whi"), hp + 1)
                dve.tensor_tensor(w_lo[:, 0:4 * P], src, w_hi[:, 0:4 * P].bitcast(F32), ALU.subtract).then_inc(s("e_w"), 1)

            def split_unit(n, u, b, src):
                hd, cols = u // NCH % 2, slice(u % NCH * CH, (u % NCH + 1) * CH)
                dve.wait_ge(s("e_proj"), n + 1)
                hi = (q_hi if u < 2 * NCH else k_e)[b][:, hd, cols]
                dve.tensor_copy(hi, src).then_inc(s("e_hi"), 1)
                dve.wait_ge(s("e_hi"), n + 1)
                if u < 2 * NCH:
                    dve.tensor_tensor(q_lo[b][:, hd, cols], src, hi.bitcast(F32), ALU.subtract).then_inc(s("e_proj_read"), 1)
                else:
                    lo = k_e[b][D:P, hd, cols]
                    dve.tensor_tensor(lo, src[D:P, :], lo.bitcast(F32), ALU.subtract).then_inc(s("e_proj_read"), 1)

            dve.wait_ge(s("qk_in"), 16)
            weights_of(0)
            dve.wait_ge(s("h3"), 2)
            first(0)
            first(1)
            second(0)
            second(1)
            for u in range(UNITS):
                split_unit(u, u, 0, bank(4 + u % 4, 0, CH))

            def pair_work(it, last):
                for b in range(B):
                    if not (last and b == B - 1):
                        for u in range(UNITS):
                            split_unit(it * (B * UNITS) + ((b + 1) * UNITS + u), u, 1 - b, bank(7, 0, CH))
                    if b == 0 and not last:
                        weights_of(it + 1)
                    for c in range(NCH):
                        dve.wait_ge(s("e_pv"), it * (B * STEPS) + (b * STEPS + STEPS - NCH + c + 1 + PV0))
                        dve.tensor_copy(wv[:, bass.ds(it, 1), b, c * CH:(c + 1) * CH].rearrange("p a t -> p (a t)"),
                                        bank(c, 0, CH)).then_inc(s("e_acc_read"), 1)

            with dve.Fori(0, PAIRS - 1) as it:
                pair_work(it, False)
            pair_work(PAIRS - 1, True)
            for b in range(B):
                t = slice(b * J, (b + 1) * J)
                dve.wait_ge(s("e_o"), b + 1)
                o = (3 + 2 * b) * BANK
                dve.scalar_tensor_tensor(out=h[:, t, :], in0=ps[:, o:o + J * D].rearrange("p (j d) -> p j d", d=D), scalar=0.0,
                                         in1=h[:, t, :], op0=ALU.max, op1=ALU.add).then_inc(s("h4"), 1)
            first, second = norm_dve(dve, "f")
            dve.wait_ge(s("h4"), 2)
            first(0)
            first(1)
            second(0)
            second(1)
            dve.wait_ge(s("sel_in"), 16)
            dve.tensor_copy(sel, sel_in).then_inc(s("f_sel"), 1)
            step = [0]

            def chain(ins):
                step[0] += 1
                ins.then_inc(s("f_gate"), 1)
                dve.wait_ge(s("f_gate"), step[0])

            def bc(v):
                return v.unsqueeze(2).broadcast_to([P, NT, ME])

            rev = plain[:, K_REV:K_REV + ME].unsqueeze(1).broadcast_to([P, NT, ME])
            shifted, expd, prob, eq, ranked, sel1, rest = gate
            top, total, inv, p1, r1, p2, r2, winv = per_tok
            logits = bank(0, 0, NT * ME).rearrange("p (t e) -> p t e", e=ME)
            dve.wait_ge(s("f_r"), 1)
            chain(dve.reduce_max(top, logits, AX_X))
            dve.tensor_tensor(shifted, logits, bc(top), ALU.subtract).then_inc(s("f_shift"), 1)
            dve.wait_ge(s("f_exp"), 1)
            chain(dve.reduce_sum(total, expd, AX_X))
            chain(dve.reciprocal(inv, total))
            chain(dve.tensor_tensor(prob, expd, bc(inv), ALU.mult))
            chain(dve.reduce_max(p1, prob, AX_X))
            chain(dve.tensor_tensor(eq, prob, bc(p1), ALU.is_equal))
            chain(dve.tensor_tensor(ranked, eq, rev, ALU.mult))
            chain(dve.reduce_max(r1, ranked, AX_X))
            chain(dve.tensor_tensor(sel1, ranked, bc(r1), ALU.is_equal))
            chain(dve.scalar_tensor_tensor(out=rest, in0=sel1, scalar=-2.0, in1=prob, op0=ALU.mult, op1=ALU.add))
            chain(dve.reduce_max(p2, rest, AX_X))
            chain(dve.tensor_tensor(eq, rest, bc(p2), ALU.is_equal))
            chain(dve.tensor_tensor(ranked, eq, rev, ALU.mult))
            chain(dve.reduce_max(r2, ranked, AX_X))
            chain(dve.tensor_tensor(eq, ranked, bc(r2), ALU.is_equal))
            chain(dve.tensor_tensor(eq, eq, sel1, ALU.add))
            chain(dve.tensor_tensor(winv, p1, p2, ALU.add))
            chain(dve.tensor_scalar(winv, winv, 1e-12, None, ALU.max))
            chain(dve.reciprocal(winv, winv))
            chain(dve.tensor_tensor(prob, prob, eq, ALU.mult))
            chain(dve.tensor_tensor(prob, prob, bc(winv), ALU.mult))
            dve.wait_ge(s("f_zero"), 1)
            chain(dve.tensor_copy(cc[:, :, 0:ME], prob))
            dve.tensor_tensor(cc[:, :, ME:2 * ME], prob, cc[:, :, 0:ME].bitcast(F32), ALU.subtract).then_inc(s("f_cc"), 1)
            for n, (ch, u) in enumerate(FUNITS):
                cols = slice(ch * CH, (ch + 1) * CH)
                dve.wait_ge(s("f_gelu"), n + 1)
                dve.wait_ge(s("f_cb"), n + 1)
                dve.tensor_tensor(act_f[:, u, cols], act_f[:, u, cols], bank(n % 4, 0, CH), ALU.mult).then_inc(s("f_hc"), 1)
            for b in range(B):
                t = slice(b * J, (b + 1) * J)
                o = (4 + 2 * b) * BANK
                dve.wait_ge(s("f_y"), b + 1)
                dve.tensor_tensor(xc[:, t, :], xc[:, t, :], ps[:, o:o + J * D].rearrange("p (j d) -> p j d", d=D),
                                  ALU.add).then_inc(s("f_moe"), 1)
                dve.wait_ge(s("f_moe"), b + 1)
                dve.tensor_tensor(h[:, t, :], h[:, t, :], xc[:, t, :], ALU.add).then_inc(s("h5"), 1)

        @block.scalar
        def _(act):
            act.wait_ge(s("plain_in"), 16)
            for c in range(4):
                cols = slice(c * BANK, (c + 1) * BANK)
                act.wait_ge(s("a_q"), c + 1)
                act.activation(qa_hi[:, cols], bank(4 + c % 2), ACT.Identity, bias=plain[:, C_BQ:C_BQ + 1]).then_inc(s("qa_hi"), 1)
                act.wait_ge(s("a_k"), c + 1)
                act.activation(ka[:, cols], bank(6 + c % 2), ACT.Identity, bias=plain[:, C_BK:C_BK + 1]).then_inc(s("ka_hi"), 1)
            act.wait_ge(s("a_pv"), JI)
            act.copy(ret[:, BANK:2 * BANK], bank(5)).then_inc(s("ret"), 1)
            act.wait_ge(s("b_tr"), 1)
            act.copy(powers_t[:, :, :].rearrange("p b t -> p (b t)"), ps[0:TURNS * DEGS, 2 * BANK:2 * BANK + B * P])\
               .then_inc(s("powers_t"), 1)
            transposes_act(act, "c")
            for n, (b, u) in enumerate(CU):
                if u < 6:
                    dst = (qc_hi if u < 3 else kc)[b][:, u % 3 * CH:(u % 3 + 1) * CH]
                    act.wait_ge(s("c_proj"), n + 1)
                    act.copy(dst, bank(n % 6, 0, CH)).then_inc(s("c_hi"), 1)
            for n, (b, j) in enumerate(CSTEP):
                o, w = (n % 2) * 3 * BANK, c_width(j)
                act.wait_ge(s("c_bias"), n + 1)
                if n >= 2:
                    act.wait_ge(s("c_pv"), n - 1)
                    act.wait_ge(s("c_inv"), n - 1)
                act.activation(pc[n % 2][:, 0:w], ps[:, o:o + w], ACT.Exp, bias=small[:, 2 + n % 2:3 + n % 2],
                               scale=D ** -0.5, accum_out=small[:, 4 + n % 2:5 + n % 2]).then_inc(s("c_exp"), 1)
            transposes_act(act, "d")
            for n in range(B * NCH):
                act.wait_ge(s("d_in"), n + 1)
                act.activation(hid[0][:, n * CH:(n + 1) * CH], bank(n % 4, 0, CH), ACT.Relu, bias=plain[:, C_BI:C_BI + 1])\
                   .then_inc(s("d_h0"), 1)
            for l in range(LAYERS):
                for c in range(NDC):
                    cols = slice(c * DW, (c + 1) * DW)
                    act.wait_ge(s("d_z"), l * NDC + c + 1)
                    act.activation(hid[l + 1][:, cols], res[:, cols], ACT.Relu).then_inc(s(f"d_h{l + 1}"), 1)
            transposes_act(act, "e")
            for t in range(NT):
                act.wait_ge(s("e_v"), t + 1)
                act.copy(v_all[:, t, :], bank(t % 4)).then_inc(s("e_v_read"), 1)
            with act.Fori(0, PAIRS) as it:
                for n in range(B * STEPS):
                    o = (3 + 2 * (n % 2)) * BANK
                    act.wait_ge(s("e_qk"), it * (B * STEPS) + (n + 1))
                    act.wait_ge(s("e_pv"), it * (B * STEPS) + (n + 1))
                    act.activation(pe_ring[:, n % 3, :, :],
                                   ps[:, o:o + 2 * BANK].rearrange("p (h t) -> p h t", h=2)[:, :, 0:CH],
                                   ACT.Sigmoid, scale=float(D) ** 0.5).then_inc(s("e_sig"), 1)
            transposes_act(act, "f")
            act.wait_ge(s("f_shift"), 1)
            act.activation(gate[1], gate[0], ACT.Exp).then_inc(s("f_exp"), 1)
            for n, (ch, u) in enumerate(FUNITS):
                act.wait_ge(s("f_1"), n + 1)
                act.activation(act_f[:, u, ch * CH:(ch + 1) * CH], bank(1 + n % 4, 0, CH), ACT.Gelu,
                               bias=plain[:, C_B1 + u:C_B1 + u + 1]).then_inc(s("f_gelu"), 1)
            for n, (b, j0, k) in enumerate(TG):
                act.wait_ge(s("f_ctr"), n + 1)
                act.copy(c_hl[:, (b * J + j0) * P:(b * J + j0 + k) * P], bank(6 + n % 2, 0, k * P)).then_inc(s("f_ct"), 1)


def arrays_of(inputs):
    g = {k: np.asarray(v) for k, v in inputs.items()}
    f = np.float32

    def twice(w):
        return np.concatenate([w, w], 0)

    def dup(w):
        return np.concatenate([w, w], 1)

    def heads(w):
        return np.moveaxis(w.reshape(D, D, HEADS), 2, 0)

    xt = g["x"].reshape(B * T_IMG, D).T
    w1 = np.moveaxis(g["L1_ffn_w1"], 0, 1).reshape(D, ME * D)
    b2 = g["L1_ffn_b2"]
    w_stack = np.concatenate([
        twice(dup(g["L0_tok_Wq"])), twice(dup(g["L0_tok_Wk"])), twice(g["L0_tok_Wv"]),
        twice(dup(g["L0_attn_Wq"].T)), twice(dup(g["L0_attn_Wk"].T)), twice(g["L0_attn_Wv"].T),
        twice(g["L0_ffn_Wi"].T),
        twice(np.concatenate(list(heads(g["L1_attn_Wv"])), 1)),
        twice(g["L1_ffn_router_w"].T), twice(w1),
        np.concatenate([b2, b2, np.zeros((P - 2 * ME, D), f)], 0),
    ], 1)
    hq, hk = heads(g["L1_attn_Wq"]), heads(g["L1_attn_Wk"])
    w_qk = twice(np.concatenate([np.concatenate([dup(hq[2 * p]), dup(hq[2 * p + 1]), dup(hk[2 * p]), dup(hk[2 * p + 1])], 1)
                                 for p in range(PAIRS)], 1))
    zero = np.zeros((D, D), f)
    wo = g["L0_tok_Wo"]

    def row(v, n=P):
        return np.broadcast_to(v.reshape(1, -1), (n, v.size))

    def col(v):
        return v.reshape(P, 1)

    b1 = g["L1_ffn_b1"].reshape(ME // 2, P)
    cols = [col(np.tile(g["L0_tok_bq"], 2)), col(np.tile(g["L0_tok_bk"], 2)), col(g["L0_ffn_bi"])]
    cols += [col(g["L0_ffn_bs"][l, 0]) for l in range(LAYERS)] + [col(b1[u]) for u in range(ME // 2)]
    cols += [col(np.broadcast_to(g["L0_tok_prelu_a"].reshape(1), (P,))), col(np.arange(P, dtype=f))]
    mask = np.where(np.arange(P)[None, :] >= np.arange(P)[:, None], f(MASKED), f(0)).astype(f)
    w_plain = np.concatenate([
        np.block([[wo, zero], [zero, wo]]),
        *[g["L0_ffn_Ws"][l, 0].T for l in range(LAYERS)],
        g["L0_ffn_Wo"].T, np.eye(P, dtype=f), mask,
        row(g["L0_tok_bv"]), row(g["L0_tok_bo"]), row(g["L0_ffn_bo"]),
        row(np.arange(ME, 0, -1).astype(f)), *cols], 1)
    woe = g["L1_attn_Wo"].reshape(D, HEADS, D)
    wo_pairs = [np.concatenate([woe[:, 2 * p], woe[:, 2 * p + 1]], 0) for p in range(PAIRS)]
    w2 = g["L1_ffn_w2"].reshape(ME // 2, P, D)
    sel = np.zeros((P, ME * D), f)
    for e in range(ME):
        sel[[e, e + ME], e * D:(e + 1) * D] = 1
    w_late = np.concatenate([*wo_pairs, *w2, sel], 1)
    ins = {
        "x_stack": twice(xt), "w_stack": w_stack, "w_plain": w_plain, "w_qk": w_qk, "w_late": w_late,
        "gamma_t": g["L0_tok_d_gamma_batched"].T.reshape(JI, P, T_IMG),
        "w_br": np.moveaxis(g["L0_ffn_br"], 0, 1).reshape(EXPERTS, LAYERS * HID),
        "w_poly": g["L0_txt_poly_coeffs"].reshape(TURNS * DEGS, D),
        "ids": g["x_txt"].T, "turns": g["L0_txt_turns"],
        "route": g["L0_ffn_route_id"].reshape(1, GROUPS),
        "w_route": np.moveaxis(g["L0_ffn_Wr"], (1, 3, 0, 2), (0, 1, 2, 3)).reshape(EXPERTS, HID, LAYERS * HID),
    }
    return {k: np.ascontiguousarray(v) for k, v in ins.items()}


def kernel(**inputs):
    import concourse.bacc as bacc
    from concourse.bass_utils import run_bass_kernel_spmd

    nc = bacc.Bacc("TRN2", target_bir_lowering=False, num_devices=1)
    arrays = arrays_of(inputs)
    args = {k: nc.dram_tensor(k, a.shape, mybir.dt.from_np(a.dtype), kind="ExternalInput").ap() for k, a in arrays.items()}
    out = nc.dram_tensor("out", (B, S, D), F32, kind="ExternalOutput").ap()
    program(nc, **args, out=out)
    result = run_bass_kernel_spmd(nc, [arrays], core_ids=[0])
    return result.results[0]["out"]
```

```python
from contextlib import ExitStack

import numpy as np

import concourse.bass as bass
from concourse import mybir

ALU = mybir.AluOpType
ACT = mybir.ActivationFunctionType
F32 = mybir.dt.float32
F32R = mybir.dt.float32r
I32 = mybir.dt.int32
AX_X = mybir.AxisListType.X

P = 128
B = 2
D = 64
T_IMG = 1024
JI = T_IMG // P
T_TXT = 128
J = JI + 1
S = J * P
NT = B * J
TOK = B * S
TURNS, DEGS = 4, 5
HID = 128
LAYERS, EXPERTS = 2, 16
GROUPS = 64
GT = TOK // GROUPS
HEADS = 8
PAIRS = HEADS // 2
ME = 8
EARLY = 56
WG = LAYERS * HID
EPS = 1e-5
MASKED = -1e10
CH = 384
NCH = S // CH
BANK = 512

W_AQ, W_AK, W_AV = 0, 128, 256
W_CQ, W_CK, W_CV = 320, 448, 576
W_DI = 640
W_EV = 768
W_FR = W_EV + HEADS * D
W_F1 = W_FR + ME
W_FB2 = W_F1 + ME * D
NW = W_FB2 + D
K_WOA = 0
K_WS = 128
K_WOD = K_WS + LAYERS * HID
K_ID = K_WOD + D
K_MASK = K_ID + P
K_BVA, K_BOA, K_BOD = K_MASK + P, K_MASK + P + D, K_MASK + P + 2 * D
K_REV = K_BOD + D
K_COL = K_REV + ME
NK = K_COL + 11
C_BQ, C_BK, C_BI, C_BS, C_B1, C_SLOPE, C_EIDX = (K_COL + n for n in (0, 1, 2, 3, 5, 9, 10))


def program(nc, x_stack, w_stack, w_plain, w_qk, w_late, gamma_t, w_br, w_poly, ids, turns, route, w_route, out):
    with ExitStack() as ctx:
        def sb(name, shape, dt=F32):
            return ctx.enter_context(nc.sbuf_tensor(name, shape, dt))

        sems = {}

        def s(name):
            if name not in sems:
                sems[name] = ctx.enter_context(nc.semaphore(name))
            return sems[name]

        raw1 = sb("raw1", [P, 2048])
        raw2 = sb("raw2", [P, NW])
        w_hi = sb("w_hi", [P, NW], F32R)
        w_lo = sb("w_lo", [P, NW], F32R)
        plain = sb("plain", [P, NK])
        halves = sb("halves", [P, TOK + 2 * 6 * S], F32R)
        big = sb("big", [P, GROUPS * LAYERS * HID])
        mid = sb("mid", [P, 4 * TOK])
        tmp = sb("tmp", [P, B * J * P])
        br = sb("br", [EXPERTS, LAYERS * HID])
        idx = sb("idx", [P, B], I32)
        route_row = sb("route_row", [1, GROUPS], I32)
        route_all = sb("route_all", [EXPERTS, GROUPS], I32)
        onehot = sb("onehot", [EXPERTS, GROUPS])
        stat = sb("stat", [P, 4, NT])
        tok4i = sb("tok4i", [P, B * TURNS], I32)
        small = sb("small", [P, 16])
        ps = ctx.enter_context(nc.psum_tensor("ps", [P, 8 * BANK], F32))

        def bank(n, lo=0, hi=BANK):
            return ps[:, n * BANK + lo:n * BANK + hi]

        h = raw2[:, 0:NT * D].rearrange("p (t d) -> p t d", d=D)
        wo_e = raw2[:, NT * D:NT * D + PAIRS * D]
        w2_f = raw2[:, NT * D + PAIRS * D:NT * D + 2 * PAIRS * D]
        bias_g = raw2[:, NT * D + 2 * PAIRS * D:NT * D + 2 * PAIRS * D + LAYERS * GROUPS].rearrange("p (l g) -> p l g", l=LAYERS)
        ident = plain[:, K_ID:K_ID + P]
        x_hl = halves[:, 0:TOK]
        split = halves[:, TOK + 2 * 5 * S:TOK + 2 * 6 * S].rearrange("p (t c) -> p t c", c=P)
        xc = tmp[:, 0:NT * D].rearrange("p (t d) -> p t d", d=D)
        sq = tmp[:, NT * D:2 * NT * D].rearrange("p (t d) -> p t d", d=D)

        def stacked(sec, n):
            return w_hi[:, sec:sec + n], w_lo[:, sec:sec + n]

        xa = halves[:, 0:B * T_IMG]
        qa_hi = halves[:, TOK:TOK + B * T_IMG]
        qa_lo = halves[:, TOK + B * T_IMG:TOK + 2 * B * T_IMG]
        ka = halves[:, TOK + 2 * B * T_IMG:TOK + 3 * B * T_IMG]
        va = big[:, EARLY * WG:EARLY * WG + B * JI * D]
        o = EARLY * WG + B * JI * D
        poly = big[0:TURNS * DEGS, o:o + D]
        powers_t = big[0:TURNS * DEGS, o + D:o + D + B * P].rearrange("p (b t) -> p b t", b=B)
        o += D + B * P
        tok4 = big[:, o:o + 8 * B * TURNS].rearrange("p (n t) -> p n t", n=8)
        o += 8 * B * TURNS
        powers = big[:, o:o + B * TURNS * DEGS].rearrange("p (b t k) -> p b t k", b=B, t=TURNS)
        gamma = mid[:, 0:JI * T_IMG].rearrange("p (j t) -> p j t", j=JI)
        ret = mid[:, JI * T_IMG:JI * T_IMG + T_IMG]
        ASTEPS = B * JI
        as_bank = (0, 2, 6)
        pa = [v[:, n * T_IMG:(n + 1) * T_IMG] for v in (tmp, raw1) for n in range(2)]
        qc_hi = [halves[:, TOK + b * 3 * S:TOK + b * 3 * S + S] for b in range(B)]
        qc_lo = [halves[:, TOK + b * 3 * S + S:TOK + b * 3 * S + 2 * S] for b in range(B)]
        kc = [halves[:, TOK + b * 3 * S + 2 * S:TOK + b * 3 * S + 3 * S] for b in range(B)]
        vc = mid[:, 0:NT * D]
        pc = [mid[:, NT * D + n * S:NT * D + n * S + S] for n in range(3)]
        vs = [mid[:, NT * D + 3 * S + n * D:NT * D + 3 * S + n * D + D] for n in range(3)]
        hid = [mid[:, n * TOK:(n + 1) * TOK] for n in range(3)]
        res = mid[:, 3 * TOK:4 * TOK]
        wr = big[:, :].rearrange("p (g l n) -> p g l n", g=GROUPS, l=LAYERS)
        v_all = mid[:, :].rearrange("p (t n) -> p t n", n=HEADS * D)
        wv = big[:, 0:PAIRS * B * S].rearrange("p (hp b t) -> p hp b t", hp=PAIRS, b=B)
        pe_ring = big[:, PAIRS * B * S:PAIRS * B * S + 3 * 2 * CH].rearrange("p (n h t) -> p n h t", n=3, h=2)
        v_cur = [big[:, PAIRS * B * S + 6 * CH + b * S:PAIRS * B * S + 6 * CH + b * S + S]
                 .rearrange("p (j n) -> p j n", n=P) for b in range(B)]
        q_hi, q_lo, k_e = ([halves[:, TOK + b * 6 * S + m * 2 * S:TOK + b * 6 * S + (m + 1) * 2 * S]
                            .rearrange("p (h t) -> p h t", h=2) for b in range(B)] for m in range(3))

        act_f = mid[:, :].rearrange("p (u t) -> p u t", u=ME // 2)
        c_hl = halves[:, TOK:2 * TOK]
        cc = halves[:, 2 * TOK:3 * TOK].rearrange("p (t c) -> p t c", c=P)
        sel = halves[:, 3 * TOK:3 * TOK + ME * D]
        sel_in = big[:, PAIRS * B * S + 6 * CH + B * S:PAIRS * B * S + 6 * CH + B * S + ME * D]
        slot = [tmp[:, (NT * D) + n * NT * ME:(NT * D) + (n + 1) * NT * ME] for n in range(8)]
        gate = [v.rearrange("p (t e) -> p t e", e=ME) for v in slot[:7]]
        per_tok = [slot[7][:, n * NT:(n + 1) * NT] for n in range(8)]

        DG = 8
        DW = DG * GT
        NDC = GROUPS // DG
        DBC = NDC // B
        D_IN_BANK = (0, 1, 2, 6, 7, 6)
        D_OUT_BANK = (6, 0)

        STEPS = J * NCH
        PV0 = 3
        AF0 = NCH
        UNITS = 4 * NCH
        FUNITS = [(ch, u) for ch in range(B * NCH) for u in range(ME // 2)]

        block = ctx.enter_context(nc.Block())

        @block.sync
        def _(sp):
            sp.dma_start(raw1[:, :], x_stack).then_inc(s("x_in"), 16)
            sp.dma_start(raw2[:, 0:W_CQ], w_stack[:, 0:W_CQ]).then_inc(s("w_first_in"), 16)
            sp.dma_start(plain[:, :], w_plain).then_inc(s("plain_in"), 16)
            sp.dma_start(idx[:, :], ids).then_inc(s("ids_in"), 16)
            for j in range(JI):
                sp.dma_start(gamma[:, j, :], gamma_t[j]).then_inc(s(f"gamma_in{j}"), 16)
            sp.dma_start(raw2[:, W_CQ:NW], w_stack[:, W_CQ:NW]).then_inc(s("w_rest_in"), 16)
            sp.dma_start(br[:, :], w_br).then_inc(s("small_in"), 16)
            sp.dma_start(poly[:, :], w_poly).then_inc(s("small_in"), 16)
            sp.dma_start(route_row[:, :], route).then_inc(s("route_in"), 16)
            sp.dma_start(route_all[:, :], route.broadcast_to([EXPERTS, GROUPS])).then_inc(s("small_in"), 16)
            sp.wait_ge(s("route_in"), 16)
            for g0, g1 in ((0, EARLY), (EARLY, GROUPS)):
                if g0:
                    sp.wait_ge(s("a_pv"), JI)
                    sp.dma_start(raw1[:, :], w_qk).then_inc(s("qk_in"), 16)
                    sp.wait_ge(s("b_emb"), 1)
                with sp.Fori(g0 // 4, g1 // 4) as g4:
                    for n in range(4):
                        e = sp.value_load(route_row[0:1, bass.ds(g4 * 4 + n, 1)], min_val=0, max_val=EXPERTS - 1)
                        sp.dma_start(big[:, bass.ds((g4 * 4 + n) * WG, WG)],
                                     w_route[bass.ds(e, 1), :, :].rearrange("e p n -> p (e n)")).then_inc(s(f"wr_in{n}"), 16)
            sp.wait_ge(s("w_rest_lo"), 1)
            sp.dma_start(raw2[:, NT * D:NT * D + 2 * PAIRS * D], w_late[:, 0:2 * PAIRS * D]).then_inc(s("late_in"), 16)
            sp.wait_ge(s("h3"), 2)
            sp.dma_start(sel_in, w_late[:, 2 * PAIRS * D:2 * PAIRS * D + ME * D]).then_inc(s("sel_in"), 16)
            for b in range(B):
                sp.wait_ge(s("h5"), b + 1)
                sp.dma_start(out[b].rearrange("(j p) d -> p j d", p=P), h[:, b * J:(b + 1) * J, :]).then_inc(s("out"), 16)
            sp.wait_ge(s("out"), 32)

        def nth(st, b):
            return B * "cdef".index(st) + b + 1

        @block.gpsimd
        def _(pool):
            pool.memset(stat[:, 3, :], -0.5).then_inc(s("expo"), 1)
            pool.wait_ge(s("ids_in"), 16)
            for b in range(B):
                pool.indirect_dma_start(tok4[:, 0, b * TURNS:(b + 1) * TURNS], None, turns,
                                        bass.IndirectOffsetOnAxis(ap=idx[:, b:b + 1], axis=0)).then_inc(s("turns_in"), 16)

            def rstd(st, b):
                t = slice(b * J, (b + 1) * J)
                pool.wait_ge(s(st + "_var"), b + 1)
                pool.tensor_tensor(stat[:, 2, t], stat[:, 1, t], stat[:, 3, t], ALU.pow).then_inc(s(st + "_rstd"), 1)

            pool.wait_ge(s("expo"), 1)
            for b in range(B):
                rstd("c", b)
            def d_res(n):
                l, c = n // NDC, n % NDC
                cols = slice(c * DW, (c + 1) * DW)
                if l == 0:
                    pool.wait_ge(s("d_h0"), NCH if c < DBC else B * NCH)
                else:
                    pool.wait_ge(s("d_h1"), c + 1)
                pool.tensor_tensor(res[:, cols].rearrange("p (g t) -> p g t", t=GT),
                                   hid[l][:, cols].rearrange("p (g t) -> p g t", t=GT),
                                   bias_g[:, l, c * DG:(c + 1) * DG].unsqueeze(2).broadcast_to([P, DG, GT]),
                                   ALU.add).then_inc(s("d_res"), 1)

            def d_bias_out(b):
                t = slice(b * J, (b + 1) * J)
                pool.wait_ge(s("norm_xc"), nth("d", b))
                pool.tensor_tensor(h[:, t, :], h[:, t, :], plain[:, K_BOD:K_BOD + D].unsqueeze(1).broadcast_to([P, J, D]),
                                   ALU.add).then_inc(s("d_hb"), 1)

            rstd("d", 0)
            d_bias_out(0)
            rstd("d", 1)
            pool.wait_ge(s("d_bias"), LAYERS)
            for n in range(LAYERS * NDC):
                if n == 2:
                    d_bias_out(1)
                d_res(n)
                if n == NDC + DBC + 2:
                    rstd("e", 0)
            rstd("e", 1)
            def v_copy(hp, b):
                pool.tensor_copy(v_cur[b], v_all[:, b * J:(b + 1) * J, bass.ds(hp * P, P)]).then_inc(s("e_vcur"), 1)

            for b in range(B):
                pool.wait_ge(s("e_v_read"), J * (b + 1))
                v_copy(0, b)
            with pool.Fori(1, PAIRS) as hp:
                for b in range(B):
                    pool.wait_ge(s("e_pv"), hp * (B * STEPS) + (b - 1) * STEPS + PV0)
                    v_copy(hp, b)
            pool.wait_ge(s("h4"), 2)
            pool.memset(cc.rearrange("p t c -> p (t c)").bitcast(F32), 0.0).then_inc(s("f_zero"), 1)
            for b in range(B):
                rstd("f", b)

        def product(pe, dst, stationary, moving_hi, moving_lo, sem=None):
            pe.matmul(dst, stationary, moving_hi, start=True, stop=False)
            m = pe.matmul(dst, stationary, moving_lo, start=False, stop=True)
            if sem is not None:
                m.then_inc(sem, 1)

        def product_w(pe, dst, w_pair, moving, sem=None):
            pe.matmul(dst, w_pair[0], moving, start=True, stop=False)
            m = pe.matmul(dst, w_pair[1], moving, start=False, stop=True)
            if sem is not None:
                m.then_inc(sem, 1)

        def norm_dve(dve, st):
            def first(b):
                t = slice(b * J, (b + 1) * J)
                dve.reduce_sum(stat[:, 0, t], h[:, t, :], AX_X).then_inc(s("norm_sum"), 1)
                dve.wait_ge(s("norm_sum"), nth(st, b))
                dve.scalar_tensor_tensor(out=xc[:, t, :], in0=stat[:, 0, t].unsqueeze(2).broadcast_to([P, J, D]),
                                         scalar=-1.0 / D, in1=h[:, t, :], op0=ALU.mult, op1=ALU.add).then_inc(s("norm_xc"), 1)
                dve.wait_ge(s("norm_xc"), nth(st, b))
                dve.tensor_tensor(sq[:, t, :], xc[:, t, :], xc[:, t, :], ALU.mult).then_inc(s("norm_sq"), 1)
                dve.wait_ge(s("norm_sq"), nth(st, b))
                dve.reduce_sum(stat[:, 1, t], sq[:, t, :], AX_X).then_inc(s("norm_ssq"), 1)
                dve.wait_ge(s("norm_ssq"), nth(st, b))
                dve.tensor_scalar(stat[:, 1, t], stat[:, 1, t], 1.0 / D, EPS, ALU.mult, ALU.add).then_inc(s(st + "_var"), 1)

            def second(b):
                t = slice(b * J, (b + 1) * J)
                dve.wait_ge(s(st + "_rstd"), b + 1)
                dve.tensor_tensor(xc[:, t, :], xc[:, t, :], stat[:, 2, t].unsqueeze(2).broadcast_to([P, J, D]),
                                  ALU.mult).then_inc(s("norm_xn"), 1)
                dve.wait_ge(s("norm_xn"), nth(st, b))
                dve.tensor_copy(split[:, t, 0:D], xc[:, t, :]).then_inc(s("norm_xhi"), 1)
                dve.wait_ge(s("norm_xhi"), nth(st, b))
                dve.tensor_tensor(split[:, t, D:P], xc[:, t, :], split[:, t, 0:D].bitcast(F32),
                                  ALU.subtract).then_inc(s(st + "_split"), 1)
            return first, second

        TG = [(b, j0, n) for b in range(B) for j0, n in ((0, 4), (4, 4), (8, 1))]

        def transposes_pe(pe, st, b):
            pe.wait_ge(s(st + "_split"), b + 1)
            for n in range(3 * b, 3 * b + 3):
                _, j0, k = TG[n]
                if n >= 2:
                    pe.wait_ge(s(st + "_xt"), n - 1)
                for i in range(k):
                    m = pe.transpose(bank(6 + n % 2, i * P, (i + 1) * P), split[:, b * J + j0 + i, :].bitcast(F32), ident)
                m.then_inc(s(st + "_tr"), 1)

        def transposes_act(act, st, b):
            for n in range(3 * b, 3 * b + 3):
                _, j0, k = TG[n]
                act.wait_ge(s(st + "_tr"), n + 1)
                act.copy(x_hl[:, (b * J + j0) * P:(b * J + j0 + k) * P], bank(6 + n % 2, 0, k * P)).then_inc(s(st + "_xt"), 1)

        NX = [3, 6]

        CU = [(b, u) for b in range(B) for u in range(8)]
        CSTEP = [(b, j) for b in range(B) for j in range(J)]

        def c_width(j):
            return S if j == 0 else (j + 1) * P

        @block.tensor
        def _(pe):
            pe.wait_ge(s("w_first_lo"), 1)
            for c in range(4):
                pe.wait_ge(s("xa_lo"), c + 1)
                cols = slice(c * BANK, (c + 1) * BANK)
                if c >= 2:
                    pe.wait_ge(s("qa_lo"), c - 1)
                product_w(pe, bank(4 + c % 2), stacked(W_AQ, P), xa[:, cols], s("a_q"))
                if c >= 2:
                    pe.wait_ge(s("ka_lo"), c - 1)
                product_w(pe, bank(6 + c % 2), stacked(W_AK, P), xa[:, cols], s("a_k"))
            for t in range(B * JI):
                product(pe, bank(t // JI, (t % JI) * D, (t % JI + 1) * D), xa[:, t * P:(t + 1) * P],
                        *stacked(W_AV, D), s("a_v"))
            def a_scores(m):
                if m >= ASTEPS:
                    return
                j, b = m // B, m % B
                if m == 0:
                    pe.wait_ge(s("va"), 2)
                if m < 2:
                    pe.wait_ge(s("qa_lo"), 2 * (b + 1))
                    pe.wait_ge(s("ka_lo"), 2 * (b + 1))
                if m >= 3:
                    pe.wait_ge(s("pa"), m - 2)
                st = ka[:, b * T_IMG + j * P:b * T_IMG + (j + 1) * P]
                for c in range(2):
                    q = slice(b * T_IMG + c * BANK, b * T_IMG + (c + 1) * BANK)
                    product(pe, bank(as_bank[m % 3] + c), st, qa_hi[:, q], qa_lo[:, q], s("a_s") if c == 1 else None)

            for m in range(3):
                a_scores(m)
            for j in range(JI):
                a_scores(B * j + 3)
                if j == JI - 1:
                    pe.wait_ge(s("powers"), 4)
                    pe.wait_ge(s("pa"), ASTEPS - 2)
                    for b in range(B):
                        m = pe.transpose(ps[0:TURNS * DEGS, 2 * BANK + b * P:2 * BANK + (b + 1) * P],
                                         powers[:, b, :, :].rearrange("p t k -> p (t k)"), ident)
                    m.then_inc(s("b_tr"), 1)
                pe.wait_ge(s("pa"), B * (j + 1))
                for c in range(2):
                    for b in range(B):
                        m = pe.matmul(ps[b * D:(b + 1) * D, (4 + c) * BANK:(5 + c) * BANK],
                                      va[:, (b * JI + j) * D:(b * JI + j + 1) * D],
                                      pa[(B * j + b) % 4][:, c * BANK:(c + 1) * BANK], start=(j == 0), stop=(j == JI - 1),
                                      skip_group_check=True)
                m.then_inc(s("a_pv"), 1)
                a_scores(B * j + 4)
            pe.wait_ge(s("powers_t"), 1)
            pe.wait_ge(s("small_in"), 48)
            for b in range(B):
                m = pe.matmul(bank(3, b * D, (b + 1) * D), powers_t[:, b, :], poly[:, :], start=True, stop=True)
            m.then_inc(s("b_emb"), 1)
            pe.wait_ge(s("d_onehot"), 1)
            for l in range(LAYERS):
                m = pe.matmul(bank(2, l * GROUPS, (l + 1) * GROUPS), br[:, l * HID:(l + 1) * HID], onehot[:, :],
                              start=True, stop=True)
            m.then_inc(s("d_bp"), 1)
            pe.wait_ge(s("ret"), 2)
            for j in range(JI):
                m = pe.matmul(bank(j // 4, (j % 4) * P, (j % 4 + 1) * P), ret[:, j * P:(j + 1) * P],
                              plain[:, K_WOA:K_WOA + P], start=True, stop=True)
            m.then_inc(s("a_y"), 1)
            for b in range(B):
                transposes_pe(pe, "c", b)
            pe.wait_ge(s("w_rest_lo"), 1)
            pe.wait_ge(s("d_bias"), LAYERS)
            for n, (b, u) in enumerate(CU):
                if u == 0:
                    pe.wait_ge(s("c_xt"), NX[b])
                if n >= 6:
                    pe.wait_ge(s("c_proj_read"), n - 5)
                if u < 6:
                    x = x_hl[:, b * S + u % 3 * CH:b * S + (u % 3 + 1) * CH]
                    product_w(pe, bank(n % 6, 0, CH), stacked(W_CQ if u < 3 else W_CK, P), x, s("c_proj"))
                else:
                    tiles = range(8) if u == 6 else [8]
                    for t in tiles:
                        product(pe, bank(n % 6, (t % 8) * D, (t % 8 + 1) * D), x_hl[:, (b * J + t) * P:(b * J + t + 1) * P],
                                *stacked(W_CV, D), s("c_proj") if t == tiles[-1] else None)

            def c_pv(n):
                b, j = CSTEP[n]
                pe.wait_ge(s("c_vs"), n + 1)
                if j == 0:
                    if b == 0:
                        pe.wait_ge(s("c_xt"), NX[1])
                    else:
                        pe.wait_ge(s("h2"), 1)
                tiles = range(J if j == 0 else j + 1)
                for i in tiles:
                    m = pe.matmul(ps[:, 6 * BANK + i * D:6 * BANK + (i + 1) * D], pc[n % 3][:, i * P:(i + 1) * P], vs[n % 3],
                                  start=(j == 0 and i % 8 == 0), stop=(j == J - 1), skip_group_check=True)
                m.then_inc(s("c_pv"), 1)

            def c_scores(n):
                b, j = CSTEP[n]
                if n == 0:
                    pe.wait_ge(s("c_proj_read"), 16)
                if n >= 2:
                    pe.wait_ge(s("c_exp"), n - 1)
                w = c_width(j)
                o = n % 2 * 3 * BANK
                for c0 in range(0, w, BANK):
                    c1 = min(c0 + BANK, w)
                    product(pe, ps[:, o + c0:o + c1], kc[b][:, j * P:(j + 1) * P],
                            qc_hi[b][:, c0:c1], qc_lo[b][:, c0:c1], s("c_s") if c1 == w else None)

            c_scores(0)
            c_scores(1)
            for n in range(len(CSTEP)):
                if n + 2 < len(CSTEP):
                    c_scores(n + 2)
                c_pv(n)
            def d_input(b):
                transposes_pe(pe, "d", b)
                for n in range(b * NCH, (b + 1) * NCH):
                    pe.wait_ge(s("d_xt"), NX[b])
                    if n == B * NCH - 1:
                        pe.wait_ge(s("d_h0"), n - 1)
                    product_w(pe, bank(D_IN_BANK[n], 0, CH), stacked(W_DI, HID), x_hl[:, n * CH:(n + 1) * CH], s("d_in"))

            def d_chunk(n):
                l, c = n // NDC, n % NDC
                if l == 0:
                    pe.wait_ge(s("d_h0"), NCH if c < DBC else B * NCH)
                else:
                    pe.wait_ge(s("d_h1"), c + 1)
                if n >= 3:
                    pe.wait_ge(s("d_z"), n - 2)
                o = c * DW
                pe.matmul(bank(n % 3 * 2 + 1, 0, DW), plain[:, K_WS + l * HID:K_WS + (l + 1) * HID], hid[l][:, o:o + DW],
                          start=True, stop=True)
                for g in range(DG):
                    m = pe.matmul(bank(n % 3 * 2, g * GT, (g + 3) * GT).rearrange("p (r t) -> p r t", r=3), wr[:, c * DG + g, l, :],
                                  hid[l][:, o + g * GT:o + (g + 1) * GT].unsqueeze(1).broadcast_to([P, 3, GT]),
                                  start=True, stop=True)
                m.then_inc(s("d_f"), 1)

            def d_output(b):
                pe.wait_ge(s("d_h2"), DBC * (b + 1))
                if b == 1:
                    pe.wait_ge(s("d_z"), LAYERS * NDC)
                for j in range(J):
                    o = D_OUT_BANK[b] * BANK + j * D
                    m = pe.matmul(ps[:, o:o + D], hid[2][:, (b * J + j) * P:(b * J + j + 1) * P], plain[:, K_WOD:K_WOD + D],
                                  start=True, stop=True)
                m.then_inc(s("d_o"), 1)

            pe.wait_ge(s("h2"), 2)
            d_input(0)
            for n in range(4):
                pe.wait_ge(s(f"wr_in{n}"), 16 * GROUPS // 4)
            for n in range(LAYERS * NDC):
                if n == DBC:
                    d_input(1)
                d_chunk(n)
                if n == NDC + DBC:
                    d_output(0)
            d_output(1)
            def unit(parity, u, b_x, dst):
                c = u % NCH
                product_w(pe, dst, stacked(u // NCH * P, P), x_hl[:, b_x * S + c * CH:b_x * S + (c + 1) * CH], s("e_proj"))

            def scores(step):
                b, k = step // STEPS % B, step % STEPS
                j, c = k // NCH, k % NCH
                for hd in range(2):
                    product(pe, bank(3 + 2 * (step % 2) + hd, 0, CH), k_e[b][:, hd, j * P:(j + 1) * P],
                            q_hi[b][:, hd, c * CH:(c + 1) * CH], q_lo[b][:, hd, c * CH:(c + 1) * CH],
                            s("e_qk") if hd == 1 else None)

            for b in range(B):
                transposes_pe(pe, "e", b)
            pe.sem_inc(s("e_pv"), PV0)
            pe.wait_ge(s("e_xt"), NX[1])
            pe.wait_ge(s("e_w"), 1)
            for t in range(NT):
                if t < UNITS:
                    if t >= 4:
                        pe.wait_ge(s("e_proj_read"), t - 3)
                    unit(0, t, 0, bank(4 + t % 4, 0, CH))
                if t >= 4:
                    pe.wait_ge(s("e_v_read"), t - 3)
                product(pe, bank(t % 4), x_hl[:, t * P:(t + 1) * P], *stacked(W_EV, HEADS * D), s("e_v"))
            pe.wait_ge(s("e_v_read"), NT)
            pe.wait_ge(s("e_proj_read"), UNITS)
            scores(0)
            scores(1)

            def pair_steps(it, last):
                for n in range(B * STEPS):
                    b, k = n // STEPS, n % STEPS
                    j, c = k // NCH, k % NCH
                    if k == 0:
                        pe.wait_ge(s("e_vcur"), it * B + (b + 1))
                    if j == 0:
                        pe.wait_ge(s("e_acc_read"), it * (B * NCH) + (b * NCH + c + 1))
                    pe.wait_ge(s("e_sig"), it * (B * STEPS) + (n + 1))
                    for hd in range(2):
                        m = pe.matmul(ps[hd * D:(hd + 1) * D, c * BANK:c * BANK + CH], v_cur[b][:, j, hd * D:(hd + 1) * D],
                                      pe_ring[:, n % 3, hd, :], start=(j == 0), stop=(j == J - 1), skip_group_check=True)
                    m.then_inc(s("e_pv"), 1)
                    if not (last and n + 2 >= B * STEPS):
                        if (n + 2) % STEPS == 0:
                            pe.wait_ge(s("e_proj_read"), it * (B * UNITS) + ((n + 2) // STEPS + 1) * UNITS)
                        scores((n + 2) % (B * STEPS))
                    if k >= 2 and k % 2 == 0 and (k - 2) // 2 < UNITS and not (last and b == B - 1):
                        u = (k - 2) // 2
                        if u == 0 and b == B - 1:
                            pe.wait_ge(s("e_w"), it + 2)
                        pe.wait_ge(s("e_proj_read"), it * (B * UNITS) + ((b + 1) * UNITS + u))
                        unit(1 - b, u, 1 - b, bank(7, 0, CH))

            with pe.Fori(0, PAIRS - 1) as it:
                pair_steps(it, False)
            pair_steps(PAIRS - 1, True)
            pe.wait_ge(s("e_acc_read"), PAIRS * B * NCH + AF0)
            pe.wait_ge(s("late_in"), 16)
            for b in range(B):
                for j in range(J):
                    for hp in range(PAIRS):
                        o = (3 + 2 * b) * BANK + j * D
                        m = pe.matmul(ps[:, o:o + D], wv[:, hp, b, j * P:(j + 1) * P], wo_e[:, hp * D:(hp + 1) * D],
                                      start=(hp == 0), stop=(hp == PAIRS - 1))
                m.then_inc(s("e_o"), 1)
            for b in range(B):
                transposes_pe(pe, "f", b)
            for b in range(B):
                pe.wait_ge(s("f_xt"), NX[b])
                for t in range(b * J, (b + 1) * J):
                    product(pe, bank(0, t * ME, (t + 1) * ME), x_hl[:, t * P:(t + 1) * P], *stacked(W_FR, ME),
                            s("f_r") if t == NT - 1 else None)
            for n, (ch, u) in enumerate(FUNITS):
                if n >= 4:
                    pe.wait_ge(s("f_gelu"), n - 3)
                product_w(pe, bank(1 + n % 4, 0, CH), stacked(W_F1 + u * P, P), x_hl[:, ch * CH:(ch + 1) * CH], s("f_1"))
            for n, (b, j0, k) in enumerate(TG):
                pe.wait_ge(s("f_cc"), 1)
                if n >= 2:
                    pe.wait_ge(s("f_ct"), n - 1)
                for i in range(k):
                    m = pe.transpose(bank(6 + n % 2, i * P, (i + 1) * P), cc[:, b * J + j0 + i, :].bitcast(F32), ident)
                m.then_inc(s("f_ctr"), 1)
            pe.wait_ge(s("f_ct"), len(TG))
            pe.wait_ge(s("f_sel"), 1)
            pe.wait_ge(s("f_gelu"), len(FUNITS))

            def second_layer(ch):
                pe.wait_ge(s("f_hc"), 4 * (ch + 1))
                for t in range(3 * ch, 3 * ch + 3):
                    o = (4 + 2 * (t // J)) * BANK + t % J * D
                    for u in range(ME // 2):
                        pe.matmul(ps[:, o:o + D], act_f[:, u, t * P:(t + 1) * P], w2_f[:, u * D:(u + 1) * D],
                                  start=(u == 0), stop=False)
                    pe.matmul(ps[:, o:o + D], c_hl[:, t * P:(t + 1) * P], w_hi[:, W_FB2:W_FB2 + D], start=False, stop=False)
                    m = pe.matmul(ps[:, o:o + D], c_hl[:, t * P:(t + 1) * P], w_lo[:, W_FB2:W_FB2 + D], start=False, stop=True)
                    if t % J == J - 1:
                        m.then_inc(s("f_y"), 1)

            for n, (ch, u) in enumerate(FUNITS):
                if n >= 4:
                    pe.wait_ge(s("f_hc"), n - 3)
                pe.matmul(bank(n % 4, 0, CH), sel[:, u * P:(u + 1) * P], c_hl[:, ch * CH:(ch + 1) * CH],
                          start=True, stop=True).then_inc(s("f_cb"), 1)
                if u == ME // 2 - 1 and ch >= 1:
                    second_layer(ch - 1)
            second_layer(B * NCH - 1)

        @block.vector
        def _(dve):
            dve.wait_ge(s("w_first_in"), 16)
            dve.tensor_copy(w_hi[:, 0:W_CQ], raw2[:, 0:W_CQ]).then_inc(s("w_first_hi"), 1)
            dve.wait_ge(s("w_first_hi"), 1)
            dve.tensor_tensor(w_lo[:, 0:W_CQ], raw2[:, 0:W_CQ], w_hi[:, 0:W_CQ].bitcast(F32),
                              ALU.subtract).then_inc(s("w_first_lo"), 1)
            dve.wait_ge(s("x_in"), 16)
            for c in range(4):
                cols = slice(c * BANK, (c + 1) * BANK)
                dve.tensor_copy(xa[:, cols], raw1[:, cols]).then_inc(s("xa_hi"), 1)
                dve.wait_ge(s("xa_hi"), c + 1)
                dve.tensor_tensor(xa[D:P, cols], raw1[D:P, cols], xa[D:P, cols].bitcast(F32),
                                  ALU.subtract).then_inc(s("xa_lo"), 1)
            dve.wait_ge(s("plain_in"), 16)
            for c in range(4):
                cols = slice(c * BANK, (c + 1) * BANK)
                dve.wait_ge(s("qa_hi"), c + 1)
                dve.scalar_tensor_tensor(out=qa_lo[:, cols], in0=bank(4 + c % 2), scalar=plain[:, C_BQ:C_BQ + 1],
                                         in1=qa_hi[:, cols].bitcast(F32), op0=ALU.add, op1=ALU.subtract).then_inc(s("qa_lo"), 1)
                dve.wait_ge(s("ka_hi"), c + 1)
                dve.scalar_tensor_tensor(out=ka[D:P, cols], in0=bank(6 + c % 2)[D:P, :], scalar=plain[D:P, C_BK:C_BK + 1],
                                         in1=ka[D:P, cols].bitcast(F32), op0=ALU.add, op1=ALU.subtract).then_inc(s("ka_lo"), 1)
            for b in range(B):
                dve.wait_ge(s("a_v"), JI * (b + 1))
                dve.tensor_tensor(va[:, b * JI * D:(b + 1) * JI * D].rearrange("p (j d) -> p j d", d=D),
                                  bank(b).rearrange("p (j d) -> p j d", d=D),
                                  plain[:, K_BVA:K_BVA + D].unsqueeze(1).broadcast_to([P, JI, D]), ALU.add).then_inc(s("va"), 1)
            def gated(j):
                dve.wait_ge(s(f"gamma_in{j}"), 16)
                for m in range(B * j, B * (j + 1)):
                    if j >= 2:
                        dve.wait_ge(s("a_pv"), j - 1)
                    dve.wait_ge(s("a_s"), m + 1)
                    o = as_bank[m % 3] * BANK
                    dve.tensor_tensor(pa[m % 4], ps[:, o:o + T_IMG], gamma[:, j, :], ALU.mult).then_inc(s("pa"), 1)

            for j in range(3):
                gated(j)
            flat = [tok4[:, n, :] for n in range(8)]
            dve.wait_ge(s("turns_in"), 32)
            dve.scalar_tensor_tensor(out=flat[1], in0=flat[0], scalar=-1.0, in1=flat[0], op0=ALU.mult, op1=ALU.max)\
               .then_inc(s("b_abs"), 1)
            dve.wait_ge(s("b_abs"), 1)
            dve.tensor_copy(tok4i[:, :], flat[1]).then_inc(s("b_int"), 1)
            dve.wait_ge(s("b_int"), 1)
            dve.tensor_copy(flat[2], tok4i[:, :]).then_inc(s("b_round"), 1)
            dve.wait_ge(s("b_round"), 1)
            dve.tensor_tensor(flat[3], flat[2], flat[1], ALU.is_gt).then_inc(s("b_over"), 1)
            dve.wait_ge(s("b_over"), 1)
            dve.tensor_tensor(flat[4], flat[2], flat[3], ALU.subtract).then_inc(s("b_floor"), 1)
            dve.tensor_scalar(flat[5], flat[0], 0.0, 2.0, ALU.is_ge, ALU.mult).then_inc(s("b_sign"), 1)
            dve.wait_ge(s("b_floor"), 1)
            dve.wait_ge(s("b_sign"), 1)
            dve.scalar_tensor_tensor(out=flat[6], in0=flat[5], scalar=-1.0, in1=flat[4], op0=ALU.add, op1=ALU.mult)\
               .then_inc(s("b_trunc"), 1)
            pw = [powers[:, :, :, k].rearrange("p b t -> p (b t)") for k in range(DEGS)]
            dve.memset(pw[0], 1.0).then_inc(s("b_one"), 1)
            dve.wait_ge(s("b_trunc"), 1)
            dve.tensor_copy(pw[1], flat[6]).then_inc(s("powers"), 1)
            dve.tensor_tensor(pw[2], flat[6], flat[6], ALU.mult).then_inc(s("powers"), 1)
            dve.wait_ge(s("powers"), 2)
            dve.tensor_tensor(pw[3], pw[2], flat[6], ALU.mult).then_inc(s("powers"), 1)
            dve.tensor_tensor(pw[4], pw[2], pw[2], ALU.mult).then_inc(s("powers"), 1)
            dve.wait_ge(s("small_in"), 48)
            dve.tensor_scalar(onehot[:, :], route_all[:, :], plain[0:EXPERTS, C_EIDX:C_EIDX + 1], None, ALU.is_equal)\
               .then_inc(s("d_onehot"), 1)
            gated(3)
            dve.wait_ge(s("w_rest_in"), 16)
            dve.tensor_copy(w_hi[:, W_CQ:NW], raw2[:, W_CQ:NW]).then_inc(s("w_rest_hi"), 1)
            gated(4)
            dve.wait_ge(s("w_rest_hi"), 1)
            dve.tensor_tensor(w_lo[:, W_CQ:NW], raw2[:, W_CQ:NW], w_hi[:, W_CQ:NW].bitcast(F32),
                              ALU.subtract).then_inc(s("w_rest_lo"), 1)
            for j in range(5, JI):
                gated(j)
            dve.wait_ge(s("a_pv"), JI)
            dve.tensor_copy(ret[:, 0:BANK], bank(4)).then_inc(s("ret"), 1)
            dve.wait_ge(s("a_y"), 1)
            y = tmp[:, 0:2 * BANK]
            neg = tmp[:, 2 * BANK:4 * BANK]
            dve.tensor_tensor(y.rearrange("p (c d) -> p c d", d=D), ps[:, 0:2 * BANK].rearrange("p (c d) -> p c d", d=D),
                              plain[:, K_BOA:K_BOA + D].unsqueeze(1).broadcast_to([P, B * JI, D]), ALU.add).then_inc(s("a_yb"), 1)
            dve.wait_ge(s("a_yb"), 1)
            dve.tensor_scalar(neg, y, 0.0, plain[:, C_SLOPE:C_SLOPE + 1], ALU.min, ALU.mult).then_inc(s("a_neg"), 1)
            dve.wait_ge(s("a_neg"), 1)
            dve.wait_ge(s("w_rest_lo"), 1)
            dve.wait_ge(s("b_emb"), 1)
            for b in range(B):
                dve.tensor_copy(h[:, b * J + JI, :], bank(3, b * D, (b + 1) * D)).then_inc(s("h1t"), 1)
            for b in range(B):
                view = [v.rearrange("p (j b d) -> p b j d", b=B, d=D)[:, b, :, :] for v in (y, neg)]
                dve.scalar_tensor_tensor(out=h[:, b * J:b * J + JI, :], in0=view[0], scalar=0.0, in1=view[1],
                                         op0=ALU.max, op1=ALU.add).then_inc(s("h1"), 1)
            first, second = norm_dve(dve, "c")
            dve.wait_ge(s("h1t"), 2)
            dve.wait_ge(s("h1"), 2)
            first(0)
            first(1)
            second(0)
            second(1)
            dve.wait_ge(s("d_bp"), 1)
            for l in range(LAYERS):
                dve.tensor_scalar(bias_g[:, l, :], bank(2, l * GROUPS, (l + 1) * GROUPS), plain[:, C_BS + l:C_BS + l + 1], None,
                                  ALU.add).then_inc(s("d_bias"), 1)
            for n, (b, u) in enumerate(CU):
                if u < 3:
                    cols = slice(u * CH, (u + 1) * CH)
                    dve.wait_ge(s("c_hi"), 6 * b + u + 1)
                    dve.tensor_tensor(qc_lo[b][:, cols], bank(n % 6, 0, CH), qc_hi[b][:, cols].bitcast(F32),
                                      ALU.subtract).then_inc(s("c_proj_read"), 1)
                elif u < 6:
                    cols = slice((u - 3) * CH, (u - 2) * CH)
                    dve.wait_ge(s("c_hi"), 6 * b + u + 1)
                    dve.tensor_tensor(kc[b][D:P, cols], bank(n % 6, 0, CH)[D:P, :], kc[b][D:P, cols].bitcast(F32),
                                      ALU.subtract).then_inc(s("c_proj_read"), 1)
                else:
                    dve.wait_ge(s("c_proj"), n + 1)
                    t0, t1 = (0, 8) if u == 6 else (8, 9)
                    dve.tensor_copy(vc[:, (b * J + t0) * D:(b * J + t1) * D], bank(n % 6, 0, (t1 - t0) * D))\
                       .then_inc(s("c_proj_read"), 1)

            d_first, d_second = norm_dve(dve, "d")

            def c_scale_v(n):
                b, j = CSTEP[n]
                den, inv = small[:, 4 + n % 2:5 + n % 2], small[:, 6 + n % 2:7 + n % 2]
                dve.wait_ge(s("c_exp"), n + 1)
                dve.reciprocal(inv, den).then_inc(s("c_inv"), 1)
                dve.wait_ge(s("c_inv"), n + 1)
                if n >= 3:
                    dve.wait_ge(s("c_pv"), n - 2)
                dve.tensor_scalar(vs[n % 3], vc[:, (b * J + j) * D:(b * J + j + 1) * D], inv, None, ALU.mult)\
                   .then_inc(s("c_vs"), 1)

            def c_add(b):
                t = slice(b * J, (b + 1) * J)
                dve.wait_ge(s("c_pv"), J * (b + 1))
                dve.tensor_tensor(h[:, t, :], ps[:, 6 * BANK:6 * BANK + J * D].rearrange("p (j d) -> p j d", d=D),
                                  h[:, t, :], ALU.add).then_inc(s("h2"), 1)

            for n, (b, j) in enumerate(CSTEP):
                o, w = (n % 2) * 3 * BANK, c_width(j)
                dve.wait_ge(s("c_s"), n + 1)
                diag = ps[:, o + j * P:o + (j + 1) * P]
                dve.tensor_tensor(diag, diag, plain[:, K_MASK:K_MASK + P], ALU.add).then_inc(s("c_mask"), 1)
                if j == 0:
                    rest = ps[:, o + P:o + S]
                    dve.tensor_scalar(rest, rest, MASKED, None, ALU.add).then_inc(s("c_mask0"), 1)
                    dve.wait_ge(s("c_mask0"), b + 1)
                dve.wait_ge(s("c_mask"), n + 1)
                dve.reduce_max(small[:, n % 2:n % 2 + 1], ps[:, o:o + w], AX_X, negate=True).then_inc(s("c_max"), 1)
                dve.wait_ge(s("c_max"), n + 1)
                dve.tensor_scalar(small[:, 2 + n % 2:3 + n % 2], small[:, n % 2:n % 2 + 1], D ** -0.5, None,
                                  ALU.mult).then_inc(s("c_bias"), 1)
                if n >= 1:
                    c_scale_v(n - 1)
                if n == J:
                    c_add(0)
                if n == J + 2:
                    dve.wait_ge(s("h2"), 1)
                    d_first(0)
                if n == J + 5:
                    d_second(0)
            c_scale_v(len(CSTEP) - 1)
            c_add(1)
            e_first, e_second = norm_dve(dve, "e")

            def d_sum(n):
                cols = slice(n % NDC * DW, (n % NDC + 1) * DW)
                dve.wait_ge(s("d_res"), n + 1)
                dve.wait_ge(s("d_f"), n + 1)
                dve.tensor_tensor(res[:, cols], bank(n % 3 * 2 + 1, 0, DW), res[:, cols], ALU.add).then_inc(s("d_zs"), 1)
                dve.wait_ge(s("d_zs"), n + 1)
                dve.tensor_tensor(res[:, cols], bank(n % 3 * 2, 0, DW), res[:, cols], ALU.add).then_inc(s("d_z"), 1)

            def d_add(b):
                t, o = slice(b * J, (b + 1) * J), D_OUT_BANK[b] * BANK
                dve.wait_ge(s("d_hb"), b + 1)
                dve.wait_ge(s("d_o"), b + 1)
                dve.tensor_tensor(h[:, t, :], ps[:, o:o + J * D].rearrange("p (j d) -> p j d", d=D), h[:, t, :],
                                  ALU.add).then_inc(s("h3"), 1)

            dve.wait_ge(s("h2"), 2)
            d_first(1)
            d_sum(0)
            d_sum(1)
            d_second(1)
            for n in range(2, NDC + DBC + 1):
                d_sum(n)
            d_add(0)
            dve.wait_ge(s("h3"), 1)
            e_first(0)
            d_sum(NDC + DBC + 1)
            d_sum(NDC + DBC + 2)
            e_second(0)
            d_sum(NDC + DBC + 3)
            d_add(1)
            dve.sem_inc(s("e_acc_read"), AF0)

            def weights_of(hp):
                src = raw1[:, bass.ds(hp * 4 * P, 4 * P)]
                dve.tensor_copy(w_hi[:, 0:4 * P], src).then_inc(s("e_whi"), 1)
                dve.wait_ge(s("e_whi"), hp + 1)
                dve.tensor_tensor(w_lo[:, 0:4 * P], src, w_hi[:, 0:4 * P].bitcast(F32), ALU.subtract).then_inc(s("e_w"), 1)

            def split_unit(n, u, b, src):
                hd, cols = u // NCH % 2, slice(u % NCH * CH, (u % NCH + 1) * CH)
                dve.wait_ge(s("e_proj"), n + 1)
                hi = (q_hi if u < 2 * NCH else k_e)[b][:, hd, cols]
                dve.tensor_copy(hi, src).then_inc(s("e_hi"), 1)
                dve.wait_ge(s("e_hi"), n + 1)
                if u < 2 * NCH:
                    dve.tensor_tensor(q_lo[b][:, hd, cols], src, hi.bitcast(F32), ALU.subtract).then_inc(s("e_proj_read"), 1)
                else:
                    lo = k_e[b][D:P, hd, cols]
                    dve.tensor_tensor(lo, src[D:P, :], lo.bitcast(F32), ALU.subtract).then_inc(s("e_proj_read"), 1)

            dve.wait_ge(s("qk_in"), 16)
            weights_of(0)
            dve.wait_ge(s("h3"), 2)
            e_first(1)
            e_second(1)
            for u in range(UNITS):
                split_unit(u, u, 0, bank(4 + u % 4, 0, CH))

            def pair_work(it, last):
                for b in range(B):
                    if not (last and b == B - 1):
                        for u in range(UNITS):
                            split_unit(it * (B * UNITS) + ((b + 1) * UNITS + u), u, 1 - b, bank(7, 0, CH))
                    if b == 0 and not last:
                        weights_of(it + 1)
                    for c in range(NCH):
                        dve.wait_ge(s("e_pv"), it * (B * STEPS) + (b * STEPS + STEPS - NCH + c + 1 + PV0))
                        dve.tensor_copy(wv[:, bass.ds(it, 1), b, c * CH:(c + 1) * CH].rearrange("p a t -> p (a t)"),
                                        bank(c, 0, CH)).then_inc(s("e_acc_read"), 1)

            with dve.Fori(0, PAIRS - 1) as it:
                pair_work(it, False)
            pair_work(PAIRS - 1, True)
            for b in range(B):
                t = slice(b * J, (b + 1) * J)
                dve.wait_ge(s("e_o"), b + 1)
                o = (3 + 2 * b) * BANK
                dve.scalar_tensor_tensor(out=h[:, t, :], in0=ps[:, o:o + J * D].rearrange("p (j d) -> p j d", d=D), scalar=0.0,
                                         in1=h[:, t, :], op0=ALU.max, op1=ALU.add).then_inc(s("h4"), 1)
            first, second = norm_dve(dve, "f")
            dve.wait_ge(s("h4"), 2)
            first(0)
            first(1)
            second(0)
            second(1)
            dve.wait_ge(s("sel_in"), 16)
            dve.tensor_copy(sel, sel_in).then_inc(s("f_sel"), 1)
            step = [0]

            def chain(ins):
                step[0] += 1
                ins.then_inc(s("f_gate"), 1)
                dve.wait_ge(s("f_gate"), step[0])

            def bc(v):
                return v.unsqueeze(2).broadcast_to([P, NT, ME])

            rev = plain[:, K_REV:K_REV + ME].unsqueeze(1).broadcast_to([P, NT, ME])
            shifted, expd, prob, eq, ranked, sel1, rest = gate
            top, total, inv, p1, r1, p2, r2, winv = per_tok
            logits = bank(0, 0, NT * ME).rearrange("p (t e) -> p t e", e=ME)
            dve.wait_ge(s("f_r"), 1)
            chain(dve.reduce_max(top, logits, AX_X))
            dve.tensor_tensor(shifted, logits, bc(top), ALU.subtract).then_inc(s("f_shift"), 1)
            dve.wait_ge(s("f_exp"), 1)
            chain(dve.reduce_sum(total, expd, AX_X))
            chain(dve.reciprocal(inv, total))
            chain(dve.tensor_tensor(prob, expd, bc(inv), ALU.mult))
            chain(dve.reduce_max(p1, prob, AX_X))
            chain(dve.tensor_tensor(eq, prob, bc(p1), ALU.is_equal))
            chain(dve.tensor_tensor(ranked, eq, rev, ALU.mult))
            chain(dve.reduce_max(r1, ranked, AX_X))
            chain(dve.tensor_tensor(sel1, ranked, bc(r1), ALU.is_equal))
            chain(dve.scalar_tensor_tensor(out=rest, in0=sel1, scalar=-2.0, in1=prob, op0=ALU.mult, op1=ALU.add))
            chain(dve.reduce_max(p2, rest, AX_X))
            chain(dve.tensor_tensor(eq, rest, bc(p2), ALU.is_equal))
            chain(dve.tensor_tensor(ranked, eq, rev, ALU.mult))
            chain(dve.reduce_max(r2, ranked, AX_X))
            chain(dve.tensor_tensor(eq, ranked, bc(r2), ALU.is_equal))
            chain(dve.tensor_tensor(eq, eq, sel1, ALU.add))
            chain(dve.tensor_tensor(winv, p1, p2, ALU.add))
            chain(dve.tensor_scalar(winv, winv, 1e-12, None, ALU.max))
            chain(dve.reciprocal(winv, winv))
            chain(dve.tensor_tensor(prob, prob, eq, ALU.mult))
            chain(dve.tensor_tensor(prob, prob, bc(winv), ALU.mult))
            dve.wait_ge(s("f_zero"), 1)
            chain(dve.tensor_copy(cc[:, :, 0:ME], prob))
            dve.tensor_tensor(cc[:, :, ME:2 * ME], prob, cc[:, :, 0:ME].bitcast(F32), ALU.subtract).then_inc(s("f_cc"), 1)
            for n, (ch, u) in enumerate(FUNITS):
                cols = slice(ch * CH, (ch + 1) * CH)
                dve.wait_ge(s("f_gelu"), n + 1)
                dve.wait_ge(s("f_cb"), n + 1)
                dve.tensor_tensor(act_f[:, u, cols], act_f[:, u, cols], bank(n % 4, 0, CH), ALU.mult).then_inc(s("f_hc"), 1)
            for b in range(B):
                t = slice(b * J, (b + 1) * J)
                o = (4 + 2 * b) * BANK
                dve.wait_ge(s("f_y"), b + 1)
                dve.tensor_tensor(xc[:, t, :], xc[:, t, :], ps[:, o:o + J * D].rearrange("p (j d) -> p j d", d=D),
                                  ALU.add).then_inc(s("f_moe"), 1)
                dve.wait_ge(s("f_moe"), b + 1)
                dve.tensor_tensor(h[:, t, :], h[:, t, :], xc[:, t, :], ALU.add).then_inc(s("h5"), 1)

        @block.scalar
        def _(act):
            act.wait_ge(s("plain_in"), 16)
            for c in range(4):
                cols = slice(c * BANK, (c + 1) * BANK)
                act.wait_ge(s("a_q"), c + 1)
                act.activation(qa_hi[:, cols], bank(4 + c % 2), ACT.Identity, bias=plain[:, C_BQ:C_BQ + 1]).then_inc(s("qa_hi"), 1)
                act.wait_ge(s("a_k"), c + 1)
                act.activation(ka[:, cols], bank(6 + c % 2), ACT.Identity, bias=plain[:, C_BK:C_BK + 1]).then_inc(s("ka_hi"), 1)
            act.wait_ge(s("b_tr"), 1)
            act.copy(powers_t[:, :, :].rearrange("p b t -> p (b t)"), ps[0:TURNS * DEGS, 2 * BANK:2 * BANK + B * P])\
               .then_inc(s("powers_t"), 1)
            act.wait_ge(s("a_pv"), JI)
            act.copy(ret[:, BANK:2 * BANK], bank(5)).then_inc(s("ret"), 1)
            for b in range(B):
                transposes_act(act, "c", b)
            for n, (b, u) in enumerate(CU):
                if u < 6:
                    dst = (qc_hi if u < 3 else kc)[b][:, u % 3 * CH:(u % 3 + 1) * CH]
                    act.wait_ge(s("c_proj"), n + 1)
                    act.copy(dst, bank(n % 6, 0, CH)).then_inc(s("c_hi"), 1)
            for n, (b, j) in enumerate(CSTEP):
                o, w = (n % 2) * 3 * BANK, c_width(j)
                act.wait_ge(s("c_bias"), n + 1)
                if n >= 2:
                    act.wait_ge(s("c_inv"), n - 1)
                if n >= 3:
                    act.wait_ge(s("c_pv"), n - 2)
                act.activation(pc[n % 3][:, 0:w], ps[:, o:o + w], ACT.Exp, bias=small[:, 2 + n % 2:3 + n % 2],
                               scale=D ** -0.5, accum_out=small[:, 4 + n % 2:5 + n % 2]).then_inc(s("c_exp"), 1)
            def d_input(b):
                transposes_act(act, "d", b)
                for n in range(b * NCH, (b + 1) * NCH):
                    act.wait_ge(s("d_in"), n + 1)
                    act.activation(hid[0][:, n * CH:(n + 1) * CH], bank(D_IN_BANK[n], 0, CH), ACT.Relu, bias=plain[:, C_BI:C_BI + 1])\
                       .then_inc(s("d_h0"), 1)

            d_input(0)
            for n in range(LAYERS * NDC):
                l, c = n // NDC, n % NDC
                if n == 2:
                    d_input(1)
                cols = slice(c * DW, (c + 1) * DW)
                act.wait_ge(s("d_z"), n + 1)
                act.activation(hid[l + 1][:, cols], res[:, cols], ACT.Relu).then_inc(s(f"d_h{l + 1}"), 1)
            for b in range(B):
                transposes_act(act, "e", b)
            for t in range(NT):
                act.wait_ge(s("e_v"), t + 1)
                act.copy(v_all[:, t, :], bank(t % 4)).then_inc(s("e_v_read"), 1)
            with act.Fori(0, PAIRS) as it:
                for n in range(B * STEPS):
                    o = (3 + 2 * (n % 2)) * BANK
                    act.wait_ge(s("e_qk"), it * (B * STEPS) + (n + 1))
                    act.wait_ge(s("e_pv"), it * (B * STEPS) + (n + 1))
                    act.activation(pe_ring[:, n % 3, :, :],
                                   ps[:, o:o + 2 * BANK].rearrange("p (h t) -> p h t", h=2)[:, :, 0:CH],
                                   ACT.Sigmoid, scale=float(D) ** 0.5).then_inc(s("e_sig"), 1)
            for b in range(B):
                transposes_act(act, "f", b)
            act.wait_ge(s("f_shift"), 1)
            act.activation(gate[1], gate[0], ACT.Exp).then_inc(s("f_exp"), 1)
            for n, (ch, u) in enumerate(FUNITS):
                act.wait_ge(s("f_1"), n + 1)
                act.activation(act_f[:, u, ch * CH:(ch + 1) * CH], bank(1 + n % 4, 0, CH), ACT.Gelu,
                               bias=plain[:, C_B1 + u:C_B1 + u + 1]).then_inc(s("f_gelu"), 1)
            for n, (b, j0, k) in enumerate(TG):
                act.wait_ge(s("f_ctr"), n + 1)
                act.copy(c_hl[:, (b * J + j0) * P:(b * J + j0 + k) * P], bank(6 + n % 2, 0, k * P)).then_inc(s("f_ct"), 1)


def arrays_of(inputs):
    g = {k: np.asarray(v) for k, v in inputs.items()}
    f = np.float32

    def twice(w):
        return np.concatenate([w, w], 0)

    def dup(w):
        return np.concatenate([w, w], 1)

    def heads(w):
        return np.moveaxis(w.reshape(D, D, HEADS), 2, 0)

    xt = g["x"].reshape(B * T_IMG, D).T
    w1 = np.moveaxis(g["L1_ffn_w1"], 0, 1).reshape(D, ME * D)
    b2 = g["L1_ffn_b2"]
    w_stack = np.concatenate([
        twice(dup(g["L0_tok_Wq"])), twice(dup(g["L0_tok_Wk"])), twice(g["L0_tok_Wv"]),
        twice(dup(g["L0_attn_Wq"].T)), twice(dup(g["L0_attn_Wk"].T)), twice(g["L0_attn_Wv"].T),
        twice(g["L0_ffn_Wi"].T),
        twice(np.concatenate(list(heads(g["L1_attn_Wv"])), 1)),
        twice(g["L1_ffn_router_w"].T), twice(w1),
        np.concatenate([b2, b2, np.zeros((P - 2 * ME, D), f)], 0),
    ], 1)
    hq, hk = heads(g["L1_attn_Wq"]), heads(g["L1_attn_Wk"])
    w_qk = twice(np.concatenate([np.concatenate([dup(hq[2 * p]), dup(hq[2 * p + 1]), dup(hk[2 * p]), dup(hk[2 * p + 1])], 1)
                                 for p in range(PAIRS)], 1))
    zero = np.zeros((D, D), f)
    wo = g["L0_tok_Wo"]

    def row(v, n=P):
        return np.broadcast_to(v.reshape(1, -1), (n, v.size))

    def col(v):
        return v.reshape(P, 1)

    b1 = g["L1_ffn_b1"].reshape(ME // 2, P)
    cols = [col(np.tile(g["L0_tok_bq"], 2)), col(np.tile(g["L0_tok_bk"], 2)), col(g["L0_ffn_bi"])]
    cols += [col(g["L0_ffn_bs"][l, 0]) for l in range(LAYERS)] + [col(b1[u]) for u in range(ME // 2)]
    cols += [col(np.broadcast_to(g["L0_tok_prelu_a"].reshape(1), (P,))), col(np.arange(P, dtype=f))]
    mask = np.where(np.arange(P)[None, :] >= np.arange(P)[:, None], f(MASKED), f(0)).astype(f)
    w_plain = np.concatenate([
        np.block([[wo, zero], [zero, wo]]),
        *[g["L0_ffn_Ws"][l, 0].T for l in range(LAYERS)],
        g["L0_ffn_Wo"].T, np.eye(P, dtype=f), mask,
        row(g["L0_tok_bv"]), row(g["L0_tok_bo"]), row(g["L0_ffn_bo"]),
        row(np.arange(ME, 0, -1).astype(f)), *cols], 1)
    woe = g["L1_attn_Wo"].reshape(D, HEADS, D)
    wo_pairs = [np.concatenate([woe[:, 2 * p], woe[:, 2 * p + 1]], 0) for p in range(PAIRS)]
    w2 = g["L1_ffn_w2"].reshape(ME // 2, P, D)
    sel = np.zeros((P, ME * D), f)
    for e in range(ME):
        sel[[e, e + ME], e * D:(e + 1) * D] = 1
    w_late = np.concatenate([*wo_pairs, *w2, sel], 1)
    ins = {
        "x_stack": twice(xt), "w_stack": w_stack, "w_plain": w_plain, "w_qk": w_qk, "w_late": w_late,
        "gamma_t": g["L0_tok_d_gamma_batched"].T.reshape(JI, P, T_IMG),
        "w_br": np.moveaxis(g["L0_ffn_br"], 0, 1).reshape(EXPERTS, LAYERS * HID),
        "w_poly": g["L0_txt_poly_coeffs"].reshape(TURNS * DEGS, D),
        "ids": g["x_txt"].T, "turns": g["L0_txt_turns"],
        "route": g["L0_ffn_route_id"].reshape(1, GROUPS),
        "w_route": np.moveaxis(g["L0_ffn_Wr"], (1, 3, 0, 2), (0, 1, 2, 3)).reshape(EXPERTS, HID, LAYERS * HID),
    }
    return {k: np.ascontiguousarray(v) for k, v in ins.items()}


def kernel(**inputs):
    import concourse.bacc as bacc
    from concourse.bass_utils import run_bass_kernel_spmd

    nc = bacc.Bacc("TRN2", target_bir_lowering=False, num_devices=1)
    arrays = arrays_of(inputs)
    args = {k: nc.dram_tensor(k, a.shape, mybir.dt.from_np(a.dtype), kind="ExternalInput").ap() for k, a in arrays.items()}
    out = nc.dram_tensor("out", (B, S, D), F32, kind="ExternalOutput").ap()
    program(nc, **args, out=out)
    result = run_bass_kernel_spmd(nc, [arrays], core_ids=[0])
    return result.results[0]["out"]
```

```python
from contextlib import ExitStack

import numpy as np

import concourse.bass as bass
from concourse import mybir

ALU = mybir.AluOpType
ACT = mybir.ActivationFunctionType
F32 = mybir.dt.float32
F32R = mybir.dt.float32r
I32 = mybir.dt.int32
AX_X = mybir.AxisListType.X

P = 128
B = 2
D = 64
T_IMG = 1024
JI = T_IMG // P
T_TXT = 128
J = JI + 1
S = J * P
NT = B * J
TOK = B * S
TURNS, DEGS = 4, 5
HID = 128
LAYERS, EXPERTS = 2, 16
GROUPS = 64
GT = TOK // GROUPS
HEADS = 8
PAIRS = HEADS // 2
ME = 8
EARLY = 40
WG = LAYERS * HID
EPS = 1e-5
MASKED = -1e10
CH = 384
NCH = S // CH
BANK = 512

W_AQ, W_AK, W_AV = 0, 128, 256
W_CV = 320
W_DI = 384
W_FR = 512
W_F1 = W_FR + ME
W_FB2 = W_F1 + ME * D
NW = W_FB2 + D
W_CM = NW
W_EM = W_CM + P
W_EV = W_EM + HEADS * P
NWM = W_EV + HEADS * D
W_CUR = 0
M_CQ, M_CK = 0, P
M_EQ = 2 * P
M_EK = M_EQ + HEADS * P
M_EV = M_EK + HEADS * P
M_EO = M_EV + HEADS * P
NM = M_EO + HEADS * D
K_WOA = 0
K_WS = 128
K_WOD = K_WS + LAYERS * HID
K_ID = K_WOD + D
K_MASK = K_ID + P
K_ID2 = K_MASK + P
K_BVA, K_BOA, K_BOD = K_ID2 + D, K_ID2 + 2 * D, K_ID2 + 3 * D
K_REV = K_BOD + D
K_COL = K_REV + ME
NK = K_COL + 11
C_BQ, C_BK, C_BI, C_BS, C_B1, C_SLOPE, C_EIDX = (K_COL + n for n in (0, 1, 2, 3, 5, 9, 10))


def program(nc, x_stack, w_stack, w_plain, w_factors, w_late, gamma_t, w_br, w_poly, ids, turns, route, w_route, out):
    with ExitStack() as ctx:
        def sb(name, shape, dt=F32):
            return ctx.enter_context(nc.sbuf_tensor(name, shape, dt))

        sems = {}

        def s(name):
            if name not in sems:
                sems[name] = ctx.enter_context(nc.semaphore(name))
            return sems[name]

        raw1 = sb("raw1", [P, 2048])
        raw2 = sb("raw2", [P, NT * D + PAIRS * D + LAYERS * GROUPS])
        w_hi = sb("w_hi", [P, NWM], F32R)
        w_lo = sb("w_lo", [P, NWM], F32R)
        plain = sb("plain", [P, NK])
        halves = sb("halves", [P, TOK + 2 * 5 * S], F32R)
        big = sb("big", [P, GROUPS * LAYERS * HID])
        mid = sb("mid", [P, 4 * TOK])
        tmp = sb("tmp", [P, B * J * P])
        br = sb("br", [EXPERTS, LAYERS * HID])
        idx = sb("idx", [P, B], I32)
        route_row = sb("route_row", [1, GROUPS], I32)
        route_all = sb("route_all", [EXPERTS, GROUPS], I32)
        onehot = sb("onehot", [EXPERTS, GROUPS])
        stat = sb("stat", [P, 4, NT])
        tok4i = sb("tok4i", [P, B * TURNS], I32)
        small = sb("small", [P, 16])
        ident_r = sb("ident_r", [P, P], F32R)
        mask_hl = sb("mask_hl", [P, 2 * P], F32R)
        w_router = sb("w_router", [P, 2 * ME], F32R)
        w_b2 = sb("w_b2", [P, 2 * D], F32R)
        ps = ctx.enter_context(nc.psum_tensor("ps", [P, 8 * BANK], F32))

        def bank(n, lo=0, hi=BANK):
            return ps[:, n * BANK + lo:n * BANK + hi]

        h = raw2[:, 0:NT * D].rearrange("p (t d) -> p t d", d=D)
        w2_f = raw2[:, NT * D:NT * D + PAIRS * D]
        bias_g = raw2[:, NT * D + PAIRS * D:NT * D + PAIRS * D + LAYERS * GROUPS].rearrange("p (l g) -> p l g", l=LAYERS)
        ident = plain[:, K_ID:K_ID + P]
        x_hl = halves[:, 0:TOK]
        split = halves[:, TOK + 2 * 4 * S:TOK + 2 * 5 * S].rearrange("p (t c) -> p t c", c=P)
        xc = tmp[:, 0:NT * D].rearrange("p (t d) -> p t d", d=D)
        sq = tmp[:, NT * D:2 * NT * D].rearrange("p (t d) -> p t d", d=D)

        def stacked(sec, n):
            return w_hi[:, sec:sec + n], w_lo[:, sec:sec + n]

        xa = halves[:, 0:B * T_IMG]
        qa_hi = halves[:, TOK:TOK + B * T_IMG]
        qa_lo = halves[:, TOK + B * T_IMG:TOK + 2 * B * T_IMG]
        ka = halves[:, TOK + 2 * B * T_IMG:TOK + 3 * B * T_IMG]
        va = big[:, EARLY * WG:EARLY * WG + B * JI * D]
        o = EARLY * WG + B * JI * D
        poly = big[0:TURNS * DEGS, o:o + D]
        powers_t = big[0:TURNS * DEGS, o + D:o + D + B * P].rearrange("p (b t) -> p b t", b=B)
        o += D + B * P
        tok4 = big[:, o:o + 8 * B * TURNS].rearrange("p (n t) -> p n t", n=8)
        o += 8 * B * TURNS
        powers = big[:, o:o + B * TURNS * DEGS].rearrange("p (b t k) -> p b t k", b=B, t=TURNS)
        o += B * TURNS * DEGS
        factors = big[0:D, o:o + NM]
        gamma = mid[:, 0:JI * T_IMG].rearrange("p (j t) -> p j t", j=JI)
        ret = mid[:, JI * T_IMG:JI * T_IMG + T_IMG]
        ASTEPS = B * JI
        as_bank = (2, 0, 6)
        pa = [v[:, n * T_IMG:(n + 1) * T_IMG] for v in (tmp, raw1) for n in range(2)]
        gc_hi = [halves[:, TOK + b * 2 * S:TOK + b * 2 * S + S] for b in range(B)]
        gc_lo = [halves[:, TOK + b * 2 * S + S:TOK + b * 2 * S + 2 * S] for b in range(B)]
        vc = mid[:, 0:NT * D]
        pc = [mid[:, NT * D + n * S:NT * D + n * S + S] for n in range(3)]
        pc_tiles = [v[:, 0:8 * P].rearrange("p (t r q) -> p r t q", r=2, q=P) for v in pc]
        out_t = mid[:, NT * D + 3 * S + 3 * D:NT * D + 3 * S + 3 * D + 5 * P]
        vs = [mid[:, NT * D + 3 * S + n * D:NT * D + 3 * S + n * D + D] for n in range(3)]
        hid = [mid[:, n * TOK:(n + 1) * TOK] for n in range(3)]
        res = mid[:, 3 * TOK:4 * TOK]
        wr = big[:, :].rearrange("p (g l n) -> p g l n", g=GROUPS, l=LAYERS)
        v_all = mid[:, :].rearrange("p (t n) -> p t n", n=HEADS * D)
        acc = big[:, 0:B * S].rearrange("p (b t) -> p b t", b=B)
        base = B * S
        RING = 6
        pe_ring = big[:, base:base + RING * 2 * CH].rearrange("p (n h t) -> p n h t", n=RING, h=2)
        base += RING * 2 * CH
        v_cur = [big[:, base + b * S:base + (b + 1) * S].rearrange("p (j n) -> p j n", n=P) for b in range(B)]
        base += B * S
        g_hi, g_lo = ([halves[:, TOK + b * 4 * S + m * 2 * S:TOK + b * 4 * S + (m + 1) * 2 * S]
                       .rearrange("p (h t) -> p h t", h=2) for b in range(B)] for m in range(2))

        act_f = mid[:, :].rearrange("p (u t) -> p u t", u=ME // 2)
        c_hl = halves[:, TOK:2 * TOK]
        cc = halves[:, 2 * TOK:3 * TOK].rearrange("p (t c) -> p t c", c=P)
        sel = halves[:, 3 * TOK:3 * TOK + ME * D]
        sel_in = big[:, base:base + ME * D]
        base += ME * D
        slot = [big[:, base + n * NT * ME:base + (n + 1) * NT * ME] for n in range(8)]
        gate = [v.rearrange("p (t e) -> p t e", e=ME) for v in slot[:7]]
        per_tok = [slot[7][:, n * NT:(n + 1) * NT] for n in range(8)]
        base += 8 * NT * ME
        y_t = [big[:, base + n * CH:base + (n + 1) * CH] for n in range(2)]

        NORM_FIRST, NORM_STEPS = 4, 7

        DG = 8
        DW = DG * GT
        NDC = GROUPS // DG
        DBC = NDC // B
        DSTEP = [(l, c) for b in range(B) for l in range(LAYERS) for c in range(b * DBC, (b + 1) * DBC)]
        NDS = len(DSTEP)
        SUM_BEFORE = 6
        D_NORM = ((0, 1), (2, 3), (), (4, 5), (6,))
        D_TR_AT, D_IN_AT = {5: (3, 4), 6: (5,)}, 6
        D_OUT_AT, E_NORM_AT = NDS // B, NDS // B + 1
        D_IN_BANK = (3, 4, 5, 6, 7, 6)
        D_OUTS = ((0, 9, 6), (9, 6, 5), (15, 3, 4))

        STEPS = J * NCH
        PV0 = RING
        AF0 = NCH
        UNITS = 2 * NCH
        E_TG = ((0, 4, 6), (4, 4, 7), (8, 1, 3), (9, 4, 6), (13, 2, 7), (15, 3, 6))
        E_TR_LAST = 13
        UNIT_AT = (2, 3, 7, 8, 11, 12)
        V_BANKS = 3
        V_LATE = NT - 3
        SCORES_AT = (16, 17)
        K_OUT = (2, 5, 11, 20)
        K_TR = (13, 15, 17, 18)
        K_R = 19
        OUTS = ((0, 8, 7), (8, 1, 7), (9, 3, 7), (12, 3, 1), (15, 3, 2))
        NORM_PARTS = {"c": ((0, J), (J, J)), "d": ((0, J), (J, J)), "e": [v[:2] for v in D_OUTS],
                      "f": ((0, 9), (9, 3), (12, 3), (15, 3))}
        F_TG = ((0, 4, 7), (4, 4, 7), (8, 1, 7), (9, 3, 0), (12, 3, 1), (15, 3, 2))
        F_X = (4, 6)
        F_PART = ((0, 12, 7), (12, 6, 1))
        F_CC = ((0, 4, 6), (4, 4, 7), (8, 4, 6), (12, 4, 1), (16, 2, 5))
        F_CC_OF = ((0, 3), (3, 5))
        F_Y_BANK = (0, 3)
        FU = [(ch, u) for ch in range(B * NCH) for u in range(ME // 2)]

        block = ctx.enter_context(nc.Block())

        @block.sync
        def _(sp):
            sp.dma_start(raw2[:, 0:W_CV], w_stack[:, 0:W_CV]).then_inc(s("w_first_in"), 16)
            for c in range(4):
                sp.dma_start(raw1[:, c * BANK:(c + 1) * BANK], x_stack[c]).then_inc(s(f"x_in{c}"), 16)
            sp.dma_start(plain[:, :], w_plain).then_inc(s("plain_in"), 16)
            sp.dma_start(idx[:, :], ids).then_inc(s("ids_in"), 16)
            sp.dma_start(route_row[:, :], route).then_inc(s("route_in"), 16)
            for j in range(JI):
                sp.dma_start(gamma[:, j, :], gamma_t[j]).then_inc(s(f"gamma_in{j}"), 16)
            sp.dma_start(raw2[:, W_CV:NW], w_stack[:, W_CV:NW]).then_inc(s("w_rest_in"), 16)
            sp.dma_start(factors, w_factors).then_inc(s("factors_in"), 16)
            sp.dma_start(br[:, :], w_br).then_inc(s("small_in"), 16)
            sp.dma_start(poly[:, :], w_poly).then_inc(s("small_in"), 16)
            sp.dma_start(route_all[:, :], route.broadcast_to([EXPERTS, GROUPS])).then_inc(s("small_in"), 16)
            sp.wait_ge(s("route_in"), 16)
            for g0, g1 in ((0, EARLY), (EARLY, GROUPS)):
                if g0:
                    sp.wait_ge(s("b_emb"), 1)
                    sp.wait_ge(s("e_merge"), 3)
                with sp.Fori(g0 // 4, g1 // 4) as g4:
                    for n in range(4):
                        e = sp.value_load(route_row[0:1, bass.ds(g4 * 4 + n, 1)], min_val=0, max_val=EXPERTS - 1)
                        sp.dma_start(big[:, bass.ds((g4 * 4 + n) * WG, WG)],
                                     w_route[bass.ds(e, 1), :, :].rearrange("e p n -> p (e n)")).then_inc(s(f"wr_{'late' if g0 else 'early'}{n % 2}"), 16)
            sp.wait_ge(s("w_rest_lo"), 1)
            sp.dma_start(raw2[:, NT * D:NT * D + PAIRS * D], w_late[:, 0:PAIRS * D]).then_inc(s("late_in"), 16)
            sp.wait_ge(s("h3"), 3)
            sp.dma_start(sel_in, w_late[:, PAIRS * D:PAIRS * D + ME * D]).then_inc(s("sel_in"), 16)
            for b in range(B):
                sp.wait_ge(s("h5"), b + 1)
                sp.dma_start(out[b].rearrange("(j p) d -> p j d", p=P), h[:, b * J:(b + 1) * J, :]).then_inc(s("out"), 16)
            sp.wait_ge(s("out"), 32)

        def tiles_of(st, n):
            t0, k = NORM_PARTS[st][n]
            return slice(t0, t0 + k)

        def nth(st, n):
            return sum(len(parts) for name, parts in NORM_PARTS.items() if name < st) + n + 1

        @block.gpsimd
        def _(pool):
            pool.memset(stat[:, 3, :], -0.5).then_inc(s("expo"), 1)
            pool.wait_ge(s("ids_in"), 16)
            for b in range(B):
                pool.indirect_dma_start(tok4[:, 0, b * TURNS:(b + 1) * TURNS], None, turns,
                                        bass.IndirectOffsetOnAxis(ap=idx[:, b:b + 1], axis=0)).then_inc(s("turns_in"), 16)

            def rstd(st, b):
                t = tiles_of(st, b)
                pool.wait_ge(s(st + "_var"), b + 1)
                pool.tensor_tensor(stat[:, 2, t], stat[:, 1, t], stat[:, 3, t], ALU.pow).then_inc(s(st + "_rstd"), 1)

            pool.wait_ge(s("expo"), 1)
            for b in range(B):
                rstd("c", b)
            pool.wait_ge(s("merged"), 3)
            pool.tensor_copy(w_hi[:, W_EM:NWM], raw1[:, 0:NWM - W_EM]).then_inc(s("merged_hi"), 1)
            pool.wait_ge(s("merged_hi"), 1)
            pool.tensor_tensor(w_lo[:, W_EM:NWM], raw1[:, 0:NWM - W_EM], w_hi[:, W_EM:NWM].bitcast(F32),
                               ALU.subtract).then_inc(s("merged_lo"), 1)
            def v_copy(hp, b):
                pool.tensor_copy(v_cur[b], v_all[:, b * J:(b + 1) * J, bass.ds(hp * P, P)]).then_inc(s("e_vcur"), 1)

            def w_copy(hp):
                for w in (w_hi, w_lo):
                    pool.tensor_copy(w[:, W_CUR:W_CUR + 2 * P], w[:, bass.ds(hp * 2 * P + W_EM, 2 * P)]).then_inc(s("e_w"), 1)

            pool.wait_ge(s("merged_lo"), 1)
            w_copy(0)
            def add_shared(c):
                for n in range(2):
                    if c == 0:
                        pool.wait_ge(s(f"wr_early{n}"), 16 * EARLY // 2)
                    if c == EARLY // DG:
                        pool.wait_ge(s(f"wr_late{n}"), 16 * (GROUPS - EARLY) // 2)
                w = big[:, c * DG * WG:(c + 1) * DG * WG].rearrange("p (g n) -> p g n", n=WG)
                pool.tensor_tensor(w, w, plain[:, K_WS:K_WS + WG].unsqueeze(1).broadcast_to([P, DG, WG]), ALU.add)\
                    .then_inc(s("wr_sum"), 1)

            def d_bias_out(b):
                t = slice(b * J, (b + 1) * J)
                pool.wait_ge(s("norm_xc"), nth("d", b))
                pool.tensor_tensor(h[:, t, :], h[:, t, :], plain[:, K_BOD:K_BOD + D].unsqueeze(1).broadcast_to([P, J, D]),
                                   ALU.add).then_inc(s("d_hb"), 1)

            for l in range(LAYERS):
                ws = plain[:, K_WS + l * HID:K_WS + (l + 1) * HID]
                pool.tensor_tensor(ws, ws, ident, ALU.add).then_inc(s("ws_id"), 1)
            pool.wait_ge(s("ws_id"), LAYERS)
            for c in range(NDC):
                if c == SUM_BEFORE:
                    rstd("d", 0)
                    d_bias_out(0)
                add_shared(c)
            rstd("d", 1)
            d_bias_out(1)
            for n in range(3):
                rstd("e", n)
            for b in range(B):
                pool.wait_ge(s("e_v_read"), min(J * (b + 1), V_LATE))
                if b == B - 1:
                    pool.wait_ge(s("e_v_late"), NT - V_LATE)
                v_copy(0, b)
            pool.memset(acc, 0.0).then_inc(s("e_zero"), 1)
            with pool.Fori(1, PAIRS) as hp:
                pool.wait_ge(s("e_proj"), hp * (B * UNITS))
                w_copy(hp)
                for b in range(B):
                    pool.wait_ge(s("e_pv"), hp * (B * STEPS) + (b - 1) * STEPS + PV0)
                    v_copy(hp, b)
            pool.wait_ge(s("e_pv"), (PAIRS * B - 1) * STEPS + PV0)
            pool.memset(cc.rearrange("p t c -> p (t c)").bitcast(F32), 0.0).then_inc(s("f_zero"), 1)
            for n in range(len(NORM_PARTS["f"])):
                t = tiles_of("f", n)
                rstd("f", n)
                pool.wait_ge(s("f_split"), n + 1)
                pool.tensor_tensor(h[:, t, :], h[:, t, :], xc[:, t, :], ALU.add).then_inc(s("f_hx"), 1)

        def product(pe, dst, stationary, moving_hi, moving_lo, sem=None):
            pe.matmul(dst, stationary, moving_hi, start=True, stop=False)
            m = pe.matmul(dst, stationary, moving_lo, start=False, stop=True)
            if sem is not None:
                m.then_inc(sem, 1)

        def product_w(pe, dst, w_pair, moving, sem=None):
            pe.matmul(dst, w_pair[0], moving, start=True, stop=False)
            m = pe.matmul(dst, w_pair[1], moving, start=False, stop=True)
            if sem is not None:
                m.then_inc(sem, 1)

        def norm_step(dve, st, b, i):
            t = tiles_of(st, b)
            n_t = t.stop - t.start
            n = nth(st, b)
            if i == 0:
                dve.reduce_sum(stat[:, 0, t], h[:, t, :], AX_X).then_inc(s("norm_sum"), 1)
            if i == 1:
                dve.wait_ge(s("norm_sum"), n)
                dve.scalar_tensor_tensor(out=xc[:, t, :], in0=stat[:, 0, t].unsqueeze(2).broadcast_to([P, n_t, D]),
                                         scalar=-1.0 / D, in1=h[:, t, :], op0=ALU.mult, op1=ALU.add).then_inc(s("norm_xc"), 1)
            if i == 2 and st != "c":
                dve.wait_ge(s("norm_xc"), n)
                dve.tensor_tensor(sq[:, t, :], xc[:, t, :], xc[:, t, :], ALU.mult).then_inc(s("norm_sq"), 1)
            if i == 3:
                dve.wait_ge(s("norm_sq"), n)
                dve.reduce_sum(stat[:, 1, t], sq[:, t, :], AX_X).then_inc(s("norm_ssq"), 1)
                dve.wait_ge(s("norm_ssq"), n)
                dve.tensor_scalar(stat[:, 1, t], stat[:, 1, t], 1.0 / D, EPS, ALU.mult, ALU.add).then_inc(s(st + "_var"), 1)
            if i == 4:
                dve.wait_ge(s(st + "_rstd"), b + 1)
                dve.tensor_tensor(xc[:, t, :], xc[:, t, :], stat[:, 2, t].unsqueeze(2).broadcast_to([P, n_t, D]),
                                  ALU.mult).then_inc(s("norm_xn"), 1)
            if i == 5 and st != "c":
                dve.wait_ge(s("norm_xn"), n)
                dve.tensor_copy(split[:, t, 0:D], xc[:, t, :]).then_inc(s("norm_xhi"), 1)
            if i == 6:
                dve.wait_ge(s("norm_xhi"), n)
                dve.tensor_tensor(split[:, t, D:P], xc[:, t, :], split[:, t, 0:D].bitcast(F32),
                                  ALU.subtract).then_inc(s(st + "_split"), 1)

        def norm_act(act, i):
            for b in range(B):
                t = slice(b * J, (b + 1) * J)
                if i == 2:
                    act.wait_ge(s("norm_xc"), b + 1)
                    act.activation(sq[:, t, :], xc[:, t, :], ACT.Square).then_inc(s("norm_sq"), 1)
                if i == 5:
                    act.wait_ge(s("norm_xn"), b + 1)
                    act.copy(split[:, t, 0:D], xc[:, t, :]).then_inc(s("norm_xhi"), 1)

        def norm_first(dve, st, b):
            for i in range(NORM_FIRST):
                norm_step(dve, st, b, i)

        def norm_second(dve, st, b):
            for i in range(NORM_FIRST, NORM_STEPS):
                norm_step(dve, st, b, i)

        TG = [(b, j0, n) for b in range(B) for j0, n in ((0, 4), (4, 4), (8, 1))]

        def tr_bank(st, n):
            if st == "d" and n < 3:
                return n
            return {"e": E_TG, "f": F_TG}[st][n][2] if st in "ef" else 6 + n % 2

        def tr_tiles(st, n):
            return {"e": E_TG, "f": F_TG}[st][n][:2] if st in "ef" else (TG[n][0] * J + TG[n][1], TG[n][2])

        def transpose_group(pe, st, n):
            t0, k = tr_tiles(st, n)
            before = [m for m in range(n) if tr_bank(st, m) == tr_bank(st, n)]
            if before:
                pe.wait_ge(s(st + "_xt"), before[-1] + 1)
            for i in range(k):
                m = pe.transpose(bank(tr_bank(st, n), i * P, (i + 1) * P), split[:, t0 + i, :].bitcast(F32), ident)
            m.then_inc(s(st + "_tr"), 1)

        def transposes_pe(pe, st, b):
            pe.wait_ge(s(st + "_split"), b + 1)
            for n in range(3 * b, 3 * b + 3):
                transpose_group(pe, st, n)

        def copy_group(act, st, n):
            t0, k = tr_tiles(st, n)
            act.wait_ge(s(st + "_tr"), n + 1)
            act.copy(x_hl[:, t0 * P:(t0 + k) * P], bank(tr_bank(st, n), 0, k * P)).then_inc(s(st + "_xt"), 1)

        def transposes_act(act, st, b):
            for n in range(3 * b, 3 * b + 3):
                copy_group(act, st, n)

        NX = [3, 6]

        CUN = 5
        CU = [(b, u) for b in range(B) for u in range(CUN)]
        CSTEP = [(b, j) for b in range(B) for j in range(J)]

        def c_width(j):
            return S if j == 0 else (j + 1) * P

        @block.tensor
        def _(pe):
            pe.wait_ge(s("w_first_lo"), 1)
            for c in range(4):
                pe.wait_ge(s("xa_lo"), c + 1)
                cols = slice(c * BANK, (c + 1) * BANK)
                if c >= 2:
                    pe.wait_ge(s("qa_lo"), c - 1)
                product_w(pe, bank(4 + c % 2), stacked(W_AQ, P), xa[:, cols], s("a_q"))
                if c >= 2:
                    pe.wait_ge(s("ka_lo"), c - 1)
                product_w(pe, bank(6 + c % 2), stacked(W_AK, P), xa[:, cols], s("a_k"))
            def a_scores(m):
                if m >= ASTEPS:
                    return
                j, b = m // B, m % B
                if m == 1:
                    pe.wait_ge(s("va"), 2)
                if m < 2:
                    pe.wait_ge(s("qa_lo"), 2 * (b + 1))
                    pe.wait_ge(s("ka_lo"), 2 * (b + 1))
                if m >= 3:
                    pe.wait_ge(s("pa"), m - 2)
                st = ka[:, b * T_IMG + j * P:b * T_IMG + (j + 1) * P]
                for c in range(2):
                    q = slice(b * T_IMG + c * BANK, b * T_IMG + (c + 1) * BANK)
                    product(pe, bank(as_bank[m % 3] + c), st, qa_hi[:, q], qa_lo[:, q], s("a_s") if c == 1 else None)

            a_scores(0)
            for t in range(B * JI):
                product(pe, bank(t // JI, (t % JI) * D, (t % JI + 1) * D), xa[:, t * P:(t + 1) * P],
                        *stacked(W_AV, D), s("a_v"))
            a_scores(1)
            a_scores(2)
            for j in range(JI):
                a_scores(B * j + 3)
                if j == JI - 1:
                    pe.wait_ge(s("powers"), 4)
                    pe.wait_ge(s("pa"), ASTEPS - 2)
                    for b in range(B):
                        m = pe.transpose(ps[0:TURNS * DEGS, b * P:(b + 1) * P],
                                         powers[:, b, :, :].rearrange("p t k -> p (t k)"), ident)
                    m.then_inc(s("b_tr"), 1)
                pe.wait_ge(s("pa"), B * (j + 1))
                for c in range(2):
                    for b in range(B):
                        m = pe.matmul(ps[b * D:(b + 1) * D, (4 + c) * BANK:(5 + c) * BANK],
                                      va[:, (b * JI + j) * D:(b * JI + j + 1) * D],
                                      pa[(B * j + b) % 4][:, c * BANK:(c + 1) * BANK], start=(j == 0), stop=(j == JI - 1),
                                      skip_group_check=True)
                m.then_inc(s("a_pv"), 1)
                a_scores(B * j + 4)
            pe.wait_ge(s("powers_t"), 1)
            pe.wait_ge(s("small_in"), 48)
            for b in range(B):
                m = pe.matmul(bank(1, b * D, (b + 1) * D), powers_t[:, b, :], poly[:, :], start=True, stop=True)
            m.then_inc(s("b_emb"), 1)
            pe.wait_ge(s("d_onehot"), 1)
            for l in range(LAYERS):
                m = pe.matmul(bank(0, l * GROUPS, (l + 1) * GROUPS), br[:, l * HID:(l + 1) * HID], onehot[:, :],
                              start=True, stop=True)
            m.then_inc(s("d_bp"), 1)
            pe.wait_ge(s("factors_in"), 16)
            pe.matmul(bank(7, 0, P), factors[:, M_CQ:M_CQ + P], factors[:, M_CK:M_CK + P],
                      start=True, stop=True).then_inc(s("c_merge"), 1)
            for n in range(HEADS):
                m = pe.matmul(bank(6, n * D, (n + 1) * D), factors[:, M_EV + n * P:M_EV + (n + 1) * P],
                              factors[:, M_EO + n * D:M_EO + (n + 1) * D], start=True, stop=True)
            m.then_inc(s("e_merge"), 1)
            pe.wait_ge(s("ret"), 2)
            for j in range(JI):
                m = pe.matmul(bank(2 + j // 4, (j % 4) * P, (j % 4 + 1) * P), ret[:, j * P:(j + 1) * P],
                              plain[:, K_WOA:K_WOA + P], start=True, stop=True)
                if j % 4 == 3:
                    m.then_inc(s("a_y"), 1)
            for n in range(HEADS):
                m = pe.matmul(bank(4 + n // 4, n % 4 * P, (n % 4 + 1) * P), factors[:, M_EQ + n * P:M_EQ + (n + 1) * P],
                              factors[:, M_EK + n * P:M_EK + (n + 1) * P], start=True, stop=True)
                if n % 4 == 3:
                    m.then_inc(s("e_merge"), 1)
            pe.wait_ge(s("merged"), 1)
            pe.wait_ge(s("cm_lo"), 1)
            for b in range(B):
                transposes_pe(pe, "c", b)
            pe.wait_ge(s("w_rest_lo"), 1)
            pe.wait_ge(s("d_bias"), LAYERS)
            pe.wait_ge(s("merged"), 3)
            for n, (b, u) in enumerate(CU):
                if u == 0:
                    pe.wait_ge(s("c_xt"), NX[b])
                if 6 <= n < 9:
                    pe.wait_ge(s("c_lo"), n - 5)
                if n == 9:
                    pe.wait_ge(s("c_v"), 1)
                if u < 3:
                    x = x_hl[:, b * S + u * CH:b * S + (u + 1) * CH]
                    product_w(pe, bank(n % 6, 0, CH), stacked(W_CM, P), x, s("c_proj"))
                else:
                    tiles = range(8) if u == 3 else [8]
                    for t in tiles:
                        product(pe, bank(n % 6, (t % 8) * D, (t % 8 + 1) * D), x_hl[:, (b * J + t) * P:(b * J + t + 1) * P],
                                *stacked(W_CV, D), s("c_proj") if t == tiles[-1] else None)

            def c_pv(n):
                b, j = CSTEP[n]
                pe.wait_ge(s("c_vs"), n + 1)
                if j == 0:
                    if b == 0:
                        pe.wait_ge(s("c_xt"), NX[1])
                    else:
                        pe.wait_ge(s("h2"), 1)
                last = 8 if j in (0, J - 1) else j + 1
                for r in range(2):
                    k = (last + 1 - r) // 2
                    m = pe.matmul(ps[r * D:(r + 1) * D, 6 * BANK:6 * BANK + k * P], vs[n % 3], pc_tiles[n % 3][:, r, 0:k, :],
                                  start=(j == 0), stop=(j == J - 1), skip_group_check=True)
                if j in (0, J - 1):
                    m = pe.matmul(ps[0:D, 7 * BANK:7 * BANK + P], vs[n % 3], pc[n % 3][:, 8 * P:9 * P],
                                  start=(j == 0), stop=(j == J - 1), skip_group_check=True)
                m.then_inc(s("c_pv"), 1)

            def c_output(b):
                pe.wait_ge(s("c_out"), 2 * (b + 1))
                for i in range(4):
                    pe.transpose(bank(6, i * P, (i + 1) * P), out_t[:, i * P:(i + 1) * P], ident)
                pe.transpose(bank(7, 0, D), out_t[0:D, 4 * P:5 * P], plain[0:D, K_ID:K_ID + D]).then_inc(s("c_otr"), 1)

            def c_scores(n):
                b, j = CSTEP[n]
                if n == 0:
                    pe.wait_ge(s("c_lo"), B * 3)
                    pe.wait_ge(s("c_v"), B * 2)
                    pe.wait_ge(s("mask_lo"), 1)
                if n >= 2:
                    pe.wait_ge(s("c_exp"), n - 1)
                w = c_width(j)
                o = n % 2 * 3 * BANK
                for c0 in range(0, w, BANK):
                    c1 = min(c0 + BANK, w)
                    d0, d1 = j * P, (j + 1) * P
                    masked = [(d0, d1, [mask_hl[:, m * P:(m + 1) * P] for m in range(2)])] if c0 <= d0 < c1 else []
                    if j == 0:
                        r0 = max(c0, P)
                        masked.append((r0, c1, [mask_hl[:, (m + 1) * P - 1:(m + 1) * P].broadcast_to([P, c1 - r0]) for m in range(2)]))
                    pe.matmul(ps[:, o + c0:o + c1], x_hl[:, (b * J + j) * P:(b * J + j + 1) * P], gc_hi[b][:, c0:c1],
                              start=True, stop=False, skip_group_check=True)
                    m = pe.matmul(ps[:, o + c0:o + c1], x_hl[:, (b * J + j) * P:(b * J + j + 1) * P], gc_lo[b][:, c0:c1],
                                  start=False, stop=not masked, skip_group_check=True)
                    for m0, m1, halves_of in masked:
                        for k in range(2):
                            m = pe.matmul(ps[:, o + m0:o + m1], ident_r[:, :], halves_of[k], start=False,
                                          stop=(m1 == masked[-1][1] and k == 1), skip_group_check=True)
                    if c1 == w:
                        m.then_inc(s("c_s"), 1)

            c_scores(0)
            c_scores(1)
            for n in range(len(CSTEP)):
                if n + 2 < len(CSTEP):
                    c_scores(n + 2)
                if n == J:
                    c_output(0)
                if n == len(CSTEP) - 2:
                    pe.wait_ge(s("c_exp"), n + 1)
                    transposes_pe(pe, "d", 0)
                c_pv(n)
            def d_input(b):
                for n in range(b * NCH, (b + 1) * NCH):
                    pe.wait_ge(s("d_xt"), NX[b])
                    if n == B * NCH - 1:
                        pe.wait_ge(s("d_h0"), n - 1)
                    product_w(pe, bank(D_IN_BANK[n], 0, CH), stacked(W_DI, HID), x_hl[:, n * CH:(n + 1) * CH], s("d_in"))

            def d_chunk(n):
                l, c = DSTEP[n]
                pe.wait_ge(s("wr_sum"), c + 1)
                if l == 0:
                    pe.wait_ge(s("d_h0"), NCH if c < DBC else B * NCH)
                else:
                    pe.wait_ge(s("d_h1"), c + 1)
                if n >= 4:
                    pe.wait_ge(s("d_z"), n - 3)
                o = c * DW
                for g in range(DG):
                    m = pe.matmul(bank(n % 4, g * GT, (g + 3) * GT).rearrange("p (r t) -> p r t", r=3), wr[:, c * DG + g, l, :],
                                  hid[l][:, o + g * GT:o + (g + 1) * GT].unsqueeze(1).broadcast_to([P, 3, GT]),
                                  start=True, stop=True)
                m.then_inc(s("d_f"), 1)

            def d_output(n):
                t0, k, bk = D_OUTS[n]
                pe.wait_ge(s("d_h2"), -(-(t0 + k) * P // DW))
                for i in range(k):
                    o = bk * BANK + i * D
                    m = pe.matmul(ps[:, o:o + D], hid[2][:, (t0 + i) * P:(t0 + i + 1) * P], plain[:, K_WOD:K_WOD + D],
                                  start=True, stop=True)
                m.then_inc(s("d_o"), 1)

            pe.wait_ge(s("c_exp"), len(CSTEP))
            d_input(0)
            c_output(1)
            for n in range(NDS):
                d_chunk(n)
                if n in D_TR_AT:
                    pe.wait_ge(s("d_split"), 2)
                for g in D_TR_AT.get(n, ()):
                    transpose_group(pe, "d", g)
                if n == D_IN_AT:
                    d_input(1)
                if n == D_OUT_AT:
                    d_output(0)
            d_output(1)
            d_output(2)
            def unit(u, b_x, dst):
                c = u % NCH
                product_w(pe, dst, stacked(W_CUR + u // NCH * P, P), x_hl[:, b_x * S + c * CH:b_x * S + (c + 1) * CH], s("e_proj"))

            def order(n, last):
                k = n % STEPS
                return (k % J, k // J) if last and n >= STEPS else (k // NCH, k % NCH)

            def scores(step, last=False):
                b, (j, c) = step // STEPS, order(step, last)
                for hd in range(2):
                    product(pe, bank(3 + 2 * (step % 2) + hd, 0, CH), x_hl[:, (b * J + j) * P:(b * J + j + 1) * P],
                            g_hi[b][:, hd, c * CH:(c + 1) * CH], g_lo[b][:, hd, c * CH:(c + 1) * CH],
                            s("e_qk") if hd == 1 else None)

            pe.sem_inc(s("e_pv"), PV0)
            def transposed_for(tile):
                return next(g + 1 for g, (t0, k, _) in enumerate(E_TG) if tile < t0 + k)

            for t in range(NT):
                if t in (0, J):
                    pe.wait_ge(s("e_split"), t // J + 1)
                    for g in range(3) if t == 0 else range(3, 5):
                        transpose_group(pe, "e", g)
                if t == 0:
                    pe.wait_ge(s("e_w"), 2)
                if t in UNIT_AT:
                    u = UNIT_AT.index(t)
                    pe.wait_ge(s("e_xt"), transposed_for((u % NCH + 1) * CH // P - 1))
                    if u == 0:
                        pe.wait_ge(s("h3"), 3)
                    if u >= 2:
                        pe.wait_ge(s("e_proj_read"), u - 1)
                    unit(u, 0, bank(4 + u % 2, 0, CH))
                if t in SCORES_AT:
                    pe.wait_ge(s("e_proj_read"), UNITS)
                    scores(SCORES_AT.index(t))
                pe.wait_ge(s("e_xt"), transposed_for(t))
                if t >= V_BANKS:
                    pe.wait_ge(s("e_v_read"), t - V_BANKS + 1)
                product(pe, bank(t % V_BANKS), x_hl[:, t * P:(t + 1) * P], *stacked(W_EV, HEADS * D), s("e_v"))
                if t == E_TR_LAST:
                    pe.wait_ge(s("e_split"), 3)
                    transpose_group(pe, "e", 5)

            def output(n):
                t0, k, bk = OUTS[n]
                pe.wait_ge(s("e_acc_read"), AF0 + (PAIRS * B - 1) * NCH + max(n - 1, 0))
                if n in (1, 2):
                    pe.wait_ge(s("h4"), n)
                for i in range(k):
                    b, j = (t0 + i) // J, (t0 + i) % J
                    m = pe.matmul(bank(bk, i * D, (i + 1) * D), acc[:, b, j * P:(j + 1) * P], plain[:, K_ID2:K_ID2 + D],
                                  start=True, stop=True)
                m.then_inc(s("e_o"), 1)

            def router(n):
                t0, k, bk = F_PART[n]
                pe.wait_ge(s("f_xt"), F_X[n])
                pe.wait_ge(s("w_side"), 4)
                for i in range(k):
                    m = pe.matmul(bank(bk, i * 2 * ME, (i + 1) * 2 * ME), x_hl[:, (t0 + i) * P:(t0 + i + 1) * P], w_router[:, :],
                                  start=True, stop=True)
                m.then_inc(s("f_r"), 1)

            def pv(it, n, last):
                b, (j, c) = n // STEPS, order(n, last)
                if n < NCH:
                    pe.wait_ge(s("e_v_late"), c + 1)
                if n % STEPS == 0:
                    pe.wait_ge(s("e_vcur"), it * B + (b + 1))
                if j == 0:
                    pe.wait_ge(s("e_acc_read"), it * (B * NCH) + (b * NCH + c + 1))
                pe.wait_ge(s("e_sig"), it * (B * STEPS) + (n + 1))
                for hd in range(2):
                    m = pe.matmul(ps[hd * D:(hd + 1) * D, c * BANK:c * BANK + CH], v_cur[b][:, j, hd * D:(hd + 1) * D],
                                  pe_ring[:, n % RING, hd, :], start=(j == 0), stop=(j == J - 1), skip_group_check=True)
                m.then_inc(s("e_pv"), 1)

            def pair_steps(it, last):
                for n in range(B * STEPS):
                    b, k = n // STEPS, n % STEPS
                    if n % 2 == 0:
                        for ahead in (n + 2, n + 3):
                            if not (last and ahead >= B * STEPS):
                                pe.wait_ge(s("e_sig"), it * (B * STEPS) + (ahead - 1))
                                if ahead % STEPS == 0:
                                    pe.wait_ge(s("e_proj_read"), it * (B * UNITS) + (ahead // STEPS + 1) * UNITS)
                                scores(ahead % (B * STEPS), last)
                        pv(it, n, last)
                        pv(it, n + 1, last)
                    if k % 4 == 0 and k // 4 < UNITS and not (last and b == B - 1):
                        u = k // 4
                        if u == 0 and b == B - 1:
                            pe.wait_ge(s("e_w"), it * 2 + 4)
                        pe.wait_ge(s("e_proj_read"), it * (B * UNITS) + ((b + 1) * UNITS + u))
                        unit(u, 1 - b, bank(7, 0, CH))
                    if last and b == B - 1:
                        if k == K_OUT[0]:
                            pe.wait_ge(s("e_proj_read"), PAIRS * B * UNITS)
                        if k in K_OUT:
                            output(K_OUT.index(k))
                        if k in K_TR:
                            g = K_TR.index(k)
                            pe.wait_ge(s("f_split"), 1 if g < 3 else 2)
                            pe.wait_ge(s("h4"), 3)
                            transpose_group(pe, "f", g)
                        if k == K_R:
                            router(0)

            with pe.Fori(0, PAIRS - 1) as it:
                pair_steps(it, False)
            pair_steps(PAIRS - 1, True)

            def first_layer(units):
                for n in units:
                    ch, u = FU[n]
                    if n >= 2:
                        pe.wait_ge(s("f_gelu"), n - 1)
                    product_w(pe, bank(3 + n % 2, 0, CH), stacked(W_F1 + u * P, P), x_hl[:, ch * CH:(ch + 1) * CH], s("f_1"))

            def combine_transposes(n):
                pe.wait_ge(s("f_cc"), n + 1)
                for g in range(*F_CC_OF[n]):
                    t0, k, bk = F_CC[g]
                    if g == 2:
                        pe.wait_ge(s("f_ct"), 1)
                    for i in range(k):
                        m = pe.transpose(bank(bk, i * P, (i + 1) * P), cc[:, t0 + i, :].bitcast(F32), ident)
                    m.then_inc(s("f_ctr"), 1)

            def spread(n):
                ch, u = FU[n]
                pe.wait_ge(s("f_ct"), 3 if ch < 4 else 5)
                if n >= 2:
                    pe.wait_ge(s("f_hc"), n - 1)
                pe.matmul(bank(6 + n % 2, 0, CH), sel[:, u * P:(u + 1) * P], c_hl[:, ch * CH:(ch + 1) * CH],
                          start=True, stop=True).then_inc(s("f_cb"), 1)

            def second_layer(ch):
                pe.wait_ge(s("f_hc"), ME // 2 * (ch + 1))
                if ch == 1:
                    pe.wait_ge(s("f_ct"), 5)
                if ch >= 2:
                    pe.wait_ge(s("f_yt"), ch - 1)
                o, cols = (2, 5)[ch % 2] * BANK, slice(ch * CH, (ch + 1) * CH)
                for u in range(ME // 2):
                    pe.matmul(ps[u % 2 * D:(u % 2 + 1) * D, o:o + CH], w2_f[:, u * D:(u + 1) * D], act_f[:, u, cols],
                              start=(u < 2), stop=False, skip_group_check=True)
                pe.matmul(ps[:, o:o + CH], w_b2[:, :], c_hl[:, cols], start=False, stop=True,
                          skip_group_check=True).then_inc(s("f_y2"), 1)

            def result(ch):
                pe.wait_ge(s("f_yt"), ch + 1)
                for j in range(ch * 3, ch * 3 + 3):
                    if j == J - 1:
                        pe.wait_ge(s("f_ct"), 5)
                    if j == J:
                        pe.wait_ge(s("f_gelu"), 24)
                    o = F_Y_BANK[j // J] * BANK + j % J * D
                    m = pe.matmul(ps[:, o:o + D], y_t[ch % 2][:, j % 3 * P:(j % 3 + 1) * P], plain[:, K_ID2:K_ID2 + D],
                                  start=True, stop=True)
                m.then_inc(s("f_y"), 1)

            def mixture(steps):
                for n in steps:
                    if n < len(FU):
                        spread(n)
                    if n >= 4 and n % 4 == 1:
                        second_layer(n // 4 - 1)
                    if n >= 4 and n % 4 == 3:
                        result(n // 4 - 1)

            first_layer(range(2))
            pe.wait_ge(s("f_split"), 3)
            transpose_group(pe, "f", 4)
            output(4)
            first_layer(range(2, 4))
            combine_transposes(0)
            pe.wait_ge(s("f_sel"), 1)
            mixture(range(2))
            first_layer(range(4, 6))
            pe.wait_ge(s("f_split"), 4)
            transpose_group(pe, "f", 5)
            mixture(range(2, 4))
            router(1)
            mixture(range(4, 6))
            first_layer(range(6, 16))
            combine_transposes(1)
            for n in range(6, 14):
                mixture([n])
                first_layer([n + 10])
            mixture(range(14, 28))

        @block.vector
        def _(dve):
            dve.wait_ge(s("w_first_in"), 16)
            dve.tensor_copy(w_hi[:, 0:W_CV], raw2[:, 0:W_CV]).then_inc(s("w_first_hi"), 1)
            dve.wait_ge(s("w_first_hi"), 1)
            dve.tensor_tensor(w_lo[:, 0:W_CV], raw2[:, 0:W_CV], w_hi[:, 0:W_CV].bitcast(F32),
                              ALU.subtract).then_inc(s("w_first_lo"), 1)
            for c in range(4):
                dve.wait_ge(s(f"x_in{c}"), 16)
                cols = slice(c * BANK, (c + 1) * BANK)
                dve.tensor_copy(xa[:, cols], raw1[:, cols]).then_inc(s("xa_hi"), 1)
                dve.wait_ge(s("xa_hi"), c + 1)
                dve.tensor_tensor(xa[D:P, cols], raw1[D:P, cols], xa[D:P, cols].bitcast(F32),
                                  ALU.subtract).then_inc(s("xa_lo"), 1)
            dve.wait_ge(s("plain_in"), 16)
            for c in range(4):
                cols = slice(c * BANK, (c + 1) * BANK)
                dve.wait_ge(s("qa_hi"), c + 1)
                dve.scalar_tensor_tensor(out=qa_lo[:, cols], in0=bank(4 + c % 2), scalar=plain[:, C_BQ:C_BQ + 1],
                                         in1=qa_hi[:, cols].bitcast(F32), op0=ALU.add, op1=ALU.subtract).then_inc(s("qa_lo"), 1)
                dve.wait_ge(s("ka_hi"), c + 1)
                dve.scalar_tensor_tensor(out=ka[D:P, cols], in0=bank(6 + c % 2)[D:P, :], scalar=plain[D:P, C_BK:C_BK + 1],
                                         in1=ka[D:P, cols].bitcast(F32), op0=ALU.add, op1=ALU.subtract).then_inc(s("ka_lo"), 1)
            for b in range(B):
                dve.wait_ge(s("a_v"), JI * (b + 1))
                dve.tensor_tensor(va[:, b * JI * D:(b + 1) * JI * D].rearrange("p (j d) -> p j d", d=D),
                                  bank(b).rearrange("p (j d) -> p j d", d=D),
                                  plain[:, K_BVA:K_BVA + D].unsqueeze(1).broadcast_to([P, JI, D]), ALU.add).then_inc(s("va"), 1)
            def gated(j):
                dve.wait_ge(s(f"gamma_in{j}"), 16)
                for m in range(B * j, B * (j + 1)):
                    if j >= 2:
                        dve.wait_ge(s("a_pv"), j - 1)
                    dve.wait_ge(s("a_s"), m + 1)
                    o = as_bank[m % 3] * BANK
                    dve.tensor_tensor(pa[m % 4], ps[:, o:o + T_IMG], gamma[:, j, :], ALU.mult).then_inc(s("pa"), 1)

            for j in range(3):
                gated(j)
            flat = [tok4[:, n, :] for n in range(8)]
            dve.wait_ge(s("turns_in"), 32)
            dve.scalar_tensor_tensor(out=flat[1], in0=flat[0], scalar=-1.0, in1=flat[0], op0=ALU.mult, op1=ALU.max)\
               .then_inc(s("text_step"), 1)
            dve.wait_ge(s("text_step"), 1)
            dve.tensor_copy(tok4i[:, :], flat[1]).then_inc(s("text_step"), 1)
            dve.wait_ge(s("text_step"), 2)
            dve.tensor_copy(flat[2], tok4i[:, :]).then_inc(s("text_step"), 1)
            dve.wait_ge(s("text_step"), 3)
            dve.tensor_tensor(flat[3], flat[2], flat[1], ALU.is_gt).then_inc(s("text_step"), 1)
            dve.wait_ge(s("text_step"), 4)
            dve.tensor_tensor(flat[4], flat[2], flat[3], ALU.subtract).then_inc(s("text_step"), 1)
            dve.tensor_scalar(flat[5], flat[0], 0.0, 2.0, ALU.is_ge, ALU.mult).then_inc(s("text_step"), 1)
            dve.wait_ge(s("text_step"), 6)
            dve.scalar_tensor_tensor(out=flat[6], in0=flat[5], scalar=-1.0, in1=flat[4], op0=ALU.add, op1=ALU.mult)\
               .then_inc(s("text_step"), 1)
            pw = [powers[:, :, :, k].rearrange("p b t -> p (b t)") for k in range(DEGS)]
            dve.memset(pw[0], 1.0).then_inc(s("text_step"), 1)
            dve.wait_ge(s("text_step"), 7)
            dve.tensor_copy(pw[1], flat[6]).then_inc(s("powers"), 1)
            dve.tensor_tensor(pw[2], flat[6], flat[6], ALU.mult).then_inc(s("powers"), 1)
            dve.wait_ge(s("powers"), 2)
            dve.tensor_tensor(pw[3], pw[2], flat[6], ALU.mult).then_inc(s("powers"), 1)
            dve.tensor_tensor(pw[4], pw[2], pw[2], ALU.mult).then_inc(s("powers"), 1)
            dve.wait_ge(s("small_in"), 48)
            dve.tensor_scalar(onehot[:, :], route_all[:, :], plain[0:EXPERTS, C_EIDX:C_EIDX + 1], None, ALU.is_equal)\
               .then_inc(s("d_onehot"), 1)
            gated(3)
            dve.wait_ge(s("w_rest_in"), 16)
            dve.tensor_copy(w_hi[:, W_CV:NW], raw2[:, W_CV:NW]).then_inc(s("w_rest_hi"), 1)
            gated(4)
            dve.wait_ge(s("w_rest_hi"), 1)
            dve.tensor_tensor(w_lo[:, W_CV:NW], raw2[:, W_CV:NW], w_hi[:, W_CV:NW].bitcast(F32),
                              ALU.subtract).then_inc(s("w_rest_lo"), 1)
            dve.tensor_copy(ident_r[:, :], ident).then_inc(s("ident_r"), 1)
            dve.tensor_copy(mask_hl[:, 0:P], plain[:, K_MASK:K_MASK + P]).then_inc(s("mask_hi"), 1)
            gated(5)
            dve.wait_ge(s("mask_hi"), 1)
            dve.tensor_tensor(mask_hl[:, P:2 * P], plain[:, K_MASK:K_MASK + P], mask_hl[:, 0:P].bitcast(F32),
                              ALU.subtract).then_inc(s("mask_lo"), 1)
            for j in range(6, JI):
                gated(j)
            dve.wait_ge(s("a_pv"), JI)
            dve.tensor_copy(ret[:, 0:BANK], bank(4)).then_inc(s("ret"), 1)
            dve.wait_ge(s("cm_hi"), 1)
            dve.scalar_tensor_tensor(out=w_lo[:, W_CM:W_CM + P], in0=bank(7, 0, P), scalar=D ** -0.5,
                                     in1=w_hi[:, W_CM:W_CM + P].bitcast(F32), op0=ALU.mult, op1=ALU.subtract).then_inc(s("cm_lo"), 1)
            dve.wait_ge(s("w_rest_lo"), 1)
            dve.wait_ge(s("b_emb"), 1)
            for b in range(B):
                dve.tensor_copy(h[:, b * J + JI, :], bank(1, b * D, (b + 1) * D)).then_inc(s("h1t"), 1)
            for c in range(2):
                y = tmp[:, c * 2 * BANK:c * 2 * BANK + BANK]
                neg = tmp[:, c * 2 * BANK + BANK:(c + 1) * 2 * BANK]
                dve.wait_ge(s("a_y"), c + 1)
                dve.tensor_tensor(y.rearrange("p (c d) -> p c d", d=D), bank(2 + c).rearrange("p (c d) -> p c d", d=D),
                                  plain[:, K_BOA:K_BOA + D].unsqueeze(1).broadcast_to([P, B * JI // 2, D]), ALU.add).then_inc(s("a_yb"), 1)
                dve.wait_ge(s("a_yb"), c + 1)
                dve.tensor_scalar(neg, y, 0.0, plain[:, C_SLOPE:C_SLOPE + 1], ALU.min, ALU.mult).then_inc(s("a_neg"), 1)
                dve.wait_ge(s("a_neg"), c + 1)
                for b in range(B):
                    view = [v.rearrange("p (j b d) -> p b j d", b=B, d=D)[:, b, :, :] for v in (y, neg)]
                    o = b * J + c * JI // 2
                    dve.scalar_tensor_tensor(out=h[:, o:o + JI // 2, :], in0=view[0], scalar=0.0, in1=view[1],
                                             op0=ALU.max, op1=ALU.add).then_inc(s("h1"), 1)
            dve.wait_ge(s("h1t"), 2)
            dve.wait_ge(s("h1"), 4)
            for steps in ((0, 1), (3,), (4,), (6,)):
                for b in range(B):
                    for i in steps:
                        norm_step(dve, "c", b, i)
            dve.wait_ge(s("d_bp"), 1)
            for l in range(LAYERS):
                dve.tensor_scalar(bias_g[:, l, :], bank(0, l * GROUPS, (l + 1) * GROUPS), plain[:, C_BS + l:C_BS + l + 1], None,
                                  ALU.add).then_inc(s("d_bias"), 1)
            for n, (b, u) in enumerate(CU):
                if u < 3:
                    cols = slice(u * CH, (u + 1) * CH)
                    dve.wait_ge(s("c_hi"), 3 * b + u + 1)
                    dve.tensor_tensor(gc_lo[b][:, cols], bank(n % 6, 0, CH), gc_hi[b][:, cols].bitcast(F32),
                                      ALU.subtract).then_inc(s("c_lo"), 1)

            def c_scale_v(n):
                b, j = CSTEP[n]
                den, inv = small[:, 2 + n % 2:3 + n % 2], small[:, 4 + n % 2:5 + n % 2]
                dve.wait_ge(s("c_exp"), n + 1)
                dve.reciprocal(inv, den).then_inc(s("c_inv"), 1)
                dve.wait_ge(s("c_inv"), n + 1)
                if n >= 3:
                    dve.wait_ge(s("c_pv"), n - 2)
                dve.tensor_scalar(vs[n % 3], vc[:, (b * J + j) * D:(b * J + j + 1) * D], inv, None, ALU.mult)\
                   .then_inc(s("c_vs"), 1)

            def c_add(b):
                t = slice(b * J, (b + 1) * J)
                dve.wait_ge(s("c_otr"), b + 1)
                dve.tensor_tensor(h[:, t, :], ps[:, 6 * BANK:6 * BANK + J * D].rearrange("p (j d) -> p j d", d=D),
                                  h[:, t, :], ALU.add).then_inc(s("h2"), 1)

            for n, (b, j) in enumerate(CSTEP):
                o, w = (n % 2) * 3 * BANK, c_width(j)
                dve.wait_ge(s("c_s"), n + 1)
                dve.reduce_max(small[:, n % 2:n % 2 + 1], ps[:, o:o + w], AX_X, negate=True).then_inc(s("c_max"), 1)
                if n >= 1:
                    c_scale_v(n - 1)
                if n == J + 1:
                    c_add(0)
                    dve.wait_ge(s("h2"), 1)
                if 0 <= n - J - 2 < NORM_STEPS:
                    norm_step(dve, "d", 0, n - J - 2)
            c_scale_v(len(CSTEP) - 1)
            c_add(1)

            def d_sum(n):
                l, c = DSTEP[n]
                dve.wait_ge(s("d_f"), n + 1)
                dve.tensor_tensor(res[:, c * DW:(c + 1) * DW].rearrange("p (g t) -> p g t", t=GT),
                                  bank(n % 4, 0, DW).rearrange("p (g t) -> p g t", t=GT),
                                  bias_g[:, l, c * DG:(c + 1) * DG].unsqueeze(2).broadcast_to([P, DG, GT]),
                                  ALU.add).then_inc(s("d_z"), 1)

            def d_add(n):
                t0, k, bk = D_OUTS[n]
                t, o = slice(t0, t0 + k), bk * BANK
                dve.wait_ge(s("d_hb"), 1 if n == 0 else 2)
                dve.wait_ge(s("d_o"), n + 1)
                dve.tensor_tensor(h[:, t, :], ps[:, o:o + k * D].rearrange("p (j d) -> p j d", d=D), h[:, t, :],
                                  ALU.add).then_inc(s("h3"), 1)

            for n in range(NDS):
                d_sum(n)
                if n == 0:
                    dve.wait_ge(s("h2"), 2)
                for i in D_NORM[n] if n < len(D_NORM) else ():
                    norm_step(dve, "d", 1, i)
                if n == D_OUT_AT:
                    d_add(0)
                    dve.wait_ge(s("h3"), 1)
                if 0 <= n - E_NORM_AT < NORM_STEPS:
                    norm_step(dve, "e", 0, n - E_NORM_AT)
            d_add(1)
            dve.wait_ge(s("h3"), 2)
            norm_first(dve, "e", 1)
            d_add(2)
            dve.wait_ge(s("h3"), 3)
            norm_first(dve, "e", 2)
            dve.sem_inc(s("e_acc_read"), AF0)

            def split_unit(n, u, b, src):
                hd, cols = u // NCH, slice(u % NCH * CH, (u % NCH + 1) * CH)
                dve.wait_ge(s("e_proj"), n + 1)
                hi = g_hi[b][:, hd, cols]
                dve.tensor_copy(hi, src).then_inc(s("e_hi"), 1)
                dve.wait_ge(s("e_hi"), n + 1)
                dve.tensor_tensor(g_lo[b][:, hd, cols], src, hi.bitcast(F32), ALU.subtract).then_inc(s("e_proj_read"), 1)

            for u in range(UNITS):
                split_unit(u, u, 0, bank(4 + u % 2, 0, CH))
                if u == 1:
                    norm_second(dve, "e", 1)
                    norm_second(dve, "e", 2)

            for t in range(V_LATE, NT):
                dve.wait_ge(s("e_v"), t + 1)
                dve.tensor_copy(v_all[:, t, :], bank(t % V_BANKS)).then_inc(s("e_v_late"), 1)

            def add_output(it, b, chunks=range(NCH), last=False):
                for c in chunks:
                    part = acc[:, b, c * CH:(c + 1) * CH]
                    done = (c + 1) * J if last else STEPS - NCH + c + 1
                    dve.wait_ge(s("e_pv"), it * (B * STEPS) + (b * STEPS + done + PV0))
                    dve.tensor_tensor(part, bank(c, 0, CH), part, ALU.add).then_inc(s("e_acc_read"), 1)

            def pair_work(it, last):
                for b in range(B):
                    if not (last and b == B - 1):
                        for u in range(UNITS):
                            split_unit(it * (B * UNITS) + ((b + 1) * UNITS + u), u, 1 - b, bank(7, 0, CH))
                        add_output(it, b)

            dve.wait_ge(s("e_zero"), 1)
            with dve.Fori(0, PAIRS - 1) as it:
                pair_work(it, False)
            pair_work(PAIRS - 1, True)

            def add_tiles(n):
                t0, k, bk = OUTS[n]
                dve.wait_ge(s("e_o"), n + 1)
                dve.scalar_tensor_tensor(out=h[:, t0:t0 + k, :], in0=bank(bk, 0, k * D).rearrange("p (j d) -> p j d", d=D),
                                         scalar=0.0, in1=h[:, t0:t0 + k, :], op0=ALU.max, op1=ALU.add).then_inc(s("h4"), 1)

            def add_last_output(c):
                add_output(PAIRS - 1, B - 1, [c], True)

            step = [0]

            def chain(ins):
                step[0] += 1
                ins.then_inc(s("f_gate"), 1)
                dve.wait_ge(s("f_gate"), step[0])

            shifted, expd, prob, eq, ranked, sel1, rest = gate
            top, total, inv, p1, r1, p2, r2, winv = per_tok

            def gates_start(n):
                t0, k, bk = F_PART[n]
                t = slice(t0, t0 + k)
                both = bank(bk, 0, k * 2 * ME).rearrange("p (t n e) -> p t n e", n=2, e=ME)
                logits = shifted[:, t, :]
                dve.wait_ge(s("f_r"), n + 1)
                chain(dve.tensor_copy(logits, both[:, :, 0, :]))
                chain(dve.tensor_tensor(logits, both[:, :, 1, :], logits, ALU.add))
                chain(dve.reduce_max(top[:, t], logits, AX_X))
                dve.tensor_tensor(logits, logits, top[:, t].unsqueeze(2).broadcast_to([P, k, ME]),
                                  ALU.subtract).then_inc(s("f_logits"), 1)

            def gates(n):
                t0, k, _ = F_PART[n]
                t = slice(t0, t0 + k)
                rev = plain[:, K_REV:K_REV + ME].unsqueeze(1).broadcast_to([P, k, ME])

                def bc(v):
                    return v[:, t].unsqueeze(2).broadcast_to([P, k, ME])

                def g(v):
                    return v[:, t, :]

                dve.wait_ge(s("f_exp"), n + 1)
                chain(dve.reduce_sum(total[:, t], g(expd), AX_X))
                chain(dve.reciprocal(inv[:, t], total[:, t]))
                chain(dve.tensor_tensor(g(prob), g(expd), bc(inv), ALU.mult))
                chain(dve.reduce_max(p1[:, t], g(prob), AX_X))
                chain(dve.tensor_tensor(g(eq), g(prob), bc(p1), ALU.is_equal))
                chain(dve.tensor_tensor(g(ranked), g(eq), rev, ALU.mult))
                chain(dve.reduce_max(r1[:, t], g(ranked), AX_X))
                chain(dve.tensor_tensor(g(sel1), g(ranked), bc(r1), ALU.is_equal))
                chain(dve.scalar_tensor_tensor(out=g(rest), in0=g(sel1), scalar=-2.0, in1=g(prob), op0=ALU.mult, op1=ALU.add))
                chain(dve.reduce_max(p2[:, t], g(rest), AX_X))
                chain(dve.tensor_tensor(g(eq), g(rest), bc(p2), ALU.is_equal))
                chain(dve.tensor_tensor(g(ranked), g(eq), rev, ALU.mult))
                chain(dve.reduce_max(r2[:, t], g(ranked), AX_X))
                chain(dve.tensor_tensor(g(eq), g(ranked), bc(r2), ALU.is_equal))
                chain(dve.tensor_tensor(g(eq), g(eq), g(sel1), ALU.add))
                chain(dve.tensor_tensor(winv[:, t], p1[:, t], p2[:, t], ALU.add))
                chain(dve.tensor_scalar(winv[:, t], winv[:, t], 1e-12, None, ALU.max))
                chain(dve.tensor_tensor(g(prob), g(prob), g(eq), ALU.mult))
                chain(dve.reciprocal(winv[:, t], winv[:, t]))
                chain(dve.tensor_tensor(g(prob), g(prob), bc(winv), ALU.mult))
                if n == 0:
                    dve.wait_ge(s("f_zero"), 1)
                chain(dve.tensor_copy(cc[:, t, 0:ME], g(prob)))
                dve.tensor_tensor(cc[:, t, ME:2 * ME], g(prob), cc[:, t, 0:ME].bitcast(F32), ALU.subtract).then_inc(s("f_cc"), 1)

            def weigh(units):
                for n in units:
                    ch, u = FU[n]
                    cols = slice(ch * CH, (ch + 1) * CH)
                    dve.wait_ge(s("f_gelu"), n + 1)
                    dve.wait_ge(s("f_cb"), n + 1)
                    dve.tensor_tensor(act_f[:, u, cols], act_f[:, u, cols], bank(6 + n % 2, 0, CH), ALU.mult).then_inc(s("f_hc"), 1)

            def finish(b):
                t = slice(b * J, (b + 1) * J)
                o = F_Y_BANK[b] * BANK
                dve.wait_ge(s("f_y"), NCH * (b + 1))
                dve.wait_ge(s("f_hx"), (1, len(NORM_PARTS["f"]))[b])
                dve.tensor_tensor(h[:, t, :], ps[:, o:o + J * D].rearrange("p (j d) -> p j d", d=D), h[:, t, :],
                                  ALU.add).then_inc(s("h5"), 1)

            add_tiles(0)
            add_tiles(1)
            dve.wait_ge(s("h4"), 2)
            norm_first(dve, "f", 0)
            add_last_output(0)
            norm_second(dve, "f", 0)
            add_tiles(2)
            dve.wait_ge(s("h4"), 3)
            norm_first(dve, "f", 1)
            norm_second(dve, "f", 1)
            add_last_output(1)
            gates_start(0)
            add_tiles(3)
            dve.wait_ge(s("h4"), 4)
            norm_first(dve, "f", 2)
            gates(0)
            norm_second(dve, "f", 2)
            add_last_output(2)
            dve.wait_ge(s("sel_in"), 16)
            dve.wait_ge(s("e_qk"), PAIRS * B * STEPS)
            dve.tensor_copy(sel, sel_in).then_inc(s("f_sel"), 1)
            add_tiles(4)
            dve.wait_ge(s("h4"), 5)
            norm_first(dve, "f", 3)
            norm_second(dve, "f", 3)
            weigh(range(0, 4))
            gates_start(1)
            gates(1)
            weigh(range(4, 17))
            finish(0)
            weigh(range(17, 24))
            finish(1)

        @block.scalar
        def _(act):
            act.wait_ge(s("plain_in"), 16)
            for c in range(4):
                cols = slice(c * BANK, (c + 1) * BANK)
                act.wait_ge(s("a_q"), c + 1)
                act.activation(qa_hi[:, cols], bank(4 + c % 2), ACT.Identity, bias=plain[:, C_BQ:C_BQ + 1]).then_inc(s("qa_hi"), 1)
                act.wait_ge(s("a_k"), c + 1)
                act.activation(ka[:, cols], bank(6 + c % 2), ACT.Identity, bias=plain[:, C_BK:C_BK + 1]).then_inc(s("ka_hi"), 1)
            act.wait_ge(s("b_tr"), 1)
            act.copy(powers_t[:, :, :].rearrange("p b t -> p (b t)"), ps[0:TURNS * DEGS, 0:B * P])\
               .then_inc(s("powers_t"), 1)
            act.wait_ge(s("a_pv"), JI)
            act.copy(ret[:, BANK:2 * BANK], bank(5)).then_inc(s("ret"), 1)
            act.wait_ge(s("c_merge"), 1)
            act.activation(w_hi[:, W_CM:W_CM + P], bank(7, 0, P), ACT.Identity, scale=D ** -0.5).then_inc(s("cm_hi"), 1)
            act.wait_ge(s("e_merge"), 1)
            act.copy(raw1[:, HEADS * P:HEADS * (P + D)], bank(6)).then_inc(s("merged"), 1)
            for n in range(2):
                act.wait_ge(s("e_merge"), n + 2)
                act.copy(raw1[:, n * BANK:(n + 1) * BANK], bank(4 + n)).then_inc(s("merged"), 1)
            norm_act(act, 2)
            norm_act(act, 5)
            act.wait_ge(s("w_rest_lo"), 1)
            for n, w in enumerate((w_hi, w_lo)):
                act.copy(w_router[:, n * ME:(n + 1) * ME], w[:, W_FR:W_FR + ME].bitcast(F32)).then_inc(s("w_side"), 1)
                act.copy(w_b2[:, n * D:(n + 1) * D], w[:, W_FB2:W_FB2 + D].bitcast(F32)).then_inc(s("w_side"), 1)
            for b in range(B):
                transposes_act(act, "c", b)
            for n, (b, u) in enumerate(CU):
                act.wait_ge(s("c_proj"), n + 1)
                if u < 3:
                    act.copy(gc_hi[b][:, u * CH:(u + 1) * CH], bank(n % 6, 0, CH)).then_inc(s("c_hi"), 1)
                else:
                    t0, t1 = (0, 8) if u == 3 else (8, 9)
                    act.copy(vc[:, (b * J + t0) * D:(b * J + t1) * D], bank(n % 6, 0, (t1 - t0) * D)).then_inc(s("c_v"), 1)
            def c_output(b):
                act.wait_ge(s("c_pv"), J * (b + 1))
                act.copy(out_t[:, 0:4 * P], bank(6)).then_inc(s("c_out"), 1)
                act.copy(out_t[0:D, 4 * P:5 * P], bank(7, 0, P)[0:D, :]).then_inc(s("c_out"), 1)

            for n, (b, j) in enumerate(CSTEP):
                o, w = (n % 2) * 3 * BANK, c_width(j)
                act.wait_ge(s("c_max"), n + 1)
                if n >= 2:
                    act.wait_ge(s("c_inv"), n - 1)
                if n >= 3:
                    act.wait_ge(s("c_pv"), n - 2)
                act.activation(pc[n % 3][:, 0:w], ps[:, o:o + w], ACT.Exp, bias=small[:, n % 2:n % 2 + 1],
                               accum_out=small[:, 2 + n % 2:3 + n % 2]).then_inc(s("c_exp"), 1)
                if n == J:
                    c_output(0)
            transposes_act(act, "d", 0)
            c_output(1)
            def d_input(b):
                for n in range(b * NCH, (b + 1) * NCH):
                    act.wait_ge(s("d_in"), n + 1)
                    act.activation(hid[0][:, n * CH:(n + 1) * CH], bank(D_IN_BANK[n], 0, CH), ACT.Relu, bias=plain[:, C_BI:C_BI + 1])\
                       .then_inc(s("d_h0"), 1)

            d_input(0)
            for n, (l, c) in enumerate(DSTEP):
                cols = slice(c * DW, (c + 1) * DW)
                act.wait_ge(s("d_z"), n + 1)
                act.activation(hid[l + 1][:, cols], res[:, cols], ACT.Relu).then_inc(s(f"d_h{l + 1}"), 1)
                for g in D_TR_AT.get(n, ()):
                    copy_group(act, "d", g)
                if n == D_IN_AT:
                    d_input(1)
            for t in range(NT):
                if t in (0, J):
                    for g in range(3) if t == 0 else range(3, 5):
                        copy_group(act, "e", g)
                if t < V_LATE:
                    act.wait_ge(s("e_v"), t + 1)
                    act.copy(v_all[:, t, :], bank(t % V_BANKS)).then_inc(s("e_v_read"), 1)
                if t == E_TR_LAST:
                    copy_group(act, "e", 5)

            def exponentials(n):
                t = slice(F_PART[n][0], F_PART[n][0] + F_PART[n][1])
                act.wait_ge(s("f_logits"), n + 1)
                act.activation(gate[1][:, t, :], gate[0][:, t, :], ACT.Exp).then_inc(s("f_exp"), 1)

            def pair_weights(it, last):
                for n in range(B * STEPS):
                    o = (3 + 2 * (n % 2)) * BANK
                    act.wait_ge(s("e_qk"), it * (B * STEPS) + (n + 1))
                    act.wait_ge(s("e_pv"), it * (B * STEPS) + (n + 1))
                    act.activation(pe_ring[:, n % RING, :, :],
                                   ps[:, o:o + 2 * BANK].rearrange("p (h t) -> p h t", h=2)[:, :, 0:CH],
                                   ACT.Sigmoid, scale=float(D) ** 0.5).then_inc(s("e_sig"), 1)
                    if last and n - STEPS - 3 in K_TR:
                        copy_group(act, "f", K_TR.index(n - STEPS - 3))
                    if last and n - STEPS == K_R + 4:
                        exponentials(0)

            with act.Fori(0, PAIRS - 1) as it:
                pair_weights(it, False)
            pair_weights(PAIRS - 1, True)

            def gelus(units):
                for n in units:
                    ch, u = FU[n]
                    act.wait_ge(s("f_1"), n + 1)
                    act.activation(act_f[:, u, ch * CH:(ch + 1) * CH], bank(3 + n % 2, 0, CH), ACT.Gelu,
                                   bias=plain[:, C_B1 + u:C_B1 + u + 1]).then_inc(s("f_gelu"), 1)

            def combine_copies(n):
                for g in range(*F_CC_OF[n]):
                    t0, k, bk = F_CC[g]
                    act.wait_ge(s("f_ctr"), g + 1)
                    act.copy(c_hl[:, t0 * P:(t0 + k) * P], bank(bk, 0, k * P)).then_inc(s("f_ct"), 1)

            def second_layer_copies(chunks):
                for ch in chunks:
                    act.wait_ge(s("f_y2"), ch + 1)
                    if ch >= 2:
                        act.wait_ge(s("f_y"), ch - 1)
                    act.copy(y_t[ch % 2], bank((2, 5)[ch % 2], 0, CH)).then_inc(s("f_yt"), 1)

            gelus(range(2))
            copy_group(act, "f", 4)
            gelus(range(2, 4))
            combine_copies(0)
            gelus(range(4, 6))
            copy_group(act, "f", 5)
            act.activation(small[:, 8:9], stat[:, 3, 0:1], ACT.Exp).then_inc(s("f_table"), 1)
            exponentials(1)
            second_layer_copies([0])
            gelus(range(6, 16))
            combine_copies(1)
            gelus(range(16, 19))
            second_layer_copies([1])
            gelus(range(19, 23))
            second_layer_copies([2])
            gelus([23])
            second_layer_copies(range(3, B * NCH))


def arrays_of(inputs):
    g = {k: np.asarray(v) for k, v in inputs.items()}
    f = np.float32

    def twice(w):
        return np.concatenate([w, w], 0)

    def dup(w):
        return np.concatenate([w, w], 1)

    def heads(w):
        return np.moveaxis(w.reshape(D, D, HEADS), 2, 0)

    xt = g["x"].reshape(B * T_IMG, D).T
    w1 = np.moveaxis(g["L1_ffn_w1"], 0, 1).reshape(D, ME * D)
    b2 = g["L1_ffn_b2"]
    w_stack = np.concatenate([
        twice(dup(g["L0_tok_Wq"])), twice(dup(g["L0_tok_Wk"])), twice(g["L0_tok_Wv"]),
        twice(g["L0_attn_Wv"].T),
        twice(g["L0_ffn_Wi"].T),
        twice(g["L1_ffn_router_w"].T), twice(w1),
        np.concatenate([b2, b2, np.zeros((P - 2 * ME, D), f)], 0),
    ], 1)
    hq, hk, hv = (heads(g["L1_attn_W" + n]) for n in "qkv")
    wo_heads = np.moveaxis(g["L1_attn_Wo"].reshape(D, HEADS, D), 1, 0)
    w_factors = np.concatenate([
        dup(g["L0_attn_Wq"]), dup(g["L0_attn_Wk"]),
        *[dup(w.T) for w in hq], *[dup(w.T) for w in hk], *[dup(w.T) for w in hv], *wo_heads], 1)
    zero = np.zeros((D, D), f)
    wo = g["L0_tok_Wo"]

    def row(v, n=P):
        return np.broadcast_to(v.reshape(1, -1), (n, v.size))

    def col(v):
        return v.reshape(P, 1)

    b1 = g["L1_ffn_b1"].reshape(ME // 2, P)
    cols = [col(np.tile(g["L0_tok_bq"], 2)), col(np.tile(g["L0_tok_bk"], 2)), col(g["L0_ffn_bi"])]
    cols += [col(g["L0_ffn_bs"][l, 0]) for l in range(LAYERS)] + [col(b1[u]) for u in range(ME // 2)]
    cols += [col(np.broadcast_to(g["L0_tok_prelu_a"].reshape(1), (P,))), col(np.arange(P, dtype=f))]
    mask = np.where(np.arange(P)[None, :] >= np.arange(P)[:, None], f(MASKED * D ** -0.5), f(0)).astype(f)
    w_plain = np.concatenate([
        np.block([[wo, zero], [zero, wo]]),
        *[g["L0_ffn_Ws"][l, 0].T for l in range(LAYERS)],
        g["L0_ffn_Wo"].T, np.eye(P, dtype=f), mask, twice(np.eye(D, dtype=f)),
        row(g["L0_tok_bv"]), row(g["L0_tok_bo"]), row(g["L0_ffn_bo"]),
        row(np.arange(ME, 0, -1).astype(f)), *cols], 1)
    w2 = g["L1_ffn_w2"].reshape(ME // 2, P, D)
    sel = np.zeros((P, ME * D), f)
    for e in range(ME):
        sel[[e, e + ME], e * D:(e + 1) * D] = 1
    w_late = np.concatenate([*w2, sel], 1)
    ins = {
        "x_stack": np.moveaxis(twice(xt).reshape(P, 4, BANK), 1, 0), "w_stack": w_stack, "w_plain": w_plain, "w_factors": w_factors, "w_late": w_late,
        "gamma_t": g["L0_tok_d_gamma_batched"].T.reshape(JI, P, T_IMG),
        "w_br": np.moveaxis(g["L0_ffn_br"], 0, 1).reshape(EXPERTS, LAYERS * HID),
        "w_poly": g["L0_txt_poly_coeffs"].reshape(TURNS * DEGS, D),
        "ids": g["x_txt"].T, "turns": g["L0_txt_turns"],
        "route": g["L0_ffn_route_id"].reshape(1, GROUPS),
        "w_route": np.moveaxis(g["L0_ffn_Wr"], (1, 3, 0, 2), (0, 1, 2, 3)).reshape(EXPERTS, HID, LAYERS * HID),
    }
    return {k: np.ascontiguousarray(v) for k, v in ins.items()}


def kernel(**inputs):
    import concourse.bacc as bacc
    from concourse.bass_utils import run_bass_kernel_spmd

    nc = bacc.Bacc("TRN2", target_bir_lowering=False, num_devices=1)
    arrays = arrays_of(inputs)
    args = {k: nc.dram_tensor(k, a.shape, mybir.dt.from_np(a.dtype), kind="ExternalInput").ap() for k, a in arrays.items()}
    out = nc.dram_tensor("out", (B, S, D), F32, kind="ExternalOutput").ap()
    program(nc, **args, out=out)
    result = run_bass_kernel_spmd(nc, [arrays], core_ids=[0])
    return result.results[0]["out"]
```
